# Optimizing a Trainium2 kernel written in Bass

```python
import numpy as np
import jax
import jax.numpy as jnp

def _softmax(x, axis=-1):
    return jax.nn.softmax(x, axis=axis)

def _gelu(x):
    return jax.nn.gelu(x, approximate=True)

def _silu(x):
    return jax.nn.silu(x)

def _sigmoid(x):
    return jax.nn.sigmoid(x)

def _layernorm(x, axis=-1, eps=1e-05):
    m = jnp.mean(x, axis=axis, keepdims=True)
    v = jnp.var(x, axis=axis, keepdims=True)
    return (x - m) / jnp.sqrt(v + eps)

def _scatter_add(tgt, idx, src, axis=0):
    return tgt.at[idx].add(src)

def _segment_sum(src, seg, n):
    return jax.ops.segment_sum(src, seg, n)
kernel_name = 'mk_seq_preln_d1_jaxref_r4_ffd725'

def setup_inputs(seed: int=0):
    np.random.seed(seed)
    _w = jnp.asarray

    def _L0_attn_setup():
        import jax, jax.numpy as jnp
        import numpy as np
        D_MODEL = 256
        D_STATE = 16
        D_CONV = 4
        EXPAND = 2
        D_INNER = D_MODEL * EXPAND
        B = 2
        L = 256

        def _causal_dwconv(x, w, b):
            K = w.shape[1]
            Lx = x.shape[1]
            xp = jnp.pad(x, ((0, 0), (K - 1, 0), (0, 0)))
            return sum((xp[:, k:k + Lx, :] * w[:, k] for k in range(K))) + b
        key = jax.random.key(seed)
        ks = jax.random.split(key, 8)
        s = lambda k, shape, scale: jax.random.normal(k, shape, dtype=jnp.float32) * scale
        x = s(ks[0], (B, L, D_MODEL), 1.0)
        W_in = s(ks[1], (2 * D_INNER, D_MODEL), D_MODEL ** (-0.5))
        conv_w = s(ks[2], (D_INNER, D_CONV), D_CONV ** (-0.5))
        conv_b = s(ks[3], (D_INNER,), 0.02)
        W_x = s(ks[4], (2 * D_STATE + 1, D_INNER), D_INNER ** (-0.5))
        dt_w = s(ks[5], (D_INNER, 1), 1.0)
        dt_b = s(ks[6], (D_INNER,), 0.02)
        A_log = jnp.log(jnp.broadcast_to(jnp.arange(1, D_STATE + 1, dtype=jnp.float32), (D_INNER, D_STATE)))
        D_param = jnp.ones((D_INNER,), dtype=jnp.float32)
        W_out = s(ks[7], (D_MODEL, D_INNER), D_INNER ** (-0.5))
        return dict(x=x, W_in=W_in, conv_w=conv_w, conv_b=conv_b, W_x=W_x, dt_w=dt_w, dt_b=dt_b, A_log=A_log, D_param=D_param, W_out=W_out)
    _L0_attn_in = _L0_attn_setup()

    def _L0_ffn_setup():
        import jax, jax.numpy as jnp
        import numpy as np
        EPS = 1e-05
        TOP_K = 2

        def _rmsnorm(x, w):
            xf = x.astype(jnp.float32)
            rms = jax.lax.rsqrt(jnp.mean(xf * xf, axis=-1, keepdims=True) + EPS)
            return (xf * rms).astype(x.dtype) * w

        def _attention(x, wq, wk, wv, wo, num_heads=16):
            B, S, H = x.shape
            D = H // num_heads
            q = (x @ wq.T).reshape(B, S, num_heads, D)
            k = (x @ wk.T).reshape(B, S, num_heads, D)
            v = (x @ wv.T).reshape(B, S, num_heads, D)
            scale = 1.0 / jnp.sqrt(jnp.float32(D)).astype(x.dtype)
            scores = jnp.einsum('bqhd,bkhd->bhqk', q, k) * scale
            probs = jax.nn.softmax(scores, axis=-1)
            out = jnp.einsum('bhqk,bkhd->bqhd', probs, v).reshape(B, S, H)
            return out @ wo.T

        def _moe(x, gate_w, w1, w2, w3):
            B, S, H = x.shape
            xf = x.reshape(-1, H)
            logits = xf @ gate_w.T
            rw, sel = jax.lax.top_k(logits, TOP_K)
            rw = jax.nn.softmax(rw.astype(jnp.float32), axis=-1).astype(x.dtype)
            E = gate_w.shape[0]
            out = jnp.zeros_like(xf)
            for e in range(E):
                we = jnp.sum(jnp.where(sel == e, rw, 0.0), axis=-1)
                h = jax.nn.silu(xf @ w1[e].T) * (xf @ w3[e].T)
                out = out + h @ w2[e].T * we[:, None]
            return out.reshape(B, S, H)
        key = jax.random.key(seed)
        ks = jax.random.split(key, 10)
        H, I, E, NH = (256, 512, 8, 16)
        B, S = (2, 512)
        s = 0.02
        return {'x': jax.random.normal(ks[0], (B, S, H), jnp.float32), 'ln1_w': jnp.ones((H,), jnp.float32), 'ln2_w': jnp.ones((H,), jnp.float32), 'wq': jax.random.normal(ks[1], (H, H), jnp.float32) * s, 'wk': jax.random.normal(ks[2], (H, H), jnp.float32) * s, 'wv': jax.random.normal(ks[3], (H, H), jnp.float32) * s, 'wo': jax.random.normal(ks[4], (H, H), jnp.float32) * s, 'gate_w': jax.random.normal(ks[5], (E, H), jnp.float32) * s, 'w1': jax.random.normal(ks[6], (E, I, H), jnp.float32) * s, 'w2': jax.random.normal(ks[7], (E, H, I), jnp.float32) * s, 'w3': jax.random.normal(ks[8], (E, I, H), jnp.float32) * s}
    _L0_ffn_in = _L0_ffn_setup()
    _d = {'L0_attn_x': _L0_attn_in['x'], 'L0_attn_W_in': _L0_attn_in['W_in'], 'L0_attn_conv_w': _L0_attn_in['conv_w'], 'L0_attn_conv_b': _L0_attn_in['conv_b'], 'L0_attn_W_x': _L0_attn_in['W_x'], 'L0_attn_dt_w': _L0_attn_in['dt_w'], 'L0_attn_dt_b': _L0_attn_in['dt_b'], 'L0_attn_A_log': _L0_attn_in['A_log'], 'L0_attn_D_param': _L0_attn_in['D_param'], 'L0_attn_W_out': _L0_attn_in['W_out'], 'L0_ffn_ln1_w': _L0_ffn_in['ln1_w'], 'L0_ffn_ln2_w': _L0_ffn_in['ln2_w'], 'L0_ffn_wq': _L0_ffn_in['wq'], 'L0_ffn_wk': _L0_ffn_in['wk'], 'L0_ffn_wv': _L0_ffn_in['wv'], 'L0_ffn_wo': _L0_ffn_in['wo'], 'L0_ffn_gate_w': _L0_ffn_in['gate_w'], 'L0_ffn_w1': _L0_ffn_in['w1'], 'L0_ffn_w2': _L0_ffn_in['w2'], 'L0_ffn_w3': _L0_ffn_in['w3']}
    _x0 = _d['L0_attn_x']
    _d['L0_attn_x'] = jax.random.normal(jax.random.fold_in(jax.random.key(seed), 1), (2, 2048, 256), dtype=_x0.dtype)
    del _x0
    return _d

def reference(L0_attn_x, L0_attn_W_in, L0_attn_conv_w, L0_attn_conv_b, L0_attn_W_x, L0_attn_dt_w, L0_attn_dt_b, L0_attn_A_log, L0_attn_D_param, L0_attn_W_out, L0_ffn_ln1_w, L0_ffn_ln2_w, L0_ffn_wq, L0_ffn_wk, L0_ffn_wv, L0_ffn_wo, L0_ffn_gate_w, L0_ffn_w1, L0_ffn_w2, L0_ffn_w3):

    def _L0_attn_ref(x, W_in, conv_w, conv_b, W_x, dt_w, dt_b, A_log, D_param, W_out):
        import jax, jax.numpy as jnp
        import numpy as np
        D_MODEL = 256
        D_STATE = 16
        D_CONV = 4
        EXPAND = 2
        D_INNER = D_MODEL * EXPAND
        B = 2
        L = 256

        def _causal_dwconv(x, w, b):
            K = w.shape[1]
            Lx = x.shape[1]
            xp = jnp.pad(x, ((0, 0), (K - 1, 0), (0, 0)))
            return sum((xp[:, k:k + Lx, :] * w[:, k] for k in range(K))) + b
        Bb, Ll, _ = x.shape
        xz = jnp.einsum('bld,ed->ble', x, W_in)
        x_ssm, z = jnp.split(xz, 2, axis=-1)
        xc = jax.nn.silu(_causal_dwconv(x_ssm, conv_w, conv_b))
        proj = jnp.einsum('bld,ed->ble', xc, W_x)
        dt_raw = proj[..., :1]
        B_vals = proj[..., 1:1 + D_STATE]
        C_vals = proj[..., 1 + D_STATE:]
        dt = jax.nn.softplus(dt_raw * dt_w[:, 0] + dt_b)
        A = -jnp.exp(A_log)
        dA = jnp.exp(dt[..., None] * A)
        dBx = dt[..., None] * B_vals[:, :, None, :] * xc[..., None]

        def step(h, inputs):
            dA_t, dBx_t, C_t = inputs
            h = dA_t * h + dBx_t
            y_t = jnp.einsum('bdn,bn->bd', h, C_t)
            return (h, y_t)
        h0 = jnp.zeros((Bb, D_INNER, D_STATE), dtype=x.dtype)
        xs = (jnp.moveaxis(dA, 1, 0), jnp.moveaxis(dBx, 1, 0), jnp.moveaxis(C_vals, 1, 0))
        _, ys = jax.lax.scan(step, h0, xs)
        y = jnp.moveaxis(ys, 0, 1) + xc * D_param
        y = y * jax.nn.silu(z)
        return jnp.einsum('bld,ed->ble', y, W_out)

    def _L0_ffn_ref(x, ln1_w, ln2_w, wq, wk, wv, wo, gate_w, w1, w2, w3):
        import jax, jax.numpy as jnp
        import numpy as np
        EPS = 1e-05
        TOP_K = 2

        def _rmsnorm(x, w):
            xf = x.astype(jnp.float32)
            rms = jax.lax.rsqrt(jnp.mean(xf * xf, axis=-1, keepdims=True) + EPS)
            return (xf * rms).astype(x.dtype) * w

        def _attention(x, wq, wk, wv, wo, num_heads=16):
            B, S, H = x.shape
            D = H // num_heads
            q = (x @ wq.T).reshape(B, S, num_heads, D)
            k = (x @ wk.T).reshape(B, S, num_heads, D)
            v = (x @ wv.T).reshape(B, S, num_heads, D)
            scale = 1.0 / jnp.sqrt(jnp.float32(D)).astype(x.dtype)
            scores = jnp.einsum('bqhd,bkhd->bhqk', q, k) * scale
            probs = jax.nn.softmax(scores, axis=-1)
            out = jnp.einsum('bhqk,bkhd->bqhd', probs, v).reshape(B, S, H)
            return out @ wo.T

        def _moe(x, gate_w, w1, w2, w3):
            B, S, H = x.shape
            xf = x.reshape(-1, H)
            logits = xf @ gate_w.T
            rw, sel = jax.lax.top_k(logits, TOP_K)
            rw = jax.nn.softmax(rw.astype(jnp.float32), axis=-1).astype(x.dtype)
            E = gate_w.shape[0]
            out = jnp.zeros_like(xf)
            for e in range(E):
                we = jnp.sum(jnp.where(sel == e, rw, 0.0), axis=-1)
                h = jax.nn.silu(xf @ w1[e].T) * (xf @ w3[e].T)
                out = out + h @ w2[e].T * we[:, None]
            return out.reshape(B, S, H)
        h = x + _attention(_rmsnorm(x, ln1_w), wq, wk, wv, wo)
        h = h + _moe(_rmsnorm(h, ln2_w), gate_w, w1, w2, w3)
        return h
    x = L0_attn_x
    x = x + _L0_attn_ref(_layernorm(x, axis=-1), L0_attn_W_in, L0_attn_conv_w, L0_attn_conv_b, L0_attn_W_x, L0_attn_dt_w, L0_attn_dt_b, L0_attn_A_log, L0_attn_D_param, L0_attn_W_out)
    x = x + _L0_ffn_ref(_layernorm(x, axis=-1), L0_ffn_ln1_w, L0_ffn_ln2_w, L0_ffn_wq, L0_ffn_wk, L0_ffn_wv, L0_ffn_wo, L0_ffn_gate_w, L0_ffn_w1, L0_ffn_w2, L0_ffn_w3)
    return x

_drawn_inputs = setup_inputs


def setup_inputs(seed=0):
    import zlib

    import numpy as np

    out = dict(_drawn_inputs(seed))
    spreads = {'L0_attn_D_param': (1.0, 0.2), 'L0_ffn_ln1_w': (1.0, 0.6), 'L0_ffn_ln2_w': (1.0, 0.6)}
    factors = {'L0_attn_conv_b': 3.923,
     'L0_attn_dt_b': 8.0,
     'L0_ffn_wq': 8.0,
     'L0_ffn_wk': 8.0,
     'L0_ffn_wv': 8.0,
     'L0_ffn_wo': 8.0,
     'L0_ffn_gate_w': 7.532,
     'L0_ffn_w1': 6.714,
     'L0_ffn_w2': 6.621,
     'L0_ffn_w3': 6.628}
    for name, (base, spread) in spreads.items():
        noise = np.random.default_rng([zlib.crc32(name.encode()), seed]).standard_normal(out[name].shape)
        drawn = base * np.exp(spread * noise) if base else spread * noise
        out[name] = jnp.asarray(drawn.astype(out[name].dtype))
    for name, factor in factors.items():
        out[name] = (out[name] * factor).astype(out[name].dtype)
    return out
```

```python
from contextlib import ExitStack

import concourse.bass as bass
from concourse import mybir

ALU = mybir.AluOpType
ACT = mybir.ActivationFunctionType
AX = mybir.AxisListType
F32 = mybir.dt.float32
BF16 = mybir.dt.bfloat16
U32 = mybir.dt.uint32

P = 128
CH = 512
TT = CH // P
DM = 256
KM = DM // P
DI = 512
KI = DI // P
NS = 16
TAPS = 4
EPS = 1e-5


def wait(eng, sem, value):
    if isinstance(value, int) and value <= 0:
        return
    eng.wait_ge(sem, value)


def wait_apart(eng, sem, value, met):
    if isinstance(value, int):
        wait(eng, sem, value)
    else:
        eng.compute_val(value)
        eng.wait_ge(met, 1)
        eng.wait_ge(sem, value)


def flat(ap):
    return ap.rearrange("p a b -> p (a b)")


def ssm_stage(nc, x, W_inT, conv_w, conv_b, W_xT, dt_w, dt_b, A_log, D_param, W_outT, x1_dram, b_dram):
    B, L, _ = x.shape
    NI = L // CH
    assert B == 2 and L % CH == 0 and NI >= 2
    RING = 4

    with ExitStack() as ctx:
        def sb(name, shape, dt=F32):
            return ctx.enter_context(nc.sbuf_tensor(name, shape, dt))

        def ps(name, shape, dt=F32):
            return ctx.enter_context(nc.psum_tensor(name, shape, dt))

        def sem(name):
            return ctx.enter_context(nc.semaphore(name))

        w_in = sb("w_in", [P, KM, 2 * DI])
        w_x = sb("w_x", [P, KI, 2 * NS + 1])
        w_out = sb("w_out", [P, KI, DM])
        cw = sb("cw", [P, KI, TAPS])
        cb = sb("cb", [P, KI])
        dtw = sb("dtw", [P, KI])
        dtb = sb("dtb", [P, KI])
        dpar = sb("dpar", [P, KI])
        alog = sb("alog", [P, KI, NS])
        aneg = sb("aneg", [P, KI, NS])
        ident = sb("ident", [P, P])
        epsc = sb("epsc", [P, 1])
        xn = sb("xn", [P, TT, DM])
        stats = sb("stats", [P, TT, 6])
        mv = sb("mv", [P, TT, 2])
        sd = sb("sd", [P, TT])
        rs = sb("rs", [P, TT])
        xT = sb("xT", [P, KM, CH])
        HALO = TAPS - 1
        xs = sb("xs", [P, KI, HALO + CH])
        halo = sb("halo", [P, 2, KI, HALO])
        tA = xs[:, :, 0:CH]
        tB = sb("tB", [P, KI, CH])
        xc = sb("xc", [P, 2, KI, CH])
        zs = sb("zs", [P, 2, KI, CH])
        dt = sb("dt", [P, 2, KI, CH])
        u = sb("u", [P, 2, KI, CH])
        pr = sb("pr", [2 * NS + 1, 2, CH])
        state = sb("state", [P, 2, NS, KI])
        dA = sb("dA", [P, 2, KI, CH])
        h = sb("h", [P, 2, KI, CH])
        prod = sb("prod", [P, RING, KI, CH])
        bb = sb("bb", [P, RING, CH])
        xres = sb("xres", [P, TT, DM])
        x1 = sb("x1", [P, TT, DM])

        y_ps = ps("y_ps", [P, KI, CH])
        c_ps = ps("c_ps", [P, 2, CH])
        fill = ps("fill", [P, 2, CH])

        s_w = sem("s_w")
        s_id = sem("s_id")
        s_set = sem("s_set")
        s_aexp = sem("s_aexp")
        s_an = sem("s_an")
        s_x = sem("s_x")
        s_xr = sem("s_xr")
        s_st1 = sem("s_st1")
        s_mv = sem("s_mv")
        s_sd = sem("s_sd")
        s_rs = sem("s_rs")
        s_xn = sem("s_xn")
        s_xT = sem("s_xT")
        s_full = [sem("s_full0"), sem("s_full1")]
        s_free = [sem("s_free0"), sem("s_free1")]
        s_halo = sem("s_halo")
        s_hsave = sem("s_hsave")
        s_tap = sem("s_tap")
        s_cv = sem("s_cv")
        s_xc = sem("s_xc")
        s_zs = sem("s_zs")
        s_prst = sem("s_prst")
        s_b = [sem(f"s_b{k}") for k in range(RING)]
        s_abs = sem("s_abs")
        s_e = sem("s_e")
        s_ln = sem("s_ln")
        s_q = sem("s_q")
        s_sp = sem("s_sp")
        s_dt = sem("s_dt")
        s_u = sem("s_u")
        s_da = sem("s_da")
        s_bx = sem("s_bx")
        s_h = sem("s_h")
        s_stt = sem("s_stt")
        s_cb = sem("s_cb")
        s_hc = sem("s_hc")
        s_ys = sem("s_ys")
        s_g1 = sem("s_g1")
        s_g = sem("s_g")
        s_x1st = sem("s_x1st")

        NW = 10
        FA = 6

        def prep_fill(c):
            return 0 if isinstance(c, int) and c == 0 else (FA + 1) * c - 1

        def out_fill(c, last):
            return (FA + 1) * c + (FA if last else 2 * FA)

        def tokens(c, i, b):
            return b, bass.ds(i * CH, CH)

        def nxt(i, b):
            return (i, 1) if b == 0 else (i + 1, 0)

        def prv(i, b):
            return (i, 0) if b == 1 else (i - 1, 1)

        def every_chunk(eng, prologue, chunk):
            prologue()
            for b in range(2):
                chunk(0, b, b > 0, True)
            if NI > 2:
                with eng.Fori(1, NI - 1) as i:
                    for b in range(2):
                        chunk(i, b, True, True)
            for b in range(2):
                chunk(NI - 1, b, True, b == 0)

        block = ctx.enter_context(nc.Block())

        @block.sync
        def _(sp):
            sp.dma_start(w_in[:, :, :], W_inT.rearrange("(k p) e -> p k e", p=P)).then_inc(s_w, 16)
            sp.dma_start(w_x[:, :, :], W_xT.rearrange("(k p) e -> p k e", p=P)).then_inc(s_w, 16)
            sp.dma_start(w_out[:, :, :], W_outT.rearrange("(k p) e -> p k e", p=P)).then_inc(s_w, 16)
            sp.dma_start(cw[:, :, :], conv_w.rearrange("(k p) e -> p k e", p=P)).then_inc(s_w, 16)
            sp.dma_start(alog[:, :, :], A_log.rearrange("(k p) e -> p k e", p=P)).then_inc(s_w, 16)
            with nc.allow_non_contiguous_dma(reason="five small vectors, once"):
                for dst, src in ((cb, conv_b), (dtw, dt_w), (dtb, dt_b), (dpar, D_param)):
                    sp.dma_start(dst[:, :], src.rearrange("(k p) -> p k", p=P)).then_inc(s_w, 16)

            def load_x(i, b):
                c = 2 * i + b
                bt, ts = tokens(c, i, b)
                wait_apart(sp, s_full[1], prep_fill(c - 1) + 1 if not (isinstance(c, int) and c == 0) else 0, s_w)
                sp.dma_start(xn[:, :, :], x[bt, ts, :].rearrange("(t p) e -> p t e", p=P)).then_inc(s_x, 16)

            def load_b(i, b, n):
                c = 2 * i + b
                wait_apart(sp, s_prst, 16 * (c + 1), s_w)
                wait_apart(sp, s_bx, NS * c + n - RING + 1, s_w)
                sp.dma_start(bb[:, n % RING, :], b_dram[b, n:n + 1, :].partition_broadcast(P)
                             ).then_inc(s_b[n % RING], 16)

            def store_rows(i, b):
                c = 2 * i + b
                wait_apart(sp, s_free[0], prep_fill(c) + FA, s_w)
                sp.dma_start(b_dram[b, :, :], pr[0:NS, b, :]).then_inc(s_prst, 16)
                load_b(i, b, 0)
                load_b(i, b, 1)

            def wait_x1(c, last):
                for bank in range(2):
                    wait_apart(sp, s_free[bank], out_fill(c, last) + 1, s_w)

            def store_x1(i, b, last=False):
                c = 2 * i + b
                bt, ts = tokens(c, i, b)
                wait_x1(c, last)
                sp.dma_start(x1_dram[bt, ts, :].rearrange("(t p) e -> p t e", p=P), x1[:, :, :]
                             ).then_inc(s_x1st, 16)

            def load_res(i, b):
                c = 2 * i + b
                bt, ts = tokens(c, i, b)
                if not (isinstance(c, int) and c == 0):
                    wait_x1(c - 1, False)
                sp.dma_start(xres[:, :, :], x[bt, ts, :].rearrange("(t p) e -> p t e", p=P)).then_inc(s_xr, 16)

            def prologue():
                load_x(0, 0)
                store_rows(0, 0)
                load_x(0, 1)

            def chunk(i, b, has_prev, has_next):
                for n in range(NS):
                    if n + 2 < NS:
                        load_b(i, b, n + 2)
                    if n == 4:
                        if has_prev:
                            store_x1(*prv(i, b))
                        load_res(i, b)
                    if n == 15 and has_next:
                        store_rows(*nxt(i, b))
                        if not (isinstance(i, int) and i == NI - 1):
                            load_x(*nxt(*nxt(i, b)))

            every_chunk(sp, prologue, chunk)
            store_x1(NI - 1, 1, True)
            sp.wait_ge(s_x1st, 16 * 2 * NI)

        @block.gpsimd
        def _(pool):
            nc.gpsimd.memset(ident[:, :], 0.0).then_inc(s_id, 1)
            nc.gpsimd.memset(epsc[:, :], EPS).then_inc(s_set, 1)
            nc.gpsimd.memset(halo[:, :, :, :], 0.0).then_inc(s_set, 1)
            nc.gpsimd.memset(state[:, :, :, :], 0.0).then_inc(s_set, 1)
            pool.wait_ge(s_id, 1)
            nc.gpsimd.affine_select(out=ident[:, :], in_=ident[:, :], compare_op=ALU.not_equal, fill=1.0,
                                    base=0, pattern=[[-1, P]], channel_multiplier=1).then_inc(s_id, 1)
            pool.wait_ge(s_aexp, 1)
            nc.gpsimd.tensor_scalar(aneg[:, :, :], aneg[:, :, :], -1.0, None, ALU.mult).then_inc(s_an, 1)

            def step_sizes(i, b):
                c = 2 * i + b
                wait(pool, s_ln, 2 * (c + 1))
                wait(pool, s_q, c + 1)
                nc.gpsimd.tensor_tensor(u[:, b], u[:, b], tB[:, :, :], ALU.subtract).then_inc(s_sp, 1)
                wait(pool, s_sp, c + 1)
                nc.gpsimd.tensor_tensor(dt[:, b], dt[:, b], u[:, b], ALU.add).then_inc(s_dt, 1)
                wait(pool, s_dt, c + 1)
                nc.gpsimd.tensor_tensor(u[:, b], dt[:, b], xc[:, b], ALU.mult).then_inc(s_u, 1)

            def chunk(i, b, has_prev, has_next):
                c = 2 * i + b
                wait(pool, s_u, c + 1)
                for n in range(NS):
                    wait(pool, s_b[n % RING], 16 * ((NS // RING) * c + n // RING + 1))
                    wait(pool, s_ys, NS * c + n - RING + 1)
                    nc.gpsimd.tensor_tensor(
                        prod[:, n % RING], u[:, b],
                        bb[:, n % RING, None, :].to_broadcast([P, KI, CH]), ALU.mult).then_inc(s_bx, 1)
                if has_next:
                    step_sizes(*nxt(i, b))

            every_chunk(pool, lambda: step_sizes(0, 0), chunk)

        @block.scalar
        def _(act):
            act.wait_ge(s_w, 16 * (NW - 1))
            act.wait_ge(s_set, 3)
            nc.scalar.activation(aneg[:, :, :], alog[:, :, :], ACT.Exp).then_inc(s_aexp, 1)

            def root(c):
                wait(act, s_mv, c + 1)
                nc.scalar.activation(sd[:, :], mv[:, :, 1], ACT.Sqrt, bias=epsc[:, 0:1]).then_inc(s_sd, 1)

            def take_xT(c, b):
                f = prep_fill(c)
                for k in range(KM):
                    wait(act, s_full[k], f + 1)
                    nc.scalar.copy(xT[:, k, :], fill[:, k, :]).then_inc(s_free[k], 1)
                wait(act, s_dt, c)
                wait(act, s_hsave, c - 1)
                nc.scalar.copy(xs[:, :, 0:HALO], halo[:, b]).then_inc(s_halo, 1)

            def take_conv_in(c, b, d):
                bank, f = d % 2, prep_fill(c) + 1 + d // 2
                wait(act, s_full[bank], f + 1)
                nc.scalar.copy(xs[:, d, HALO:], fill[:, bank, :]).then_inc(s_tap, 1)
                wait(act, s_g, c - 1)
                nc.scalar.activation(xc[:, b, d, :], fill[:, bank, :], ACT.Identity,
                                     bias=cb[:, d:d + 1], scale=cw[:, d, HALO:HALO + 1]
                                     ).then_inc(s_free[bank], 1)

            def take_z(c, b, d, has_prev):
                bank, f = d % 2, prep_fill(c) + 3 + d // 2
                wait(act, s_full[bank], f + 1)
                nc.scalar.copy(zs[:, b, d, :], fill[:, bank, :]).then_inc(s_free[bank], 1)

            def silus(c, b):
                wait(act, s_cv, KI * HALO * (c + 1))
                nc.scalar.copy(halo[:, b], xs[:, :, CH:CH + HALO]).then_inc(s_hsave, 1)
                nc.scalar.activation(flat(xc[:, b]), flat(xc[:, b]), ACT.Silu).then_inc(s_xc, 1)
                for k in range(2):
                    wait(act, s_free[k], prep_fill(c) + 5)
                nc.scalar.activation(flat(zs[:, b]), flat(zs[:, b]), ACT.Silu).then_inc(s_zs, 1)

            def take_rows(c, b):
                wait(act, s_full[0], prep_fill(c) + FA)
                nc.scalar.copy(pr[:, b, :], fill[0:2 * NS + 1, 0, :]).then_inc(s_free[0], 1)

            def softplus(c, b):
                wait(act, s_full[1], prep_fill(c) + FA)
                wait(act, s_hsave, c + 1)
                for d in range(KI):
                    nc.scalar.activation(tA[:, d, :], fill[:, 1, :], ACT.Abs,
                                         bias=dtb[:, d:d + 1], scale=dtw[:, d:d + 1]).then_inc(s_abs, 1)
                    last = nc.scalar.activation(dt[:, b, d, :], fill[:, 1, :], ACT.Relu,
                                                bias=dtb[:, d:d + 1], scale=dtw[:, d:d + 1])
                last.then_inc(s_free[1], 1)
                wait(act, s_abs, KI * (c + 1))
                nc.scalar.activation(tA, tA, ACT.Exp, scale=-1.0).then_inc(s_e, 1)
                wait(act, s_e, c + 1)
                nc.scalar.activation(tB[:, :, :], tA, ACT.Identity, bias=1.0).then_inc(s_ln, 1)
                nc.scalar.activation(u[:, b], tA, ACT.Ln, bias=1.0).then_inc(s_ln, 1)

            def save_state(c, b, n):
                wait(act, s_h, NS * c + n + 1)
                nc.scalar.copy(state[:, b, n, :], h[:, n % 2, :, CH - 1]).then_inc(s_stt, 1)

            def prep(c, b, n, has_prev=True):
                if n == 0:
                    root(c)
                if n == 2:
                    take_xT(c, b)
                if 3 <= n < 7:
                    take_conv_in(c, b, n - 3)
                if 7 <= n < 11:
                    take_z(c, b, n - 7, has_prev)
                if n == 11:
                    silus(c, b)
                if n == 12:
                    take_rows(c, b)
                if n == 13:
                    softplus(c, b)

            def prologue():
                for n in range(NS):
                    prep(0, 0, n)
                act.wait_ge(s_an, 1)

            def chunk(i, b, has_prev, has_next):
                c = 2 * i + b
                wait(act, s_dt, c + 1)
                for n in range(NS):
                    if n >= 2:
                        save_state(c, b, n - 2)
                    else:
                        wait(act, s_h, NS * c + n - 1)
                    for d in range(KI):
                        nc.scalar.activation(dA[:, n % 2, d, :], dt[:, b, d, :], ACT.Exp,
                                             scale=aneg[:, d, n:n + 1]).then_inc(s_da, 1)
                    if has_next:
                        prep(c + 1, 1 - b, n)
                save_state(c, b, NS - 2)
                save_state(c, b, NS - 1)

            every_chunk(act, prologue, chunk)

        @block.tensor
        def _(pe):
            pe.wait_ge(s_w, 16 * (NW - 1))
            pe.wait_ge(s_id, 2)

            def transposes(c):
                wait(pe, s_xn, c + 1)
                for k in range(KM):
                    wait(pe, s_free[k], prep_fill(c))
                    for t in range(TT):
                        last = nc.tensor.transpose(fill[:, k, t * P:(t + 1) * P],
                                                   xn[:, t, k * P:(k + 1) * P], ident[:, :])
                    last.then_inc(s_full[k], 1)

            def project_in(c, e):
                bank, f = e % 2, prep_fill(c) + 1 + e // 2
                if e == 0:
                    wait(pe, s_free[1], f)
                wait(pe, s_free[bank], f)
                for k in range(KM):
                    last = nc.tensor.matmul(fill[:, bank, :], w_in[:, k, e * P:(e + 1) * P], xT[:, k, :],
                                            start=(k == 0), stop=(k == KM - 1))
                last.then_inc(s_full[bank], 1)

            def project_rows(c, b):
                f = prep_fill(c) + FA - 1
                wait(pe, s_xc, c + 1)
                wait(pe, s_free[0], f)
                for k in range(KI):
                    last = nc.tensor.matmul(fill[0:2 * NS + 1, 0, :], w_x[:, k, :], xc[:, b, k, :],
                                            start=(k == 0), stop=(k == KI - 1))
                last.then_inc(s_full[0], 1)

            def row(r):
                return ident[0:2 * NS + 1, r:r + 1].to_broadcast([2 * NS + 1, P])

            def spread_dt(c, b):
                f = prep_fill(c) + FA - 1
                wait(pe, s_free[0], prep_fill(c) + FA)
                wait(pe, s_free[1], f)
                nc.tensor.matmul(fill[:, 1, :], row(2 * NS), pr[:, b, :],
                                 start=True, stop=True).then_inc(s_full[1], 1)

            def spread_c(c, b, n):
                wait(pe, s_hc, NS * c + n - 1)
                nc.tensor.matmul(c_ps[:, n % 2, :], row(NS + n), pr[:, b, :],
                                 start=True, stop=True).then_inc(s_cb, 1)

            def prep(c, b, n):
                if n == 2:
                    transposes(c)
                if 3 <= n < 11:
                    project_in(c, n - 3)
                if n == 12:
                    project_rows(c, b)
                if n == 13:
                    spread_dt(c, b)

            def prologue():
                for n in range(NS):
                    prep(0, 0, n)
                spread_c(0, 0, 0)
                spread_c(0, 0, 1)

            def chunk(i, b, has_prev, has_next):
                c = 2 * i + b
                for n in range(NS):
                    if n == 0:
                        wait(pe, s_g1, KI * c)
                    wait(pe, s_hc, NS * c + n + 1)
                    for d in range(KI):
                        last = nc.tensor.matmul(y_ps[:, d, :], ident[:, :], prod[:, n % RING, d, :],
                                                start=(n == 0), stop=(n == NS - 1))
                    last.then_inc(s_ys, 1)
                    if n + 2 < NS:
                        spread_c(c, b, n + 2)
                    if has_next and n + 2 < NS:
                        prep(c + 1, 1 - b, n + 2)
                if has_next:
                    spread_c(c + 1, 1 - b, 0)
                    spread_c(c + 1, 1 - b, 1)
                wait(pe, s_g, c + 1)
                f = out_fill(c, not has_next)
                for t in range(TT):
                    bank = t // 2
                    if t % 2 == 0:
                        wait(pe, s_free[bank], f)
                    for d in range(KI):
                        last = nc.tensor.matmul(fill[:, bank, (t % 2) * DM:(t % 2 + 1) * DM],
                                                zs[:, b, d, t * P:(t + 1) * P], w_out[:, d, :],
                                                start=(d == 0), stop=(d == KI - 1))
                    if t % 2 == 1:
                        last.then_inc(s_full[bank], 1)

            every_chunk(pe, prologue, chunk)

        @block.vector
        def _(dve):
            def norm_stats(c):
                wait(dve, s_x, 16 * (c + 1))
                for t in range(TT):
                    last = nc.vector.bn_stats(stats[:, t, :], xn[:, t, :])
                last.then_inc(s_st1, 1)
                wait_apart(dve, s_st1, c + 1, s_w)
                for t in range(TT):
                    last = nc.vector.bn_aggr(mv[:, t, :], stats[:, t, :])
                last.then_inc(s_mv, 1)

            def norm_apply(c):
                wait(dve, s_sd, c + 1)
                nc.vector.reciprocal(rs[:, :], sd[:, :]).then_inc(s_rs, 1)
                wait(dve, s_rs, c + 1)
                for t in range(TT):
                    last = nc.vector.tensor_scalar(xn[:, t, :], xn[:, t, :], mv[:, t, 0:1], rs[:, t:t + 1],
                                                   ALU.subtract, ALU.mult)
                last.then_inc(s_xn, 1)

            def add_taps(c, b, d):
                wait(dve, s_free[d % 2], prep_fill(c) + 2 + d // 2)
                wait(dve, s_halo, c + 1)
                for k in range(HALO):
                    if k:
                        wait(dve, s_cv, HALO * (KI * c + d) + k)
                    nc.vector.scalar_tensor_tensor(
                        out=xc[:, b, d, :], in0=xs[:, d, k:k + CH], scalar=cw[:, d, k:k + 1],
                        in1=xc[:, b, d, :], op0=ALU.mult, op1=ALU.add).then_inc(s_cv, 1)

            def rounding(c):
                wait(dve, s_ln, 2 * c + 1)
                nc.vector.scalar_tensor_tensor(out=tB[:, :, :], in0=tB[:, :, :], scalar=-1.0, in1=tA,
                                               op0=ALU.add, op1=ALU.subtract).then_inc(s_q, 1)

            def residual(c, last):
                wait(dve, s_xr, 16 * (c + 1))
                wait(dve, s_x1st, 16 * c)
                f = out_fill(c, last)
                for bank in range(2):
                    wait(dve, s_full[bank], f + 1)
                    nc.vector.tensor_tensor(flat(x1[:, 2 * bank:2 * bank + 2, :]), fill[:, bank, :],
                                            flat(xres[:, 2 * bank:2 * bank + 2, :]), ALU.add
                                            ).then_inc(s_free[bank], 1)

            def prep(c, b, n):
                if n == 0:
                    norm_stats(c)
                if n == 1:
                    norm_apply(c)
                if 4 <= n < 8:
                    add_taps(c, b, n - 4)
                if n == 13:
                    rounding(c)

            def scans(c, b, n):
                wait(dve, s_bx, NS * c + n + 1)
                wait(dve, s_stt, NS * c + n - 1)
                wait(dve, s_hc, NS * c + n - 1)
                for d in range(KI):
                    wait(dve, s_da, KI * (NS * c + n) + d + 1)
                    last = nc.vector.tensor_tensor_scan(
                        h[:, n % 2, d, :], dA[:, n % 2, d, :], prod[:, n % RING, d, :],
                        state[:, b, n, d:d + 1], ALU.mult, ALU.add)
                last.then_inc(s_h, 1)

            def times_c(c, b, n):
                wait(dve, s_h, NS * c + n + 1)
                wait(dve, s_cb, NS * c + n + 1)
                nc.vector.tensor_tensor(prod[:, n % RING], h[:, n % 2],
                                        c_ps[:, n % 2, None, :].to_broadcast([P, KI, CH]), ALU.mult
                                        ).then_inc(s_hc, 1)

            def prologue():
                dve.wait_ge(s_w, 16 * (NW - 1))
                dve.wait_ge(s_set, 3)
                for n in range(NS):
                    prep(0, 0, n)

            def chunk(i, b, has_prev, has_next):
                c = 2 * i + b
                for n in range(NS + 1):
                    if n < NS:
                        scans(c, b, n)
                    if n > 0:
                        times_c(c, b, n - 1)
                    if n == 1 and has_prev:
                        residual(c - 1, False)
                    if n < NS and has_next:
                        prep(c + 1, 1 - b, n)
                wait(dve, s_ys, NS * (c + 1))
                for d in range(KI):
                    nc.vector.scalar_tensor_tensor(
                        out=xc[:, b, d, :], in0=xc[:, b, d, :], scalar=dpar[:, d:d + 1], in1=y_ps[:, d, :],
                        op0=ALU.mult, op1=ALU.add).then_inc(s_g1, 1)
                wait(dve, s_g1, KI * (c + 1))
                wait(dve, s_zs, c + 1)
                nc.vector.tensor_tensor(zs[:, b], xc[:, b], zs[:, b], ALU.mult).then_inc(s_g, 1)

            every_chunk(dve, prologue, chunk)
            residual(2 * NI - 1, True)


NH = 16
HD = DM // NH
HP = NH // 2
VW = 2 * (HD + 1)


def qkv_stage(nc, x1_dram, ln1_w, wqT, wkT, wvT, f_dram, parts_dram, v_all):
    B, L, _ = x1_dram.shape
    NI = L // CH
    NC = B * NI
    assert B == 2

    with ExitStack() as ctx:
        def sb(name, shape, dt=F32):
            return ctx.enter_context(nc.sbuf_tensor(name, shape, dt))

        def ps(name, shape, dt=F32):
            return ctx.enter_context(nc.psum_tensor(name, shape, dt))

        def sem(name):
            return ctx.enter_context(nc.semaphore(name))

        wq = sb("wq", [P, KM, DM])
        wk = sb("wk", [P, KM, DM])
        wv = sb("wv", [P, KM, DM])
        ln1 = sb("ln1", [P, KM])
        ident = sb("q_ident", [P, P])
        epsc = sb("q_epsc", [P, 1])
        xa = sb("xa", [P, 2, TT, DM])
        an = sb("an", [P, 2, TT, DM])
        stats = sb("q_stats", [P, TT, 6])
        mv = sb("q_mv", [P, 2, TT, 2])
        sd = sb("q_sd", [P, 2, TT])
        rs = sb("q_rs", [P, 2, TT])
        ms = sb("q_ms", [P, 2, TT])
        rr = sb("q_rr", [P, 2, TT])
        aT = sb("aT", [P, KM, CH])
        part = sb("part", [P, 3, 2 * KM, CH], BF16)
        rest = sb("rest", [P, 2 * KM, CH])
        tr_ps = ps("tr_ps", [P, KM, CH])
        qk_ps = ps("qk_ps", [P, 2 * KM, CH])
        v_ps = ps("v_ps", [P, TT, DM])

        s_w = sem("q_w")
        s_id = sem("q_id")
        s_set = sem("q_set")
        s_x = [sem("q_x0"), sem("q_x1")]
        s_st = sem("q_st")
        s_sd = sem("q_sd_s")
        s_rs = sem("q_rs_s")
        s_ms = sem("q_ms_s")
        s_f = sem("q_f")
        s_a = sem("q_a")
        s_fst = sem("q_fst")
        s_tr = sem("q_tr")
        s_aT = sem("q_aT")
        s_qk = sem("q_qk")
        s_v = sem("q_v")
        s_p1 = sem("q_p1")
        s_r = sem("q_r")
        s_p2 = sem("q_p2")
        s_p3 = sem("q_p3")
        s_pst = sem("q_pst")
        s_vout = sem("q_vout")

        block = ctx.enter_context(nc.Block())

        def every_chunk(eng, front, back):
            front(0, 0)
            front(0, 1)
            back(0, 0)
            with eng.Fori(1, NI) as i:
                front(i, 0)
                back(i - 1, 1)
                front(i, 1)
                back(i, 0)
            back(NI - 1, 1)

        @block.sync
        def _(sp):
            for dst, src in ((wq, wqT), (wk, wkT), (wv, wvT)):
                sp.dma_start(dst[:, :, :], src.rearrange("(k p) e -> p k e", p=P)).then_inc(s_w, 16)
            with nc.allow_non_contiguous_dma(reason="one small vector, once"):
                sp.dma_start(ln1[:, :], ln1_w.rearrange("(k p) -> p k", p=P)).then_inc(s_w, 16)

            def tokens(dram, i, b):
                return dram[b, bass.ds(i * CH, CH), :].rearrange("(t p) e -> p t e", p=P)

            def front(i, b):
                c = 2 * i + b
                wait_apart(sp, s_a, c - 1, s_w)
                wait_apart(sp, s_fst, 16 * (c - 1), s_w)
                sp.dma_start(xa[:, b], tokens(x1_dram, i, b)).then_inc(s_x[b], 16)

            def back(i, b):
                c = 2 * i + b
                wait_apart(sp, s_f, c + 1, s_w)
                sp.dma_start(tokens(f_dram, i, b), xa[:, b]).then_inc(s_fst, 16)
                for s, ready in enumerate((s_p1, s_p2, s_p3)):
                    wait_apart(sp, ready, c + 1, s_w)
                    for m in range(2):
                        dst = parts_dram[m, s, b * DM:(b + 1) * DM, bass.ds(i * CH, CH)]
                        sp.dma_start(dst.rearrange("(k p) l -> p k l", p=P),
                                     part[:, s, m * KM:(m + 1) * KM, :]).then_inc(s_pst, 16)

            every_chunk(sp, front, back)
            sp.wait_ge(s_fst, 16 * NC)
            sp.wait_ge(s_pst, 16 * 6 * NC)

        @block.gpsimd
        def _(pool):
            nc.gpsimd.memset(ident[:, :], 0.0).then_inc(s_id, 1)
            nc.gpsimd.memset(epsc[:, :], EPS).then_inc(s_set, 1)
            for hh in range(2):
                col = hh * (HD + 1) + HD
                nc.gpsimd.memset(v_all[:, :, :, col:col + 1], 1.0).then_inc(s_set, 1)
            pool.wait_ge(s_id, 1)
            nc.gpsimd.affine_select(out=ident[:, :], in_=ident[:, :], compare_op=ALU.not_equal, fill=1.0,
                                    base=0, pattern=[[-1, P]], channel_multiplier=1).then_inc(s_id, 1)

        @block.scalar
        def _(act):
            act.wait_ge(s_w, 64)
            act.wait_ge(s_set, 3)

            def front(i, b):
                c = 2 * i + b
                wait(act, s_st, 2 * c + 2)
                nc.scalar.activation(sd[:, b, :], mv[:, b, :, 1], ACT.Sqrt, bias=epsc[:, 0:1]
                                     ).then_inc(s_sd, 1)
                wait(act, s_ms, 2 * c + 2)
                nc.scalar.activation(sd[:, b, :], ms[:, b, :], ACT.Sqrt, bias=epsc[:, 0:1]
                                     ).then_inc(s_sd, 1)

            def back(i, b):
                c = 2 * i + b
                wait(act, s_tr, c + 1)
                wait(act, s_v, c)
                for k in range(KM):
                    nc.scalar.activation(aT[:, k, :], tr_ps[:, k, :], ACT.Identity,
                                         scale=ln1[:, k:k + 1]).then_inc(s_aT, 1)
                wait(act, s_qk, c + 1)
                wait(act, s_pst, 16 * 6 * c)
                nc.scalar.copy(part[:, 0], qk_ps[:, :, :]).then_inc(s_p1, 1)
                wait(act, s_r, c + 1)
                nc.scalar.copy(part[:, 1], rest[:, :, :]).then_inc(s_p2, 1)

            every_chunk(act, front, back)

        @block.tensor
        def _(pe):
            pe.wait_ge(s_w, 64)
            pe.wait_ge(s_id, 2)

            def chunk(i, b):
                c = 2 * i + b
                wait(pe, s_a, c + 1)
                wait(pe, s_aT, 2 * c)
                for k in range(KM):
                    for t in range(TT):
                        last = nc.tensor.transpose(tr_ps[:, k, t * P:(t + 1) * P],
                                                   an[:, b, t, k * P:(k + 1) * P], ident[:, :])
                last.then_inc(s_tr, 1)
                wait(pe, s_aT, 2 * c + 2)
                wait(pe, s_r, c)
                for m, w in enumerate((wq, wk)):
                    for o in range(KM):
                        for k in range(KM):
                            last = nc.tensor.matmul(qk_ps[:, m * KM + o, :], w[:, k, o * P:(o + 1) * P],
                                                    aT[:, k, :], start=(k == 0), stop=(k == KM - 1))
                last.then_inc(s_qk, 1)
                wait(pe, s_vout, c)
                for t in range(TT):
                    for k in range(KM):
                        last = nc.tensor.matmul(v_ps[:, t, :], aT[:, k, t * P:(t + 1) * P], wv[:, k, :],
                                                start=(k == 0), stop=(k == KM - 1))
                last.then_inc(s_v, 1)

            chunk(0, 0)
            chunk(0, 1)
            with pe.Fori(1, NI) as i:
                chunk(i, 0)
                chunk(i, 1)

        @block.vector
        def _(dve):
            dve.wait_ge(s_set, 3)

            def front(i, b):
                c = 2 * i + b
                wait(dve, s_x[b], 16 * (i + 1))
                for t in range(TT):
                    last = nc.vector.bn_stats(stats[:, t, :], xa[:, b, t, :])
                last.then_inc(s_st, 1)
                wait_apart(dve, s_st, 2 * c + 1, s_w)
                for t in range(TT):
                    last = nc.vector.bn_aggr(mv[:, b, t, :], stats[:, t, :])
                last.then_inc(s_st, 1)
                wait(dve, s_sd, 2 * c + 1)
                nc.vector.reciprocal(rs[:, b, :], sd[:, b, :]).then_inc(s_rs, 1)
                wait(dve, s_rs, 2 * c + 1)
                nc.vector.tensor_tensor(ms[:, b, :], mv[:, b, :, 1], rs[:, b, :], ALU.mult).then_inc(s_ms, 1)
                for t in range(TT):
                    last = nc.vector.tensor_scalar(xa[:, b, t, :], xa[:, b, t, :], mv[:, b, t, 0:1],
                                                   rs[:, b, t:t + 1], ALU.subtract, ALU.mult)
                last.then_inc(s_f, 1)
                wait(dve, s_ms, 2 * c + 1)
                nc.vector.tensor_tensor(ms[:, b, :], ms[:, b, :], rs[:, b, :], ALU.mult).then_inc(s_ms, 1)
                wait(dve, s_sd, 2 * c + 2)
                nc.vector.reciprocal(rr[:, b, :], sd[:, b, :]).then_inc(s_rs, 1)
                wait(dve, s_rs, 2 * c + 2)
                wait(dve, s_f, c + 1)
                wait(dve, s_tr, c - 1)
                for t in range(TT):
                    last = nc.vector.tensor_scalar(an[:, b, t, :], xa[:, b, t, :], rr[:, b, t:t + 1],
                                                   None, ALU.mult)
                last.then_inc(s_a, 1)

            def back(i, b):
                c = 2 * i + b
                wait(dve, s_p1, c + 1)
                nc.vector.tensor_tensor(rest[:, :, :], qk_ps[:, :, :], part[:, 0], ALU.subtract).then_inc(s_r, 1)
                wait_apart(dve, s_v, c + 1, s_w)
                for t in range(TT):
                    dst = v_all[:, b * HP:(b + 1) * HP, bass.ds(i * TT + t, 1), :]
                    dst = dst.rearrange("p a o (h w) -> p (a o) h w", h=2)[:, :, :, 0:HD]
                    src = v_ps[:, t, :].rearrange("p (a h w) -> p a h w", h=2, w=HD)
                    last = nc.vector.tensor_copy(dst, src)
                last.then_inc(s_vout, 1)
                wait(dve, s_p2, c + 1)
                wait(dve, s_r, c + 1)
                nc.vector.tensor_tensor(part[:, 2], rest[:, :, :], part[:, 1], ALU.subtract).then_inc(s_p3, 1)

            every_chunk(dve, front, back)


def attention_stage(nc, parts_dram, v_all, att, B, L):
    NP = B * HP
    QC = L // CH
    KT = L // P
    KK = 2 * KT
    LEAD = 4
    HW = 2 * CH
    NHALF = L // HW
    NMAX = KT * NHALF
    assert NMAX == KK and QC == 4 and NP % 2 == 0 and NP >= 6
    ROWS = 6 * HD + 2
    SC = float(HD) ** -0.5
    SR = 3
    PR = 4

    with ExitStack() as ctx:
        def sb(name, shape, dt=F32):
            return ctx.enter_context(nc.sbuf_tensor(name, shape, dt))

        def ps(name, shape, dt=F32):
            return ctx.enter_context(nc.psum_tensor(name, shape, dt))

        def sem(name):
            return ctx.enter_context(nc.semaphore(name))

        qs = sb("qs", [ROWS, 2, 2, L], BF16)
        ks = sb("ks", [ROWS, 2, 2, L], BF16)
        q4 = sb("q4", [P, 2, L], BF16)
        k4 = sb("k4", [P, 2, L], BF16)
        vst = sb("vst", [P, 2, KT, 64])
        prob = sb("prob", [P, PR, QC, CH])
        osb = sb("osb", [P, 2, CH])
        nmh = sb("nmh", [P, 2, KT, NHALF])
        nm = sb("nm", [P, 2 * KT])
        nmr = sb("nmr", [2 * KT, 2, P], BF16)
        rec = sb("rec", [P, 2, QC * TT])
        ident = sb("a_ident", [P, P])
        s_ps = ps("s_ps", [P, SR, CH])
        acc = ps("acc", [P, CH])
        ring = ps("ring", [P, 2, HW])

        s_id = sem("a_id")
        s_one = sem("a_one")
        s_op = [sem("a_op0"), sem("a_op1")]
        s_op4 = [sem("a_op40"), sem("a_op41")]
        s_mr = [sem("a_mr0"), sem("a_mr1")]
        s_vst = sem("a_vst")
        s_S = sem("a_S")
        s_exp = sem("a_exp")
        s_pv = sem("a_pv")
        s_o = sem("a_o")
        s_full = [sem("a_full0"), sem("a_full1")]
        s_free = [sem("a_free0"), sem("a_free1")]
        s_comb = sem("a_comb")
        s_nmr1 = sem("a_nmr1")
        s_rec = sem("a_rec")

        Q_PARTS = (0, 0, 1, 1, 0, 2)
        K_PARTS = (0, 1, 0, 1, 2, 0)
        LOADS = 16 * 2 * 2 * 6
        LOADS4 = 16 * 2 * 2 * 4

        MAXNEXT, MAXTHEN, ROWMAX, OUT = "maximum, next pair", "maximum, pair after", "rows of the maximum", "output"

        def plan(has_prev, has_next, has_then):
            steps = [[] for _ in range(KK)]
            if has_prev:
                steps[2].append((OUT, 1))
            steps[KT + 2].append((OUT, 0))
            if has_next:
                for j in range(LEAD, NMAX):
                    steps[j - LEAD].append((MAXNEXT, j))
                steps[NMAX - LEAD].append((ROWMAX, 0))
            if has_then:
                for j in range(LEAD):
                    steps[NMAX - LEAD + j].append((MAXTHEN, j))
            return steps

        def fills_before(pair, s):
            first = (NMAX + 1 + LEAD, NMAX + LEAD)[s]
            return first + (NMAX + 2 - s) * pair - (1 if s == 0 and not (isinstance(pair, int) and pair == 0) else 0)

        class Count:
            def __init__(self, pair, last=False, start=False):
                if start:
                    self.n = [0, 0]
                else:
                    self.n = [fills_before(pair, s) - (LEAD if last else 0) for s in range(2)]

            def next(self, s):
                self.n[s] = self.n[s] + 1
                return self.n[s]

        def every_pair(eng, prologue, pair, epilogue=None):
            prologue()
            pair(0, 0, 0, False, True, True)
            pair(1, 0, 1, True, True, True)
            with eng.Fori(1, NP // 2 - 1) as it:
                for par in range(2):
                    pair(2 * it + par, it, par, True, True, True)
            pair(NP - 2, NP // 2 - 1, 0, True, True, False)
            pair(NP - 1, NP // 2 - 1, 1, True, False, False)
            if epilogue:
                epilogue()

        block = ctx.enter_context(nc.Block())

        @block.sync
        def _(sp):
            def load(dst, at, par_hh, m, order, n, s):
                for g, part in enumerate(order):
                    src = parts_dram[m, part, bass.ds(n * 2 * HD + par_hh[-1] * HD, HD), :]
                    rows = slice(at + g * HD, at + (g + 1) * HD)
                    out = dst[rows, par_hh[0], par_hh[1], :] if dst is qs or dst is ks else dst[rows, par_hh[0], :]
                    sp.dma_start(out, src).then_inc(s, 16)

            def load_stack(n, par):
                wait_apart(sp, s_S, KK * QC * (n - 1), s_one)
                for hh in range(2):
                    load(qs, 0, (par, hh), 0, Q_PARTS, n, s_op[par])
                    load(ks, 0, (par, hh), 1, K_PARTS, n, s_op[par])

            def load_lead(n, par):
                if not isinstance(n, int) or n > 1:
                    for s in range(2):
                        wait_apart(sp, s_free[s], fills_before(n - 2, s), s_one)
                for hh in range(2):
                    load(q4, 64 * hh, (par, hh), 0, Q_PARTS[0:4], n, s_op4[par])
                    load(k4, 64 * hh, (par, hh), 1, K_PARTS[0:4], n, s_op4[par])

            def max_rows(n, par, fills):
                wait_apart(sp, s_free[0], fills, s_one)
                for hh in range(2):
                    for s in range(2):
                        sp.dma_start(qs[6 * HD + s:6 * HD + s + 1, par, hh, :],
                                     nmr[hh * KT:(hh + 1) * KT, s, :]).then_inc(s_mr[par], 16)

            def prologue():
                load_lead(0, 0)
                load_stack(0, 0)
                load_lead(1, 1)
                load_stack(1, 1)
                max_rows(0, 0, NMAX + 1)

            def pair(n, it, par, has_prev, has_next, has_then):
                if has_prev and has_next:
                    load_stack(n + 1, 1 - par)
                if has_then:
                    load_lead(n + 2, par)
                if has_next:
                    ct = Count(n)
                    for ops in plan(has_prev, has_next, has_then):
                        for op, j in ops:
                            if op == ROWMAX:
                                max_rows(n + 1, 1 - par, ct.next(0))
                            elif op == OUT:
                                ct.next(1 - j)
                            elif op == MAXNEXT or op == MAXTHEN:
                                ct.next(0)
                                ct.next(1)

            every_pair(sp, prologue, pair)

        @block.gpsimd
        def _(pool):
            nc.gpsimd.memset(ident[:, :], 0.0).then_inc(s_id, 1)
            nc.gpsimd.memset(vst[:, :, :, :], 0.0).then_inc(s_one, 1)
            for par in range(2):
                pool.wait_ge(s_one, par + 1)
                nc.gpsimd.memset(ks[6 * HD:6 * HD + 2, par, :, :], 1.0).then_inc(s_one, 1)
            pool.wait_ge(s_id, 1)
            pool.wait_ge(s_one, 3)
            nc.gpsimd.affine_select(out=ident[:, :], in_=ident[:, :], compare_op=ALU.not_equal, fill=1.0,
                                    base=0, pattern=[[-1, P]], channel_multiplier=1).then_inc(s_id, 1)

            def pair(n, it, par, has_prev, has_next, has_then):
                wait_apart(pool, s_pv, KK * (n - 1), s_id)
                src = v_all[:, bass.ds(n, 1), :, :].rearrange("p a t w -> p (a t) w")
                nc.gpsimd.tensor_copy(vst[:, par, :, 0:VW], src).then_inc(s_vst, 1)

            every_pair(pool, lambda: None, pair)

        @block.scalar
        def _(act):
            def pair(n, it, par, has_prev, has_next, has_then):
                for k in range(KK):
                    wait(act, s_pv, KK * n + k - PR + 1)
                    for j in range(QC):
                        m = QC * k + j
                        wait(act, s_S, KK * QC * n + m + 1)
                        nc.scalar.activation(prob[:, k % PR, j, :], s_ps[:, m % SR, :], ACT.Exp,
                                             scale=SC).then_inc(s_exp, 1)

            every_pair(act, lambda: None, pair)

        @block.tensor
        def _(pe):
            pe.wait_ge(s_id, 2)
            pe.wait_ge(s_one, 3)
            NU = KK * QC

            def maxima(ct, par, j):
                t, half = j // NHALF, j % NHALF
                for s in range(2):
                    wait(pe, s_free[s], ct.next(s) - 1)
                for b in range(2):
                    for hh in range(2):
                        r = slice(64 * hh, 64 * hh + 64)
                        at = half * HW + b * CH
                        ins = nc.tensor.matmul(ring[:, hh, b * CH:(b + 1) * CH],
                                               q4[r, par, t * P:(t + 1) * P], k4[r, par, at:at + CH],
                                               start=True, stop=True)
                        if b == 1:
                            ins.then_inc(s_full[hh], 1)

            def rows_of_max(ct, n):
                wait(pe, s_free[0], ct.next(0) - 1)
                wait(pe, s_comb, n + 1)
                nc.tensor.transpose(ring[0:2 * KT, 0, 0:P], nm[:, :], ident[:, :]).then_inc(s_full[0], 1)

            def outputs(ct, n, hh):
                s = 1 - hh
                wait(pe, s_free[s], ct.next(s) - 1)
                wait(pe, s_o, 2 * n + hh + 1)
                for t in range(TT):
                    last = nc.tensor.transpose(ring[:, s, t * P:(t + 1) * P], osb[:, hh, t * P:(t + 1) * P],
                                               ident[:, :])
                last.then_inc(s_full[s], 1)

            def scores(n, par, k, j):
                m = QC * k + j
                hh, t = k // KT, k % KT
                back = m - SR if m >= SR else max(x for x in range(NU) if x % SR == m % SR) - NU
                wait(pe, s_exp, NU * n + back + 1)
                nc.tensor.matmul(s_ps[:, m % SR, :], ks[:, par, hh, t * P:(t + 1) * P],
                                 qs[:, par, hh, j * CH:(j + 1) * CH], start=True, stop=True).then_inc(s_S, 1)

            def values(n, par, k):
                hh, t = k // KT, k % KT
                if t == 0:
                    wait(pe, s_o, 2 * n + hh)
                if k == 0:
                    wait(pe, s_vst, n + 1)
                wait(pe, s_exp, NU * n + QC * (k + 1))
                for j in range(QC):
                    v0 = hh * (HD + 1)
                    last = nc.tensor.matmul(acc[32 * j:32 * j + 32, :], vst[:, par, t, v0:v0 + 32],
                                            prob[:, k % PR, j, :], start=(t == 0), stop=(t == KT - 1))
                last.then_inc(s_pv, 1)

            def prologue():
                ct = Count(0, start=True)
                pe.wait_ge(s_op4[0], LOADS4)
                for j in range(NMAX):
                    maxima(ct, 0, j)
                rows_of_max(ct, 0)
                pe.wait_ge(s_op4[1], LOADS4)
                for j in range(LEAD):
                    maxima(ct, 1, j)

            def pair(n, it, par, has_prev, has_next, has_then):
                ct = Count(n, last=not has_next)
                wait(pe, s_op[par], LOADS * (it + 1))
                wait(pe, s_mr[par], 64 * (it + 1))
                steps = plan(has_prev, has_next, has_then)
                for k in range(KK):
                    scores(n, par, k, 0)
                    scores(n, par, k, 1)
                    for op, j in steps[k]:
                        if op == MAXNEXT:
                            maxima(ct, 1 - par, j)
                        elif op == MAXTHEN:
                            if j == 0:
                                wait(pe, s_op4[par], LOADS4 * (it + 2))
                            maxima(ct, par, j)
                        elif op == ROWMAX:
                            rows_of_max(ct, n + 1)
                        elif op == OUT:
                            outputs(ct, n - j, j)
                    scores(n, par, k, 2)
                    scores(n, par, k, 3)
                    if k > 0:
                        values(n, par, k - 1)
                    elif has_prev:
                        values(n - 1, 1 - par, KK - 1)

            def epilogue():
                values(NP - 1, 1, KK - 1)
                ct = Count(NP - 1, last=True)
                ct.next(0)
                ct.next(1)
                outputs(ct, NP - 1, 1)

            every_pair(pe, prologue, pair, epilogue)

        @block.vector
        def _(dve):
            def maxima(ct, j):
                t, half = j // NHALF, j % NHALF
                for s in range(2):
                    wait(dve, s_full[s], ct.next(s))
                    nc.vector.tensor_reduce(nmh[:, s, t, half:half + 1], ring[:, s, :], AX.X, ALU.max,
                                            negate=True).then_inc(s_free[s], 1)

            def rows_of_max(ct, n):
                for s in range(2):
                    wait(dve, s_free[s], ct.n[s])
                nc.vector.tensor_tensor(nm[:, :], nmh[:, :, :, 0].rearrange("p h t -> p (h t)"),
                                        nmh[:, :, :, 1].rearrange("p h t -> p (h t)"), ALU.min
                                        ).then_inc(s_comb, 1)
                wait(dve, s_full[0], ct.next(0))
                if not (isinstance(n, int) and n == 0):
                    wait(dve, s_mr_prev[0], s_mr_prev[1])
                nc.vector.tensor_copy(nmr[:, 0, :], ring[0:2 * KT, 0, 0:P]).then_inc(s_nmr1, 1)
                wait(dve, s_nmr1, n + 1)
                nc.vector.tensor_tensor(nmr[:, 1, :], ring[0:2 * KT, 0, 0:P], nmr[:, 0, :], ALU.subtract
                                        ).then_inc(s_free[0], 1)

            s_mr_prev = [None, None]

            def outputs(ct, n, hh):
                s = 1 - hh
                wait(dve, s_full[s], ct.next(s))
                wait(dve, s_free[s], ct.n[s] - 1)
                got = ring[:, s, 0:CH].rearrange("p (c j w) -> p c j w", c=TT, j=QC)
                r = rec[:, hh, :].rearrange("p (c j) -> p c j", j=QC)
                nc.vector.reciprocal(r, got[:, :, :, HD]).then_inc(s_rec, 1)
                wait(dve, s_rec, 2 * n + hh + 1)
                dst = att[:, bass.ds(n, 1), :, hh * HD:(hh + 1) * HD].rearrange(
                    "p a (j c) w -> p c (a j) w", c=TT)
                nc.vector.tensor_tensor(dst, got[:, :, :, 0:HD], r[:, :, :, None].to_broadcast([P, TT, QC, HD]),
                                        ALU.mult).then_inc(s_free[s], 1)

            def read_acc(n, hh):
                wait(dve, s_pv, KK * n + KT * (hh + 1))
                nc.vector.tensor_copy(osb[:, hh, :], acc[:, :]).then_inc(s_o, 1)

            def prologue():
                ct = Count(0, start=True)
                for j in range(NMAX):
                    maxima(ct, j)
                rows_of_max(ct, 0)
                for j in range(LEAD):
                    maxima(ct, j)

            def pair(n, it, par, has_prev, has_next, has_then):
                ct = Count(n, last=not has_next)
                steps = plan(has_prev, has_next, has_then)
                for k in range(KK):
                    if k == 1 and has_prev:
                        read_acc(n - 1, 1)
                    if k == KT + 1:
                        read_acc(n, 0)
                    for op, j in steps[k]:
                        if op == MAXNEXT or op == MAXTHEN:
                            maxima(ct, j)
                        elif op == ROWMAX:
                            s_mr_prev[0], s_mr_prev[1] = s_mr[par], 64 * (it + 1)
                            rows_of_max(ct, n + 1)
                        elif op == OUT:
                            outputs(ct, n - j, j)

            def epilogue():
                read_acc(NP - 1, 1)
                ct = Count(NP - 1, last=True)
                ct.next(0)
                ct.next(1)
                outputs(ct, NP - 1, 1)

            every_pair(dve, prologue, pair, epilogue)


def moe_stage(nc, x1_dram, f_dram, att, woT, ln2_w, gateT, w1T, w2T, w3T, out):
    B, L, _ = x1_dram.shape
    NI = L // CH
    NE, _, FI = w1T.shape
    KF = FI // P
    assert B == 2 and NE == 8

    with ExitStack() as ctx:
        def sb(name, shape, dt=F32):
            return ctx.enter_context(nc.sbuf_tensor(name, shape, dt))

        def ps(name, shape, dt=F32):
            return ctx.enter_context(nc.psum_tensor(name, shape, dt))

        def sem(name):
            return ctx.enter_context(nc.semaphore(name))

        w1 = sb("w1", [P, NE, KM, FI])
        w3 = sb("w3", [P, NE, KM, FI])
        w2 = sb("w2", [P, NE, KF, DM])
        wo = sb("wo", [P, KM, DM])
        gate = sb("gate", [P, KM, NE])
        ln2 = sb("ln2", [P, KM])
        ident = sb("m_ident", [P, P])
        epsc = sb("m_epsc", [P, 1])
        iota = sb("iota", [P, NE])
        attc = sb("attc", [P, TT, DM])
        attT = sb("attT", [P, KM, CH])
        fc = sb("fc", [P, TT, DM])
        xr = sb("xr", [P, TT, DM])
        stats = sb("m_stats", [P, TT, 6])
        mv = sb("m_mv", [P, TT, 2])
        sd = sb("m_sd", [P, TT])
        rs = sb("m_rs", [P, TT])
        lg = sb("lg", [P, TT, NE])
        top = sb("top", [P, TT, 8])
        idx = sb("idx", [P, TT, 8], U32)
        idf = sb("idf", [P, TT, 2])
        dif = sb("dif", [P, TT])
        ex = sb("ex", [P, TT])
        den = sb("den", [P, TT])
        sh = sb("sh", [P, 2, TT])
        one = sb("one", [P, TT, NE])
        gT = sb("gT", [P, 2, KM, CH])
        share = sb("share", [P, 2, TT, NE])
        acc = sb("m_acc", [P, 2, TT, DM])
        sl = sb("sl", [P, 2, CH])
        mid = sb("mid", [P, 2, KF, CH])
        a_ps = ps("a_ps", [P, 2, CH])
        c_ps = ps("c3_ps", [P, 2, CH])
        o_ps = ps("o_ps", [P, TT, DM])
        fill = ps("m_fill", [P, 2, CH])

        s_w = sem("m_w")
        s_we = [sem(f"m_we{e}") for e in range(NE)]
        s_id = sem("m_id")
        s_set = sem("m_set")
        s_f = sem("m_f")
        s_xr = sem("m_xr")
        s_at = sem("m_at")
        s_full = [sem("m_full0"), sem("m_full1")]
        s_free = [sem("m_free0"), sem("m_free1")]
        s_st = sem("m_st")
        s_sd = sem("m_sd_s")
        s_rs = sem("m_rs_s")
        s_g = sem("m_g")
        s_top = sem("m_top")
        s_ex = sem("m_ex")
        s_share = sem("m_share")
        s_base = sem("m_base")
        s_up = sem("m_up")
        s_sl = sem("m_sl")
        s_mid = sem("m_mid")
        s_dn = sem("m_dn")
        s_acc = sem("m_acc_s")
        s_out = [sem("m_out0"), sem("m_out1")]

        FB = (4, 3)
        NTOP = 6

        def every_chunk(eng, prologue, chunk, epilogue=None):
            prologue()
            for b in range(2):
                chunk(0, b, b > 0, True)
            if NI > 2:
                with eng.Fori(1, NI - 1) as i:
                    for b in range(2):
                        chunk(i, b, True, True)
            for b in range(2):
                chunk(NI - 1, b, True, b == 0)
            if epilogue:
                epilogue()

        def nxt(i, b):
            return (i, 1) if b == 0 else (i + 1, 0)

        def prv(i, b):
            return (i, 0) if b == 1 else (i - 1, 1)

        def tokens(dram, i, b):
            return dram[b, bass.ds(i * CH, CH), :].rearrange("(t p) e -> p t e", p=P)

        block = ctx.enter_context(nc.Block())

        @block.sync
        def _(sp):
            def load(i, b):
                c = 2 * i + b
                wait_apart(sp, s_base, c, s_w)
                wait_apart(sp, s_g, c, s_w)
                sp.dma_start(fc[:, :, :], tokens(f_dram, i, b)).then_inc(s_f, 16)
                sp.dma_start(xr[:, :, :], tokens(x1_dram, i, b)).then_inc(s_xr, 16)

            def prologue():
                sp.dma_start(wo[:, :, :], woT.rearrange("(k p) e -> p k e", p=P)).then_inc(s_w, 16)
                sp.dma_start(gate[:, :, :], gateT.rearrange("(k p) e -> p k e", p=P)).then_inc(s_w, 16)
                with nc.allow_non_contiguous_dma(reason="one small vector, once"):
                    sp.dma_start(ln2[:, :], ln2_w.rearrange("(k p) -> p k", p=P)).then_inc(s_w, 16)
                load(0, 0)
                for e in range(NE):
                    for dst, src in ((w1, w1T), (w3, w3T), (w2, w2T)):
                        sp.dma_start(dst[:, e], src[e].rearrange("(k p) e -> p k e", p=P)).then_inc(s_we[e], 16)
                sp.wait_ge(s_w, 16)
                load(0, 1)

            def store(i, b):
                c = 2 * i + b
                wait_apart(sp, s_acc, NE * (c + 1), s_w)
                sp.dma_start(tokens(out, i, b), acc[:, b]).then_inc(s_out[b], 16)

            def chunk(i, b, has_prev, has_next):
                if has_prev:
                    store(*prv(i, b))
                if has_next and not (isinstance(i, int) and i == NI - 1):
                    load(*nxt(*nxt(i, b)))

            every_chunk(sp, prologue, chunk, lambda: store(NI - 1, 1))
            for b in range(2):
                sp.wait_ge(s_out[b], 16 * NI)

        @block.gpsimd
        def _(pool):
            nc.gpsimd.memset(ident[:, :], 0.0).then_inc(s_id, 1)
            nc.gpsimd.memset(epsc[:, :], EPS).then_inc(s_set, 1)
            nc.gpsimd.iota(iota[:, :], pattern=[[1, NE]], base=0, channel_multiplier=0,
                           allow_small_or_imprecise_dtypes=True).then_inc(s_set, 1)
            pool.wait_ge(s_id, 1)
            nc.gpsimd.affine_select(out=ident[:, :], in_=ident[:, :], compare_op=ALU.not_equal, fill=1.0,
                                    base=0, pattern=[[-1, P]], channel_multiplier=1).then_inc(s_id, 1)

            def order(i, b):
                c = 2 * i + b
                wait_apart(pool, s_full[1], FB[1] * c, s_id)
                for t in range(TT):
                    src = att[:, b * HP:(b + 1) * HP, bass.ds(i * TT + t, 1), :]
                    last = nc.gpsimd.tensor_copy(attc[:, t, :].rearrange("p (n w) -> p n w", n=HP),
                                                 src.rearrange("p n o w -> p (n o) w"))
                last.then_inc(s_at, 1)

            def base(i, b):
                c = 2 * i + b
                wait(pool, s_xr, 16 * (c + 1))
                for bank in range(2):
                    wait(pool, s_free[bank], FB[bank] * c + 2)
                wait(pool, s_out[b], 16 * i)
                nc.gpsimd.tensor_tensor(acc[:, b], fc[:, :, :], xr[:, :, :], ALU.add).then_inc(s_base, 1)

            def prologue():
                order(0, 0)
                base(0, 0)

            def chunk(i, b, has_prev, has_next):
                if has_next:
                    order(*nxt(i, b))
                    base(*nxt(i, b))

            every_chunk(pool, prologue, chunk)

        @block.scalar
        def _(act):
            act.wait_ge(s_w, 48)
            act.wait_ge(s_set, 2)

            def prep(c, b, e):
                if e == 1:
                    for k in range(KM):
                        wait(act, s_full[k], FB[k] * c + 1)
                        nc.scalar.copy(attT[:, k, :], fill[:, k, :]).then_inc(s_free[k], 1)
                if e == 3:
                    wait(act, s_st, 4 * c + 4)
                    nc.scalar.activation(sd[:, :], mv[:, :, 1], ACT.Sqrt, bias=epsc[:, 0:1]).then_inc(s_sd, 1)
                if e == 4:
                    wait(act, s_dn, NE * (c - 1))
                    for k in range(KM):
                        wait(act, s_full[k], FB[k] * c + 3)
                        nc.scalar.activation(gT[:, b, k, :], fill[:, k, :], ACT.Identity,
                                             scale=ln2[:, k:k + 1]).then_inc(s_free[k], 1)
                if e == 6:
                    wait(act, s_top, NTOP * c + 4)
                    nc.scalar.activation(ex[:, :], dif[:, :], ACT.Exp).then_inc(s_ex, 1)

            def prologue():
                for e in range(NE):
                    prep(0, 0, e)

            def chunk(i, b, has_prev, has_next):
                c = 2 * i + b
                for e in range(NE):
                    for m in range(KF):
                        n = KF * (NE * c + e) + m
                        wait(act, s_up, n + 1)
                        wait(act, s_mid, n - 1)
                        nc.scalar.activation(sl[:, m % 2, :], a_ps[:, m % 2, :], ACT.Silu).then_inc(s_sl, 1)
                    if has_next:
                        prep(c + 1, 1 - b, e)

            every_chunk(act, prologue, chunk)

        @block.tensor
        def _(pe):
            pe.wait_ge(s_w, 48)
            pe.wait_ge(s_id, 2)

            def turn(dsts, src):
                for k in range(KM):
                    for t in range(TT):
                        last = nc.tensor.transpose(fill[:, k, t * P:(t + 1) * P],
                                                   src[:, t, k * P:(k + 1) * P], ident[:, :])
                    last.then_inc(s_full[k], 1)
                    if k + 1 < KM:
                        dsts()

            def prep(c, b, e):
                if e == 1:
                    wait(pe, s_at, c + 1)
                    wait(pe, s_free[0], FB[0] * c)
                    turn(lambda: wait(pe, s_free[1], FB[1] * c), attc)
                if e == 2:
                    for bank in range(2):
                        wait(pe, s_free[0], FB[0] * c + 1)
                        wait(pe, s_free[1], FB[1] * c + 1)
                        for t in (2 * bank, 2 * bank + 1):
                            for k in range(KM):
                                last = nc.tensor.matmul(fill[:, bank, (t % 2) * DM:(t % 2 + 1) * DM],
                                                        attT[:, k, t * P:(t + 1) * P], wo[:, k, :],
                                                        start=(k == 0), stop=(k == KM - 1))
                        last.then_inc(s_full[bank], 1)
                if e == 4:
                    wait(pe, s_g, c + 1)
                    wait(pe, s_free[0], FB[0] * c + 2)
                    turn(lambda: wait(pe, s_free[1], FB[1] * c + 2), attc)
                if e == 5:
                    wait(pe, s_free[0], FB[0] * c + 3)
                    wait(pe, s_free[1], FB[1] * c + 3)
                    for t in range(TT):
                        for k in range(KM):
                            last = nc.tensor.matmul(fill[:, 0, t * NE:(t + 1) * NE],
                                                    gT[:, b, k, t * P:(t + 1) * P], gate[:, k, :],
                                                    start=(k == 0), stop=(k == KM - 1))
                    last.then_inc(s_full[0], 1)

            def up(c, b, e):
                if isinstance(c, int) and c == 0:
                    pe.wait_ge(s_we[e], 48)
                for m in range(KF):
                    n = KF * (NE * c + e) + m
                    wait(pe, s_mid, n - 1)
                    for w, dst in ((w1, a_ps), (w3, c_ps)):
                        for k in range(KM):
                            last = nc.tensor.matmul(dst[:, m % 2, :], w[:, e, k, m * P:(m + 1) * P],
                                                    gT[:, b, k, :], start=(k == 0), stop=(k == KM - 1))
                    last.then_inc(s_up, 1)

            def down(c, e):
                n = NE * c + e
                wait(pe, s_mid, KF * (n + 1))
                wait(pe, s_acc, n)
                for t in range(TT):
                    for m in range(KF):
                        last = nc.tensor.matmul(o_ps[:, t, :], mid[:, e % 2, m, t * P:(t + 1) * P],
                                                w2[:, e, m, :], start=(m == 0), stop=(m == KF - 1))
                last.then_inc(s_dn, 1)

            def prologue():
                for e in range(NE):
                    prep(0, 0, e)

            def chunk(i, b, has_prev, has_next):
                c = 2 * i + b
                for e in range(NE):
                    up(c, b, e)
                    if has_next:
                        prep(c + 1, 1 - b, e)
                    if e > 0:
                        down(c, e - 1)
                    elif has_prev:
                        down(c - 1, NE - 1)

            every_chunk(pe, prologue, chunk, lambda: down(2 * NI - 1, NE - 1))

        @block.vector
        def _(dve):
            dve.wait_ge(s_w, 48)
            dve.wait_ge(s_set, 2)

            def prep(c, b, e):
                if e == 2:
                    wait(dve, s_f, 16 * (c + 1))
                    for bank in range(2):
                        wait(dve, s_full[bank], FB[bank] * c + 2)
                        part = flat(fc[:, 2 * bank:2 * bank + 2, :])
                        ins = nc.vector.tensor_tensor(part, fill[:, bank, :], part, ALU.add)
                        ins.then_inc(s_free[bank], 1)
                    wait(dve, s_free[0], FB[0] * c + 2)
                    wait(dve, s_free[1], FB[1] * c + 2)
                    for t in range(TT):
                        last = nc.vector.bn_stats(stats[:, t, :], fc[:, t, :])
                    last.then_inc(s_st, 1)
                    wait_apart(dve, s_st, 4 * c + 1, s_w)
                    for t in range(TT):
                        last = nc.vector.bn_aggr(mv[:, t, :], stats[:, t, :])
                    last.then_inc(s_st, 1)
                    wait(dve, s_st, 4 * c + 2)
                    nc.vector.tensor_tensor(mv[:, :, 0], mv[:, :, 0], mv[:, :, 0], ALU.mult).then_inc(s_st, 1)
                    wait(dve, s_st, 4 * c + 3)
                    nc.vector.tensor_tensor(mv[:, :, 1], mv[:, :, 1], mv[:, :, 0], ALU.add).then_inc(s_st, 1)
                if e == 3:
                    wait(dve, s_sd, c + 1)
                    nc.vector.reciprocal(rs[:, :], sd[:, :]).then_inc(s_rs, 1)
                    wait(dve, s_rs, c + 1)
                    for t in range(TT):
                        last = nc.vector.tensor_scalar(attc[:, t, :], fc[:, t, :], rs[:, t:t + 1],
                                                       None, ALU.mult)
                    last.then_inc(s_g, 1)
                if e == 5:
                    n = NTOP * c
                    wait(dve, s_full[0], FB[0] * c + 4)
                    nc.vector.tensor_copy(flat(lg[:, :, :]), fill[:, 0, 0:TT * NE]).then_inc(s_free[0], 1)
                    wait_apart(dve, s_free[0], FB[0] * c + 4, s_w)
                    for t in range(TT):
                        last = nc.vector.max(top[:, t, :], lg[:, t, :])
                    last.then_inc(s_top, 1)
                    wait_apart(dve, s_top, n + 1, s_w)
                    for t in range(TT):
                        last = nc.vector.max_index(idx[:, t, :], top[:, t, :], lg[:, t, :])
                    last.then_inc(s_top, 1)
                    wait(dve, s_top, n + 2)
                    nc.vector.tensor_copy(idf[:, :, :], idx[:, :, 0:2]).then_inc(s_top, 1)
                    nc.vector.tensor_tensor(dif[:, :], top[:, :, 1], top[:, :, 0], ALU.subtract
                                            ).then_inc(s_top, 1)
                if e == 6:
                    n = NTOP * c
                    wait(dve, s_ex, c + 1)
                    nc.vector.tensor_scalar(den[:, :], ex[:, :], 1.0, None, ALU.add).then_inc(s_top, 1)
                    wait(dve, s_top, n + 5)
                    nc.vector.reciprocal(sh[:, 0, :], den[:, :]).then_inc(s_top, 1)
                    wait(dve, s_top, n + 6)
                    nc.vector.tensor_tensor(sh[:, 1, :], sh[:, 0, :], ex[:, :], ALU.mult).then_inc(s_share, 1)
                    wait(dve, s_share, 4 * c + 1)
                    for t in range(TT):
                        last = nc.vector.tensor_scalar(share[:, b, t, :], iota[:, :], idf[:, t, 0:1],
                                                       sh[:, 0, t:t + 1], ALU.is_equal, ALU.mult)
                    last.then_inc(s_share, 1)
                    for t in range(TT):
                        last = nc.vector.tensor_scalar(one[:, t, :], iota[:, :], idf[:, t, 1:2],
                                                       sh[:, 1, t:t + 1], ALU.is_equal, ALU.mult)
                    last.then_inc(s_share, 1)
                    wait(dve, s_share, 4 * c + 3)
                    nc.vector.tensor_tensor(share[:, b], share[:, b], one[:, :, :], ALU.add).then_inc(s_share, 1)

            def products(c, b, e):
                for m in range(KF):
                    n = KF * (NE * c + e) + m
                    wait(dve, s_sl, n + 1)
                    if m == 0:
                        wait(dve, s_dn, NE * c + e - 1)
                    nc.vector.tensor_tensor(mid[:, e % 2, m, :], sl[:, m % 2, :], c_ps[:, m % 2, :],
                                            ALU.mult).then_inc(s_mid, 1)

            def add(c, b, e):
                n = NE * c + e
                if e == 0:
                    wait(dve, s_base, c + 1)
                    wait(dve, s_share, 4 * c + 4)
                wait(dve, s_dn, n + 1)
                wait(dve, s_acc, n)
                for t in range(TT):
                    last = nc.vector.scalar_tensor_tensor(
                        out=acc[:, b, t, :], in0=o_ps[:, t, :], scalar=share[:, b, t, e:e + 1],
                        in1=acc[:, b, t, :], op0=ALU.mult, op1=ALU.add)
                last.then_inc(s_acc, 1)

            def prologue():
                for e in range(NE):
                    prep(0, 0, e)

            def chunk(i, b, has_prev, has_next):
                c = 2 * i + b
                for e in range(NE):
                    products(c, b, e)
                    if e > 0:
                        add(c, b, e - 1)
                    elif has_prev:
                        add(c - 1, 1 - b, NE - 1)
                    if has_next:
                        prep(c + 1, 1 - b, e)

            every_chunk(dve, prologue, chunk, lambda: add(2 * NI - 1, 1, NE - 1))


def build(nc, a, out):
    B, L, _ = a["x"].shape
    x1 = nc.dram_tensor("x1_scratch", [B, L, DM], F32, kind="Internal").ap()
    f = nc.dram_tensor("f_scratch", [B, L, DM], F32, kind="Internal").ap()
    b_rows = nc.dram_tensor("b_rows", [2, NS, CH], F32, kind="Internal").ap()
    parts = nc.dram_tensor("parts", [2, 3, B * DM, L], BF16, kind="Internal").ap()

    ssm_stage(nc, a["x"], a["W_inT"], a["conv_w"], a["conv_b"], a["W_xT"], a["dt_w"], a["dt_b"],
              a["A_log"], a["D_param"], a["W_outT"], x1, b_rows)
    with nc.sbuf_tensor("att", [P, B * HP, L // P, 2 * HD], F32) as att:
        with nc.sbuf_tensor("v_all", [P, B * HP, L // P, VW], F32) as v_all:
            qkv_stage(nc, x1, a["ln1_w"], a["wqT"], a["wkT"], a["wvT"], f, parts, v_all)
            attention_stage(nc, parts, v_all, att, B, L)
        moe_stage(nc, x1, f, att, a["woT"], a["ln2_w"], a["gateT"], a["w1T"], a["w2T"], a["w3T"], out)


def kernel(**inputs):
    import numpy as np
    import concourse.bacc as bacc
    from concourse.bass_utils import run_bass_kernel_spmd

    a = {k.replace("L0_attn_", "").replace("L0_ffn_", ""): np.asarray(v) for k, v in inputs.items()}
    W_x = a["W_x"]
    laid = dict(
        x=a["x"], W_inT=a["W_in"].T, conv_w=a["conv_w"], conv_b=a["conv_b"],
        W_xT=np.concatenate([W_x[1:], W_x[:1]], axis=0).T, dt_w=a["dt_w"][:, 0], dt_b=a["dt_b"],
        A_log=a["A_log"], D_param=a["D_param"], W_outT=a["W_out"].T,
        ln1_w=a["ln1_w"], ln2_w=a["ln2_w"], wqT=a["wq"].T, wkT=a["wk"].T, wvT=a["wv"].T, woT=a["wo"].T,
        gateT=a["gate_w"].T, w1T=a["w1"].transpose(0, 2, 1), w2T=a["w2"].transpose(0, 2, 1),
        w3T=a["w3"].transpose(0, 2, 1))
    nc = bacc.Bacc("TRN2", target_bir_lowering=False, num_devices=1)
    arrays, aps = {}, {}
    for name, v in laid.items():
        v = np.ascontiguousarray(v)
        arrays[f"in_{name}"] = v
        aps[name] = nc.dram_tensor(f"in_{name}", v.shape, mybir.dt.from_np(v.dtype), kind="ExternalInput").ap()
    out = nc.dram_tensor("out_x", a["x"].shape, F32, kind="ExternalOutput").ap()
    build(nc, aps, out)
    r = run_bass_kernel_spmd(nc, [arrays], core_ids=[0])
    return r.results[0]["out_x"]
```

```python
from contextlib import ExitStack

import concourse.bass as bass
from concourse import mybir

ALU = mybir.AluOpType
ACT = mybir.ActivationFunctionType
AX = mybir.AxisListType
F32 = mybir.dt.float32
BF16 = mybir.dt.bfloat16
U32 = mybir.dt.uint32

P = 128
CH = 512
TT = CH // P
DM = 256
KM = DM // P
DI = 512
KI = DI // P
NS = 16
TAPS = 4
EPS = 1e-5


def wait(eng, sem, value):
    if isinstance(value, int) and value <= 0:
        return
    eng.wait_ge(sem, value)


def wait_apart(eng, sem, value, met):
    if isinstance(value, int):
        wait(eng, sem, value)
    else:
        eng.compute_val(value)
        eng.wait_ge(met, 1)
        eng.wait_ge(sem, value)


def flat(ap):
    return ap.rearrange("p a b -> p (a b)")


def ssm_stage(nc, x, W_inT, conv_w, conv_b, W_xT, dt_w, dt_b, A_log, D_param, W_outT, x1_dram, b_dram):
    B, L, _ = x.shape
    NI = L // CH
    assert B == 2 and L % CH == 0 and NI >= 2
    RING = 4

    with ExitStack() as ctx:
        def sb(name, shape, dt=F32):
            return ctx.enter_context(nc.sbuf_tensor(name, shape, dt))

        def ps(name, shape, dt=F32):
            return ctx.enter_context(nc.psum_tensor(name, shape, dt))

        def sem(name):
            return ctx.enter_context(nc.semaphore(name))

        w_in = sb("w_in", [P, KM, 2 * DI])
        w_x = sb("w_x", [P, KI, 2 * NS + 1])
        w_out = sb("w_out", [P, KI, DM])
        cw = sb("cw", [P, KI, TAPS])
        cb = sb("cb", [P, KI])
        dtw = sb("dtw", [P, KI])
        dtb = sb("dtb", [P, KI])
        dpar = sb("dpar", [P, KI])
        alog = sb("alog", [P, KI, NS])
        aneg = sb("aneg", [P, KI, NS])
        ident = sb("ident", [P, P])
        epsc = sb("epsc", [P, 1])
        xn = sb("xn", [P, TT, DM])
        stats = sb("stats", [P, TT, 6])
        mv = sb("mv", [P, TT, 2])
        sd = sb("sd", [P, TT])
        rs = sb("rs", [P, TT])
        xT = sb("xT", [P, KM, CH])
        HALO = TAPS - 1
        xs = sb("xs", [P, KI, HALO + CH])
        halo = sb("halo", [P, 2, KI, HALO])
        tA = xs[:, :, 0:CH]
        tB = sb("tB", [P, KI, CH])
        xc = sb("xc", [P, 2, KI, CH])
        zs = sb("zs", [P, 2, KI, CH])
        dt = sb("dt", [P, 2, KI, CH])
        u = sb("u", [P, 2, KI, CH])
        pr = sb("pr", [2 * NS + 1, 2, CH])
        state = sb("state", [P, 2, NS, KI])
        dA = sb("dA", [P, 2, KI, CH])
        h = sb("h", [P, 2, KI, CH])
        prod = sb("prod", [P, RING, KI, CH])
        bb = sb("bb", [P, RING, CH])
        xres = sb("xres", [P, TT, DM])
        x1 = sb("x1", [P, TT, DM])

        y_ps = ps("y_ps", [P, KI, CH])
        c_ps = ps("c_ps", [P, 2, CH])
        fill = ps("fill", [P, 2, CH])

        s_w = sem("s_w")
        s_id = sem("s_id")
        s_set = sem("s_set")
        s_aexp = sem("s_aexp")
        s_an = sem("s_an")
        s_x = sem("s_x")
        s_xr = sem("s_xr")
        s_st1 = sem("s_st1")
        s_mv = sem("s_mv")
        s_sd = sem("s_sd")
        s_rs = sem("s_rs")
        s_xn = sem("s_xn")
        s_xT = sem("s_xT")
        s_full = [sem("s_full0"), sem("s_full1")]
        s_free = [sem("s_free0"), sem("s_free1")]
        s_halo = sem("s_halo")
        s_hsave = sem("s_hsave")
        s_tap = sem("s_tap")
        s_cv = sem("s_cv")
        s_xc = sem("s_xc")
        s_zs = sem("s_zs")
        s_prst = sem("s_prst")
        s_b = [sem(f"s_b{k}") for k in range(RING)]
        s_abs = sem("s_abs")
        s_e = sem("s_e")
        s_ln = sem("s_ln")
        s_q = sem("s_q")
        s_sp = sem("s_sp")
        s_dt = sem("s_dt")
        s_u = sem("s_u")
        s_da = sem("s_da")
        s_bx = sem("s_bx")
        s_h = sem("s_h")
        s_stt = sem("s_stt")
        s_cb = sem("s_cb")
        s_hc = sem("s_hc")
        s_ys = sem("s_ys")
        s_g1 = sem("s_g1")
        s_g = sem("s_g")
        s_x1st = sem("s_x1st")

        NW = 10
        FA = 6

        def prep_fill(c):
            return 0 if isinstance(c, int) and c == 0 else (FA + 1) * c - 1

        def out_fill(c, last):
            return (FA + 1) * c + (FA if last else 2 * FA)

        def tokens(c, i, b):
            return b, bass.ds(i * CH, CH)

        def nxt(i, b):
            return (i, 1) if b == 0 else (i + 1, 0)

        def prv(i, b):
            return (i, 0) if b == 1 else (i - 1, 1)

        def every_chunk(eng, prologue, chunk):
            prologue()
            for b in range(2):
                chunk(0, b, b > 0, True)
            if NI > 2:
                with eng.Fori(1, NI - 1) as i:
                    for b in range(2):
                        chunk(i, b, True, True)
            for b in range(2):
                chunk(NI - 1, b, True, b == 0)

        block = ctx.enter_context(nc.Block())

        @block.sync
        def _(sp):
            sp.dma_start(w_in[:, :, :], W_inT.rearrange("(k p) e -> p k e", p=P)).then_inc(s_w, 16)
            sp.dma_start(w_x[:, :, :], W_xT.rearrange("(k p) e -> p k e", p=P)).then_inc(s_w, 16)
            sp.dma_start(w_out[:, :, :], W_outT.rearrange("(k p) e -> p k e", p=P)).then_inc(s_w, 16)
            sp.dma_start(cw[:, :, :], conv_w.rearrange("(k p) e -> p k e", p=P)).then_inc(s_w, 16)
            sp.dma_start(alog[:, :, :], A_log.rearrange("(k p) e -> p k e", p=P)).then_inc(s_w, 16)
            with nc.allow_non_contiguous_dma(reason="five small vectors, once"):
                for dst, src in ((cb, conv_b), (dtw, dt_w), (dtb, dt_b), (dpar, D_param)):
                    sp.dma_start(dst[:, :], src.rearrange("(k p) -> p k", p=P)).then_inc(s_w, 16)

            def load_x(i, b):
                c = 2 * i + b
                bt, ts = tokens(c, i, b)
                wait_apart(sp, s_full[1], prep_fill(c - 1) + 1 if not (isinstance(c, int) and c == 0) else 0, s_w)
                sp.dma_start(xn[:, :, :], x[bt, ts, :].rearrange("(t p) e -> p t e", p=P)).then_inc(s_x, 16)

            def load_b(i, b, n):
                c = 2 * i + b
                wait_apart(sp, s_prst, 16 * (c + 1), s_w)
                wait_apart(sp, s_bx, NS * c + n - RING + 1, s_w)
                sp.dma_start(bb[:, n % RING, :], b_dram[b, n:n + 1, :].partition_broadcast(P)
                             ).then_inc(s_b[n % RING], 16)

            def store_rows(i, b):
                c = 2 * i + b
                wait_apart(sp, s_free[0], prep_fill(c) + FA, s_w)
                sp.dma_start(b_dram[b, :, :], pr[0:NS, b, :]).then_inc(s_prst, 16)
                load_b(i, b, 0)
                load_b(i, b, 1)

            def wait_x1(c, last):
                for bank in range(2):
                    wait_apart(sp, s_free[bank], out_fill(c, last) + 1, s_w)

            def store_x1(i, b, last=False):
                c = 2 * i + b
                bt, ts = tokens(c, i, b)
                wait_x1(c, last)
                sp.dma_start(x1_dram[bt, ts, :].rearrange("(t p) e -> p t e", p=P), x1[:, :, :]
                             ).then_inc(s_x1st, 16)

            def load_res(i, b):
                c = 2 * i + b
                bt, ts = tokens(c, i, b)
                if not (isinstance(c, int) and c == 0):
                    wait_x1(c - 1, False)
                sp.dma_start(xres[:, :, :], x[bt, ts, :].rearrange("(t p) e -> p t e", p=P)).then_inc(s_xr, 16)

            def prologue():
                load_x(0, 0)
                store_rows(0, 0)
                load_x(0, 1)

            def chunk(i, b, has_prev, has_next):
                for n in range(NS):
                    if n + 2 < NS:
                        load_b(i, b, n + 2)
                    if n == 4:
                        if has_prev:
                            store_x1(*prv(i, b))
                        load_res(i, b)
                    if n == 15 and has_next:
                        store_rows(*nxt(i, b))
                        if not (isinstance(i, int) and i == NI - 1):
                            load_x(*nxt(*nxt(i, b)))

            every_chunk(sp, prologue, chunk)
            store_x1(NI - 1, 1, True)
            sp.wait_ge(s_x1st, 16 * 2 * NI)

        @block.gpsimd
        def _(pool):
            nc.gpsimd.memset(ident[:, :], 0.0).then_inc(s_id, 1)
            nc.gpsimd.memset(epsc[:, :], EPS).then_inc(s_set, 1)
            nc.gpsimd.memset(halo[:, :, :, :], 0.0).then_inc(s_set, 1)
            nc.gpsimd.memset(state[:, :, :, :], 0.0).then_inc(s_set, 1)
            pool.wait_ge(s_id, 1)
            nc.gpsimd.affine_select(out=ident[:, :], in_=ident[:, :], compare_op=ALU.not_equal, fill=1.0,
                                    base=0, pattern=[[-1, P]], channel_multiplier=1).then_inc(s_id, 1)
            pool.wait_ge(s_aexp, 1)
            nc.gpsimd.tensor_scalar(aneg[:, :, :], aneg[:, :, :], -1.0, None, ALU.mult).then_inc(s_an, 1)

            def step_sizes(i, b):
                c = 2 * i + b
                wait(pool, s_ln, 2 * (c + 1))
                wait(pool, s_q, c + 1)
                nc.gpsimd.tensor_tensor(u[:, b], u[:, b], tB[:, :, :], ALU.subtract).then_inc(s_sp, 1)
                wait(pool, s_sp, c + 1)
                nc.gpsimd.tensor_tensor(dt[:, b], dt[:, b], u[:, b], ALU.add).then_inc(s_dt, 1)
                wait(pool, s_dt, c + 1)
                nc.gpsimd.tensor_tensor(u[:, b], dt[:, b], xc[:, b], ALU.mult).then_inc(s_u, 1)

            def chunk(i, b, has_prev, has_next):
                c = 2 * i + b
                wait(pool, s_u, c + 1)
                for n in range(NS):
                    wait(pool, s_b[n % RING], 16 * ((NS // RING) * c + n // RING + 1))
                    wait(pool, s_ys, NS * c + n - RING + 1)
                    nc.gpsimd.tensor_tensor(
                        prod[:, n % RING], u[:, b],
                        bb[:, n % RING, None, :].to_broadcast([P, KI, CH]), ALU.mult).then_inc(s_bx, 1)
                if has_next:
                    step_sizes(*nxt(i, b))

            every_chunk(pool, lambda: step_sizes(0, 0), chunk)

        @block.scalar
        def _(act):
            act.wait_ge(s_w, 16 * (NW - 1))
            act.wait_ge(s_set, 3)
            nc.scalar.activation(aneg[:, :, :], alog[:, :, :], ACT.Exp).then_inc(s_aexp, 1)

            def root(c):
                wait(act, s_mv, c + 1)
                nc.scalar.activation(sd[:, :], mv[:, :, 1], ACT.Sqrt, bias=epsc[:, 0:1]).then_inc(s_sd, 1)

            def take_xT(c, b):
                f = prep_fill(c)
                for k in range(KM):
                    wait(act, s_full[k], f + 1)
                    nc.scalar.copy(xT[:, k, :], fill[:, k, :]).then_inc(s_free[k], 1)
                wait(act, s_dt, c)
                wait(act, s_hsave, c - 1)
                nc.scalar.copy(xs[:, :, 0:HALO], halo[:, b]).then_inc(s_halo, 1)

            def take_conv_in(c, b, d):
                bank, f = d % 2, prep_fill(c) + 1 + d // 2
                wait(act, s_full[bank], f + 1)
                nc.scalar.copy(xs[:, d, HALO:], fill[:, bank, :]).then_inc(s_tap, 1)
                wait(act, s_g, c - 1)
                nc.scalar.activation(xc[:, b, d, :], fill[:, bank, :], ACT.Identity,
                                     bias=cb[:, d:d + 1], scale=cw[:, d, HALO:HALO + 1]
                                     ).then_inc(s_free[bank], 1)

            def take_z(c, b, d, has_prev):
                bank, f = d % 2, prep_fill(c) + 3 + d // 2
                wait(act, s_full[bank], f + 1)
                nc.scalar.copy(zs[:, b, d, :], fill[:, bank, :]).then_inc(s_free[bank], 1)

            def silus(c, b):
                wait(act, s_cv, KI * HALO * (c + 1))
                nc.scalar.copy(halo[:, b], xs[:, :, CH:CH + HALO]).then_inc(s_hsave, 1)
                nc.scalar.activation(flat(xc[:, b]), flat(xc[:, b]), ACT.Silu).then_inc(s_xc, 1)
                for k in range(2):
                    wait(act, s_free[k], prep_fill(c) + 5)
                nc.scalar.activation(flat(zs[:, b]), flat(zs[:, b]), ACT.Silu).then_inc(s_zs, 1)

            def take_rows(c, b):
                wait(act, s_full[0], prep_fill(c) + FA)
                nc.scalar.copy(pr[:, b, :], fill[0:2 * NS + 1, 0, :]).then_inc(s_free[0], 1)

            def softplus(c, b):
                wait(act, s_full[1], prep_fill(c) + FA)
                wait(act, s_hsave, c + 1)
                for d in range(KI):
                    nc.scalar.activation(tA[:, d, :], fill[:, 1, :], ACT.Abs,
                                         bias=dtb[:, d:d + 1], scale=dtw[:, d:d + 1]).then_inc(s_abs, 1)
                    last = nc.scalar.activation(dt[:, b, d, :], fill[:, 1, :], ACT.Relu,
                                                bias=dtb[:, d:d + 1], scale=dtw[:, d:d + 1])
                last.then_inc(s_free[1], 1)
                wait(act, s_abs, KI * (c + 1))
                nc.scalar.activation(tA, tA, ACT.Exp, scale=-1.0).then_inc(s_e, 1)
                wait(act, s_e, c + 1)
                nc.scalar.activation(tB[:, :, :], tA, ACT.Identity, bias=1.0).then_inc(s_ln, 1)
                nc.scalar.activation(u[:, b], tA, ACT.Ln, bias=1.0).then_inc(s_ln, 1)

            def save_state(c, b, n):
                wait(act, s_h, NS * c + n + 1)
                nc.scalar.copy(state[:, b, n, :], h[:, n % 2, :, CH - 1]).then_inc(s_stt, 1)

            def prep(c, b, n, has_prev=True):
                if n == 0:
                    root(c)
                if n == 2:
                    take_xT(c, b)
                if 3 <= n < 7:
                    take_conv_in(c, b, n - 3)
                if 7 <= n < 11:
                    take_z(c, b, n - 7, has_prev)
                if n == 11:
                    silus(c, b)
                if n == 12:
                    take_rows(c, b)
                if n == 13:
                    softplus(c, b)

            def prologue():
                for n in range(NS):
                    prep(0, 0, n)
                act.wait_ge(s_an, 1)

            def chunk(i, b, has_prev, has_next):
                c = 2 * i + b
                wait(act, s_dt, c + 1)
                for n in range(NS):
                    if n >= 2:
                        save_state(c, b, n - 2)
                    else:
                        wait(act, s_h, NS * c + n - 1)
                    for d in range(KI):
                        nc.scalar.activation(dA[:, n % 2, d, :], dt[:, b, d, :], ACT.Exp,
                                             scale=aneg[:, d, n:n + 1]).then_inc(s_da, 1)
                    if has_next:
                        prep(c + 1, 1 - b, n)
                save_state(c, b, NS - 2)
                save_state(c, b, NS - 1)

            every_chunk(act, prologue, chunk)

        @block.tensor
        def _(pe):
            pe.wait_ge(s_w, 16 * (NW - 1))
            pe.wait_ge(s_id, 2)

            def transposes(c):
                wait(pe, s_xn, c + 1)
                for k in range(KM):
                    wait(pe, s_free[k], prep_fill(c))
                    for t in range(TT):
                        last = nc.tensor.transpose(fill[:, k, t * P:(t + 1) * P],
                                                   xn[:, t, k * P:(k + 1) * P], ident[:, :])
                    last.then_inc(s_full[k], 1)

            def project_in(c, e):
                bank, f = e % 2, prep_fill(c) + 1 + e // 2
                if e == 0:
                    wait(pe, s_free[1], f)
                wait(pe, s_free[bank], f)
                for k in range(KM):
                    last = nc.tensor.matmul(fill[:, bank, :], w_in[:, k, e * P:(e + 1) * P], xT[:, k, :],
                                            start=(k == 0), stop=(k == KM - 1))
                last.then_inc(s_full[bank], 1)

            def project_rows(c, b):
                f = prep_fill(c) + FA - 1
                wait(pe, s_xc, c + 1)
                wait(pe, s_free[0], f)
                for k in range(KI):
                    last = nc.tensor.matmul(fill[0:2 * NS + 1, 0, :], w_x[:, k, :], xc[:, b, k, :],
                                            start=(k == 0), stop=(k == KI - 1))
                last.then_inc(s_full[0], 1)

            def row(r):
                return ident[0:2 * NS + 1, r:r + 1].to_broadcast([2 * NS + 1, P])

            def spread_dt(c, b):
                f = prep_fill(c) + FA - 1
                wait(pe, s_free[0], prep_fill(c) + FA)
                wait(pe, s_free[1], f)
                nc.tensor.matmul(fill[:, 1, :], row(2 * NS), pr[:, b, :],
                                 start=True, stop=True).then_inc(s_full[1], 1)

            def spread_c(c, b, n):
                wait(pe, s_hc, NS * c + n - 1)
                nc.tensor.matmul(c_ps[:, n % 2, :], row(NS + n), pr[:, b, :],
                                 start=True, stop=True).then_inc(s_cb, 1)

            def prep(c, b, n):
                if n == 2:
                    transposes(c)
                if 3 <= n < 11:
                    project_in(c, n - 3)
                if n == 12:
                    project_rows(c, b)
                if n == 13:
                    spread_dt(c, b)

            def prologue():
                for n in range(NS):
                    prep(0, 0, n)
                spread_c(0, 0, 0)
                spread_c(0, 0, 1)

            def chunk(i, b, has_prev, has_next):
                c = 2 * i + b
                for n in range(NS):
                    if n == 0:
                        wait(pe, s_g1, KI * c)
                    wait(pe, s_hc, NS * c + n + 1)
                    for d in range(KI):
                        last = nc.tensor.matmul(y_ps[:, d, :], ident[:, :], prod[:, n % RING, d, :],
                                                start=(n == 0), stop=(n == NS - 1))
                    last.then_inc(s_ys, 1)
                    if n + 2 < NS:
                        spread_c(c, b, n + 2)
                    if has_next and n + 2 < NS:
                        prep(c + 1, 1 - b, n + 2)
                if has_next:
                    spread_c(c + 1, 1 - b, 0)
                    spread_c(c + 1, 1 - b, 1)
                wait(pe, s_g, c + 1)
                f = out_fill(c, not has_next)
                for t in range(TT):
                    bank = t // 2
                    if t % 2 == 0:
                        wait(pe, s_free[bank], f)
                    for d in range(KI):
                        last = nc.tensor.matmul(fill[:, bank, (t % 2) * DM:(t % 2 + 1) * DM],
                                                zs[:, b, d, t * P:(t + 1) * P], w_out[:, d, :],
                                                start=(d == 0), stop=(d == KI - 1))
                    if t % 2 == 1:
                        last.then_inc(s_full[bank], 1)

            every_chunk(pe, prologue, chunk)

        @block.vector
        def _(dve):
            def norm_stats(c):
                wait(dve, s_x, 16 * (c + 1))
                for t in range(TT):
                    last = nc.vector.bn_stats(stats[:, t, :], xn[:, t, :])
                last.then_inc(s_st1, 1)
                wait_apart(dve, s_st1, c + 1, s_w)
                for t in range(TT):
                    last = nc.vector.bn_aggr(mv[:, t, :], stats[:, t, :])
                last.then_inc(s_mv, 1)

            def norm_apply(c):
                wait(dve, s_sd, c + 1)
                nc.vector.reciprocal(rs[:, :], sd[:, :]).then_inc(s_rs, 1)
                wait(dve, s_rs, c + 1)
                for t in range(TT):
                    last = nc.vector.tensor_scalar(xn[:, t, :], xn[:, t, :], mv[:, t, 0:1], rs[:, t:t + 1],
                                                   ALU.subtract, ALU.mult)
                last.then_inc(s_xn, 1)

            def add_taps(c, b, d):
                wait(dve, s_free[d % 2], prep_fill(c) + 2 + d // 2)
                wait(dve, s_halo, c + 1)
                for k in range(HALO):
                    if k:
                        wait(dve, s_cv, HALO * (KI * c + d) + k)
                    nc.vector.scalar_tensor_tensor(
                        out=xc[:, b, d, :], in0=xs[:, d, k:k + CH], scalar=cw[:, d, k:k + 1],
                        in1=xc[:, b, d, :], op0=ALU.mult, op1=ALU.add).then_inc(s_cv, 1)

            def rounding(c):
                wait(dve, s_ln, 2 * c + 1)
                nc.vector.scalar_tensor_tensor(out=tB[:, :, :], in0=tB[:, :, :], scalar=-1.0, in1=tA,
                                               op0=ALU.add, op1=ALU.subtract).then_inc(s_q, 1)

            def residual(c, last):
                wait(dve, s_xr, 16 * (c + 1))
                wait(dve, s_x1st, 16 * c)
                f = out_fill(c, last)
                for bank in range(2):
                    wait(dve, s_full[bank], f + 1)
                    nc.vector.tensor_tensor(flat(x1[:, 2 * bank:2 * bank + 2, :]), fill[:, bank, :],
                                            flat(xres[:, 2 * bank:2 * bank + 2, :]), ALU.add
                                            ).then_inc(s_free[bank], 1)

            def prep(c, b, n):
                if n == 0:
                    norm_stats(c)
                if n == 1:
                    norm_apply(c)
                if 4 <= n < 8:
                    add_taps(c, b, n - 4)
                if n == 13:
                    rounding(c)

            def scans(c, b, n):
                wait(dve, s_bx, NS * c + n + 1)
                wait(dve, s_stt, NS * c + n - 1)
                wait(dve, s_hc, NS * c + n - 1)
                for d in range(KI):
                    wait(dve, s_da, KI * (NS * c + n) + d + 1)
                    last = nc.vector.tensor_tensor_scan(
                        h[:, n % 2, d, :], dA[:, n % 2, d, :], prod[:, n % RING, d, :],
                        state[:, b, n, d:d + 1], ALU.mult, ALU.add)
                last.then_inc(s_h, 1)

            def times_c(c, b, n):
                wait(dve, s_h, NS * c + n + 1)
                wait(dve, s_cb, NS * c + n + 1)
                nc.vector.tensor_tensor(prod[:, n % RING], h[:, n % 2],
                                        c_ps[:, n % 2, None, :].to_broadcast([P, KI, CH]), ALU.mult
                                        ).then_inc(s_hc, 1)

            def prologue():
                dve.wait_ge(s_w, 16 * (NW - 1))
                dve.wait_ge(s_set, 3)
                for n in range(NS):
                    prep(0, 0, n)

            def chunk(i, b, has_prev, has_next):
                c = 2 * i + b
                for n in range(NS + 1):
                    if n < NS:
                        scans(c, b, n)
                    if n > 0:
                        times_c(c, b, n - 1)
                    if n == 1 and has_prev:
                        residual(c - 1, False)
                    if n < NS and has_next:
                        prep(c + 1, 1 - b, n)
                wait(dve, s_ys, NS * (c + 1))
                for d in range(KI):
                    nc.vector.scalar_tensor_tensor(
                        out=xc[:, b, d, :], in0=xc[:, b, d, :], scalar=dpar[:, d:d + 1], in1=y_ps[:, d, :],
                        op0=ALU.mult, op1=ALU.add).then_inc(s_g1, 1)
                wait(dve, s_g1, KI * (c + 1))
                wait(dve, s_zs, c + 1)
                nc.vector.tensor_tensor(zs[:, b], xc[:, b], zs[:, b], ALU.mult).then_inc(s_g, 1)

            every_chunk(dve, prologue, chunk)
            residual(2 * NI - 1, True)


NH = 16
HD = DM // NH
HP = NH // 2
VW = 2 * (HD + 1)


def qkv_stage(nc, x1_dram, ln1_w, wqT, wkT, wvT, f_dram, parts_dram, v_all):
    B, L, _ = x1_dram.shape
    NI = L // CH
    NC = B * NI
    assert B == 2

    with ExitStack() as ctx:
        def sb(name, shape, dt=F32):
            return ctx.enter_context(nc.sbuf_tensor(name, shape, dt))

        def ps(name, shape, dt=F32):
            return ctx.enter_context(nc.psum_tensor(name, shape, dt))

        def sem(name):
            return ctx.enter_context(nc.semaphore(name))

        wq = sb("wq", [P, KM, DM])
        wk = sb("wk", [P, KM, DM])
        wv = sb("wv", [P, KM, DM])
        ln1 = sb("ln1", [P, KM])
        ident = sb("q_ident", [P, P])
        epsc = sb("q_epsc", [P, 1])
        xa = sb("xa", [P, 2, TT, DM])
        an = sb("an", [P, 2, TT, DM])
        stats = sb("q_stats", [P, TT, 6])
        mv = sb("q_mv", [P, 2, TT, 2])
        sd = sb("q_sd", [P, 2, TT])
        rs = sb("q_rs", [P, 2, TT])
        ms = sb("q_ms", [P, 2, TT])
        rr = sb("q_rr", [P, 2, TT])
        aT = sb("aT", [P, KM, CH])
        part = sb("part", [P, 3, 2 * KM, CH], BF16)
        rest = sb("rest", [P, 2 * KM, CH])
        tr_ps = ps("tr_ps", [P, KM, CH])
        qk_ps = ps("qk_ps", [P, 2 * KM, CH])
        v_ps = ps("v_ps", [P, TT, DM])

        s_w = sem("q_w")
        s_id = sem("q_id")
        s_set = sem("q_set")
        s_x = [sem("q_x0"), sem("q_x1")]
        s_st = sem("q_st")
        s_sd = sem("q_sd_s")
        s_rs = sem("q_rs_s")
        s_ms = sem("q_ms_s")
        s_f = sem("q_f")
        s_a = sem("q_a")
        s_fst = sem("q_fst")
        s_tr = sem("q_tr")
        s_aT = sem("q_aT")
        s_qk = sem("q_qk")
        s_v = sem("q_v")
        s_p1 = sem("q_p1")
        s_r = sem("q_r")
        s_p2 = sem("q_p2")
        s_p3 = sem("q_p3")
        s_pst = sem("q_pst")
        s_vout = sem("q_vout")

        block = ctx.enter_context(nc.Block())

        def every_chunk(eng, front, back):
            front(0, 0)
            front(0, 1)
            back(0, 0)
            with eng.Fori(1, NI) as i:
                front(i, 0)
                back(i - 1, 1)
                front(i, 1)
                back(i, 0)
            back(NI - 1, 1)

        @block.sync
        def _(sp):
            for dst, src in ((wq, wqT), (wk, wkT), (wv, wvT)):
                sp.dma_start(dst[:, :, :], src.rearrange("(k p) e -> p k e", p=P)).then_inc(s_w, 16)
            with nc.allow_non_contiguous_dma(reason="one small vector, once"):
                sp.dma_start(ln1[:, :], ln1_w.rearrange("(k p) -> p k", p=P)).then_inc(s_w, 16)

            def tokens(dram, i, b):
                return dram[b, bass.ds(i * CH, CH), :].rearrange("(t p) e -> p t e", p=P)

            def front(i, b):
                c = 2 * i + b
                wait_apart(sp, s_a, c - 1, s_w)
                wait_apart(sp, s_fst, 16 * (c - 1), s_w)
                sp.dma_start(xa[:, b], tokens(x1_dram, i, b)).then_inc(s_x[b], 16)

            def back(i, b):
                c = 2 * i + b
                wait_apart(sp, s_f, c + 1, s_w)
                sp.dma_start(tokens(f_dram, i, b), xa[:, b]).then_inc(s_fst, 16)
                for s, ready in enumerate((s_p1, s_p2, s_p3)):
                    wait_apart(sp, ready, c + 1, s_w)
                    for m in range(2):
                        dst = parts_dram[m, s, b * DM:(b + 1) * DM, bass.ds(i * CH, CH)]
                        sp.dma_start(dst.rearrange("(k p) l -> p k l", p=P),
                                     part[:, s, m * KM:(m + 1) * KM, :]).then_inc(s_pst, 16)

            every_chunk(sp, front, back)
            sp.wait_ge(s_fst, 16 * NC)
            sp.wait_ge(s_pst, 16 * 6 * NC)

        @block.gpsimd
        def _(pool):
            nc.gpsimd.memset(ident[:, :], 0.0).then_inc(s_id, 1)
            nc.gpsimd.memset(epsc[:, :], EPS).then_inc(s_set, 1)
            for hh in range(2):
                col = hh * (HD + 1) + HD
                nc.gpsimd.memset(v_all[:, :, :, col:col + 1], 1.0).then_inc(s_set, 1)
            pool.wait_ge(s_id, 1)
            nc.gpsimd.affine_select(out=ident[:, :], in_=ident[:, :], compare_op=ALU.not_equal, fill=1.0,
                                    base=0, pattern=[[-1, P]], channel_multiplier=1).then_inc(s_id, 1)

        @block.scalar
        def _(act):
            act.wait_ge(s_w, 64)
            act.wait_ge(s_set, 3)

            def front(i, b):
                c = 2 * i + b
                wait(act, s_st, 2 * c + 2)
                nc.scalar.activation(sd[:, b, :], mv[:, b, :, 1], ACT.Sqrt, bias=epsc[:, 0:1]
                                     ).then_inc(s_sd, 1)
                wait(act, s_ms, 2 * c + 2)
                nc.scalar.activation(sd[:, b, :], ms[:, b, :], ACT.Sqrt, bias=epsc[:, 0:1]
                                     ).then_inc(s_sd, 1)

            def back(i, b):
                c = 2 * i + b
                wait(act, s_tr, c + 1)
                wait(act, s_v, c)
                for k in range(KM):
                    nc.scalar.activation(aT[:, k, :], tr_ps[:, k, :], ACT.Identity,
                                         scale=ln1[:, k:k + 1]).then_inc(s_aT, 1)
                wait(act, s_qk, c + 1)
                wait(act, s_pst, 16 * 6 * c)
                nc.scalar.copy(part[:, 0], qk_ps[:, :, :]).then_inc(s_p1, 1)
                wait(act, s_r, c + 1)
                nc.scalar.copy(part[:, 1], rest[:, :, :]).then_inc(s_p2, 1)

            every_chunk(act, front, back)

        @block.tensor
        def _(pe):
            pe.wait_ge(s_w, 64)
            pe.wait_ge(s_id, 2)

            def chunk(i, b):
                c = 2 * i + b
                wait(pe, s_a, c + 1)
                wait(pe, s_aT, 2 * c)
                for k in range(KM):
                    for t in range(TT):
                        last = nc.tensor.transpose(tr_ps[:, k, t * P:(t + 1) * P],
                                                   an[:, b, t, k * P:(k + 1) * P], ident[:, :])
                last.then_inc(s_tr, 1)
                wait(pe, s_aT, 2 * c + 2)
                wait(pe, s_r, c)
                for m, w in enumerate((wq, wk)):
                    for o in range(KM):
                        for k in range(KM):
                            last = nc.tensor.matmul(qk_ps[:, m * KM + o, :], w[:, k, o * P:(o + 1) * P],
                                                    aT[:, k, :], start=(k == 0), stop=(k == KM - 1))
                last.then_inc(s_qk, 1)
                wait(pe, s_vout, c)
                for t in range(TT):
                    for k in range(KM):
                        last = nc.tensor.matmul(v_ps[:, t, :], aT[:, k, t * P:(t + 1) * P], wv[:, k, :],
                                                start=(k == 0), stop=(k == KM - 1))
                last.then_inc(s_v, 1)

            chunk(0, 0)
            chunk(0, 1)
            with pe.Fori(1, NI) as i:
                chunk(i, 0)
                chunk(i, 1)

        @block.vector
        def _(dve):
            dve.wait_ge(s_set, 3)

            def front(i, b):
                c = 2 * i + b
                wait(dve, s_x[b], 16 * (i + 1))
                for t in range(TT):
                    last = nc.vector.bn_stats(stats[:, t, :], xa[:, b, t, :])
                last.then_inc(s_st, 1)
                wait_apart(dve, s_st, 2 * c + 1, s_w)
                for t in range(TT):
                    last = nc.vector.bn_aggr(mv[:, b, t, :], stats[:, t, :])
                last.then_inc(s_st, 1)
                wait(dve, s_sd, 2 * c + 1)
                nc.vector.reciprocal(rs[:, b, :], sd[:, b, :]).then_inc(s_rs, 1)
                wait(dve, s_rs, 2 * c + 1)
                nc.vector.tensor_tensor(ms[:, b, :], mv[:, b, :, 1], rs[:, b, :], ALU.mult).then_inc(s_ms, 1)
                for t in range(TT):
                    last = nc.vector.tensor_scalar(xa[:, b, t, :], xa[:, b, t, :], mv[:, b, t, 0:1],
                                                   rs[:, b, t:t + 1], ALU.subtract, ALU.mult)
                last.then_inc(s_f, 1)
                wait(dve, s_ms, 2 * c + 1)
                nc.vector.tensor_tensor(ms[:, b, :], ms[:, b, :], rs[:, b, :], ALU.mult).then_inc(s_ms, 1)
                wait(dve, s_sd, 2 * c + 2)
                nc.vector.reciprocal(rr[:, b, :], sd[:, b, :]).then_inc(s_rs, 1)
                wait(dve, s_rs, 2 * c + 2)
                wait(dve, s_f, c + 1)
                wait(dve, s_tr, c - 1)
                for t in range(TT):
                    last = nc.vector.tensor_scalar(an[:, b, t, :], xa[:, b, t, :], rr[:, b, t:t + 1],
                                                   None, ALU.mult)
                last.then_inc(s_a, 1)

            def back(i, b):
                c = 2 * i + b
                wait(dve, s_p1, c + 1)
                nc.vector.tensor_tensor(rest[:, :, :], qk_ps[:, :, :], part[:, 0], ALU.subtract).then_inc(s_r, 1)
                wait_apart(dve, s_v, c + 1, s_w)
                for t in range(TT):
                    dst = v_all[:, b * HP:(b + 1) * HP, bass.ds(i * TT + t, 1), :]
                    dst = dst.rearrange("p a o (h w) -> p (a o) h w", h=2)[:, :, :, 0:HD]
                    src = v_ps[:, t, :].rearrange("p (a h w) -> p a h w", h=2, w=HD)
                    last = nc.vector.tensor_copy(dst, src)
                last.then_inc(s_vout, 1)
                wait(dve, s_p2, c + 1)
                wait(dve, s_r, c + 1)
                nc.vector.tensor_tensor(part[:, 2], rest[:, :, :], part[:, 1], ALU.subtract).then_inc(s_p3, 1)

            every_chunk(dve, front, back)


def attention_stage(nc, parts_dram, v_all, att, B, L):
    NP = B * HP
    QC = L // CH
    KT = L // P
    KK = 2 * KT
    LEAD = 4
    HW = 2 * CH
    NHALF = L // HW
    NMAX = KT * NHALF
    assert NMAX == KK and QC == 4 and NP % 2 == 0 and NP >= 6
    ROWS = 6 * HD + 2
    SC = float(HD) ** -0.5
    SR = 3
    PR = 4

    with ExitStack() as ctx:
        def sb(name, shape, dt=F32):
            return ctx.enter_context(nc.sbuf_tensor(name, shape, dt))

        def ps(name, shape, dt=F32):
            return ctx.enter_context(nc.psum_tensor(name, shape, dt))

        def sem(name):
            return ctx.enter_context(nc.semaphore(name))

        qs = sb("qs", [ROWS, 2, 2, L], BF16)
        ks = sb("ks", [ROWS, 2, 2, L], BF16)
        q4 = sb("q4", [P, 2, L], BF16)
        k4 = sb("k4", [P, 2, L], BF16)
        vst = sb("vst", [P, 2, KT, 64])
        prob = sb("prob", [P, PR, QC, CH])
        osb = sb("osb", [P, 2, CH])
        nmh = sb("nmh", [P, 2, KT, NHALF])
        nm = sb("nm", [P, 2 * KT])
        nmr = sb("nmr", [2 * KT, 2, P], BF16)
        rec = sb("rec", [P, 2, QC * TT])
        ident = sb("a_ident", [P, P])
        s_ps = ps("s_ps", [P, SR, CH])
        acc = ps("acc", [P, CH])
        ring = ps("ring", [P, 2, HW])

        s_id = sem("a_id")
        s_one = sem("a_one")
        s_op = [sem("a_op0"), sem("a_op1")]
        s_op4 = [sem("a_op40"), sem("a_op41")]
        s_mr = [sem("a_mr0"), sem("a_mr1")]
        s_vst = sem("a_vst")
        s_S = sem("a_S")
        s_exp = sem("a_exp")
        s_pv = sem("a_pv")
        s_o = sem("a_o")
        s_full = [sem("a_full0"), sem("a_full1")]
        s_free = [sem("a_free0"), sem("a_free1")]
        s_comb = sem("a_comb")
        s_nmr1 = sem("a_nmr1")
        s_rec = sem("a_rec")

        Q_PARTS = (0, 0, 1, 1, 0, 2)
        K_PARTS = (0, 1, 0, 1, 2, 0)
        LOADS = 16 * 2 * 2 * 6
        LOADS4 = 16 * 2 * 2 * 4

        MAXNEXT, MAXTHEN, ROWMAX, OUT = "maximum, next pair", "maximum, pair after", "rows of the maximum", "output"

        def plan(has_prev, has_next, has_then):
            steps = [[] for _ in range(KK)]
            if has_prev:
                steps[2].append((OUT, 1))
            steps[KT + 2].append((OUT, 0))
            if has_next:
                for j in range(LEAD, NMAX):
                    steps[j - LEAD].append((MAXNEXT, j))
                steps[NMAX - LEAD].append((ROWMAX, 0))
            if has_then:
                for j in range(LEAD):
                    steps[NMAX - LEAD + j].append((MAXTHEN, j))
            return steps

        def fills_before(pair, s):
            first = (NMAX + 1 + LEAD, NMAX + LEAD)[s]
            return first + (NMAX + 2 - s) * pair - (1 if s == 0 and not (isinstance(pair, int) and pair == 0) else 0)

        class Count:
            def __init__(self, pair, last=False, start=False):
                if start:
                    self.n = [0, 0]
                else:
                    self.n = [fills_before(pair, s) - (LEAD if last else 0) for s in range(2)]

            def next(self, s):
                self.n[s] = self.n[s] + 1
                return self.n[s]

        def every_pair(eng, prologue, pair, epilogue=None):
            prologue()
            pair(0, 0, 0, False, True, True)
            pair(1, 0, 1, True, True, True)
            with eng.Fori(1, NP // 2 - 1) as it:
                for par in range(2):
                    pair(2 * it + par, it, par, True, True, True)
            pair(NP - 2, NP // 2 - 1, 0, True, True, False)
            pair(NP - 1, NP // 2 - 1, 1, True, False, False)
            if epilogue:
                epilogue()

        block = ctx.enter_context(nc.Block())

        @block.sync
        def _(sp):
            def load(dst, at, par_hh, m, order, n, s):
                for g, part in enumerate(order):
                    src = parts_dram[m, part, bass.ds(n * 2 * HD + par_hh[-1] * HD, HD), :]
                    rows = slice(at + g * HD, at + (g + 1) * HD)
                    out = dst[rows, par_hh[0], par_hh[1], :] if dst is qs or dst is ks else dst[rows, par_hh[0], :]
                    sp.dma_start(out, src).then_inc(s, 16)

            def load_stack(n, par):
                wait_apart(sp, s_S, KK * QC * (n - 1), s_one)
                for hh in range(2):
                    load(qs, 0, (par, hh), 0, Q_PARTS, n, s_op[par])
                    load(ks, 0, (par, hh), 1, K_PARTS, n, s_op[par])

            def load_lead(n, par):
                if not isinstance(n, int) or n > 1:
                    for s in range(2):
                        wait_apart(sp, s_free[s], fills_before(n - 2, s), s_one)
                for hh in range(2):
                    load(q4, 64 * hh, (par, hh), 0, Q_PARTS[0:4], n, s_op4[par])
                    load(k4, 64 * hh, (par, hh), 1, K_PARTS[0:4], n, s_op4[par])

            def max_rows(n, par, fills):
                wait_apart(sp, s_free[0], fills, s_one)
                for hh in range(2):
                    for s in range(2):
                        sp.dma_start(qs[6 * HD + s:6 * HD + s + 1, par, hh, :],
                                     nmr[hh * KT:(hh + 1) * KT, s, :]).then_inc(s_mr[par], 16)

            def prologue():
                load_lead(0, 0)
                load_stack(0, 0)
                load_lead(1, 1)
                load_stack(1, 1)
                max_rows(0, 0, NMAX + 1)

            def pair(n, it, par, has_prev, has_next, has_then):
                if has_prev and has_next:
                    load_stack(n + 1, 1 - par)
                if has_then:
                    load_lead(n + 2, par)
                if has_next:
                    ct = Count(n)
                    for ops in plan(has_prev, has_next, has_then):
                        for op, j in ops:
                            if op == ROWMAX:
                                max_rows(n + 1, 1 - par, ct.next(0))
                            elif op == OUT:
                                ct.next(1 - j)
                            elif op == MAXNEXT or op == MAXTHEN:
                                ct.next(0)
                                ct.next(1)

            every_pair(sp, prologue, pair)

        @block.gpsimd
        def _(pool):
            nc.gpsimd.memset(ident[:, :], 0.0).then_inc(s_id, 1)
            nc.gpsimd.memset(vst[:, :, :, :], 0.0).then_inc(s_one, 1)
            for par in range(2):
                pool.wait_ge(s_one, par + 1)
                nc.gpsimd.memset(ks[6 * HD:6 * HD + 2, par, :, :], 1.0).then_inc(s_one, 1)
            pool.wait_ge(s_id, 1)
            pool.wait_ge(s_one, 3)
            nc.gpsimd.affine_select(out=ident[:, :], in_=ident[:, :], compare_op=ALU.not_equal, fill=1.0,
                                    base=0, pattern=[[-1, P]], channel_multiplier=1).then_inc(s_id, 1)

            def pair(n, it, par, has_prev, has_next, has_then):
                wait_apart(pool, s_pv, KK * (n - 1), s_id)
                src = v_all[:, bass.ds(n, 1), :, :].rearrange("p a t w -> p (a t) w")
                nc.gpsimd.tensor_copy(vst[:, par, :, 0:VW], src).then_inc(s_vst, 1)

            every_pair(pool, lambda: None, pair)

        @block.scalar
        def _(act):
            def pair(n, it, par, has_prev, has_next, has_then):
                for k in range(KK):
                    wait(act, s_pv, KK * n + k - PR + 1)
                    for j in range(QC):
                        m = QC * k + j
                        wait(act, s_S, KK * QC * n + m + 1)
                        nc.scalar.activation(prob[:, k % PR, j, :], s_ps[:, m % SR, :], ACT.Exp,
                                             scale=SC).then_inc(s_exp, 1)

            every_pair(act, lambda: None, pair)

        @block.tensor
        def _(pe):
            pe.wait_ge(s_id, 2)
            pe.wait_ge(s_one, 3)
            NU = KK * QC

            def maxima(ct, par, j):
                t, half = j // NHALF, j % NHALF
                for s in range(2):
                    wait(pe, s_free[s], ct.next(s) - 1)
                for b in range(2):
                    for hh in range(2):
                        r = slice(64 * hh, 64 * hh + 64)
                        at = half * HW + b * CH
                        ins = nc.tensor.matmul(ring[:, hh, b * CH:(b + 1) * CH],
                                               q4[r, par, t * P:(t + 1) * P], k4[r, par, at:at + CH],
                                               start=True, stop=True)
                        if b == 1:
                            ins.then_inc(s_full[hh], 1)

            def rows_of_max(ct, n):
                wait(pe, s_free[0], ct.next(0) - 1)
                wait(pe, s_comb, n + 1)
                nc.tensor.transpose(ring[0:2 * KT, 0, 0:P], nm[:, :], ident[:, :]).then_inc(s_full[0], 1)

            def outputs(ct, n, hh):
                s = 1 - hh
                wait(pe, s_free[s], ct.next(s) - 1)
                wait(pe, s_o, 2 * n + hh + 1)
                for t in range(TT):
                    last = nc.tensor.transpose(ring[:, s, t * P:(t + 1) * P], osb[:, hh, t * P:(t + 1) * P],
                                               ident[:, :])
                last.then_inc(s_full[s], 1)

            def scores(n, par, k, j):
                m = QC * k + j
                hh, t = k // KT, k % KT
                back = m - SR if m >= SR else max(x for x in range(NU) if x % SR == m % SR) - NU
                wait(pe, s_exp, NU * n + back + 1)
                nc.tensor.matmul(s_ps[:, m % SR, :], ks[:, par, hh, t * P:(t + 1) * P],
                                 qs[:, par, hh, j * CH:(j + 1) * CH], start=True, stop=True).then_inc(s_S, 1)

            def values(n, par, k):
                hh, t = k // KT, k % KT
                if t == 0:
                    wait(pe, s_o, 2 * n + hh)
                if k == 0:
                    wait(pe, s_vst, n + 1)
                wait(pe, s_exp, NU * n + QC * (k + 1))
                for j in range(QC):
                    v0 = hh * (HD + 1)
                    last = nc.tensor.matmul(acc[32 * j:32 * j + 32, :], vst[:, par, t, v0:v0 + 32],
                                            prob[:, k % PR, j, :], start=(t == 0), stop=(t == KT - 1))
                last.then_inc(s_pv, 1)

            def prologue():
                ct = Count(0, start=True)
                pe.wait_ge(s_op4[0], LOADS4)
                for j in range(NMAX):
                    maxima(ct, 0, j)
                rows_of_max(ct, 0)
                pe.wait_ge(s_op4[1], LOADS4)
                for j in range(LEAD):
                    maxima(ct, 1, j)

            def pair(n, it, par, has_prev, has_next, has_then):
                ct = Count(n, last=not has_next)
                wait(pe, s_op[par], LOADS * (it + 1))
                wait(pe, s_mr[par], 64 * (it + 1))
                steps = plan(has_prev, has_next, has_then)
                for k in range(KK):
                    scores(n, par, k, 0)
                    scores(n, par, k, 1)
                    for op, j in steps[k]:
                        if op == MAXNEXT:
                            maxima(ct, 1 - par, j)
                        elif op == MAXTHEN:
                            if j == 0:
                                wait(pe, s_op4[par], LOADS4 * (it + 2))
                            maxima(ct, par, j)
                        elif op == ROWMAX:
                            rows_of_max(ct, n + 1)
                        elif op == OUT:
                            outputs(ct, n - j, j)
                    scores(n, par, k, 2)
                    scores(n, par, k, 3)
                    if k > 0:
                        values(n, par, k - 1)
                    elif has_prev:
                        values(n - 1, 1 - par, KK - 1)

            def epilogue():
                values(NP - 1, 1, KK - 1)
                ct = Count(NP - 1, last=True)
                ct.next(0)
                ct.next(1)
                outputs(ct, NP - 1, 1)

            every_pair(pe, prologue, pair, epilogue)

        @block.vector
        def _(dve):
            def maxima(ct, j):
                t, half = j // NHALF, j % NHALF
                for s in range(2):
                    wait(dve, s_full[s], ct.next(s))
                    nc.vector.tensor_reduce(nmh[:, s, t, half:half + 1], ring[:, s, :], AX.X, ALU.max,
                                            negate=True).then_inc(s_free[s], 1)

            def rows_of_max(ct, n):
                for s in range(2):
                    wait(dve, s_free[s], ct.n[s])
                nc.vector.tensor_tensor(nm[:, :], nmh[:, :, :, 0].rearrange("p h t -> p (h t)"),
                                        nmh[:, :, :, 1].rearrange("p h t -> p (h t)"), ALU.min
                                        ).then_inc(s_comb, 1)
                wait(dve, s_full[0], ct.next(0))
                if not (isinstance(n, int) and n == 0):
                    wait(dve, s_mr_prev[0], s_mr_prev[1])
                nc.vector.tensor_copy(nmr[:, 0, :], ring[0:2 * KT, 0, 0:P]).then_inc(s_nmr1, 1)
                wait(dve, s_nmr1, n + 1)
                nc.vector.tensor_tensor(nmr[:, 1, :], ring[0:2 * KT, 0, 0:P], nmr[:, 0, :], ALU.subtract
                                        ).then_inc(s_free[0], 1)

            s_mr_prev = [None, None]

            def outputs(ct, n, hh):
                s = 1 - hh
                wait(dve, s_full[s], ct.next(s))
                wait(dve, s_free[s], ct.n[s] - 1)
                got = ring[:, s, 0:CH].rearrange("p (c j w) -> p c j w", c=TT, j=QC)
                r = rec[:, hh, :].rearrange("p (c j) -> p c j", j=QC)
                nc.vector.reciprocal(r, got[:, :, :, HD]).then_inc(s_rec, 1)
                wait(dve, s_rec, 2 * n + hh + 1)
                dst = att[:, bass.ds(n, 1), :, hh * HD:(hh + 1) * HD].rearrange(
                    "p a (j c) w -> p c (a j) w", c=TT)
                nc.vector.tensor_tensor(dst, got[:, :, :, 0:HD], r[:, :, :, None].to_broadcast([P, TT, QC, HD]),
                                        ALU.mult).then_inc(s_free[s], 1)

            def read_acc(n, hh):
                wait(dve, s_pv, KK * n + KT * (hh + 1))
                nc.vector.tensor_copy(osb[:, hh, :], acc[:, :]).then_inc(s_o, 1)

            def prologue():
                ct = Count(0, start=True)
                for j in range(NMAX):
                    maxima(ct, j)
                rows_of_max(ct, 0)
                for j in range(LEAD):
                    maxima(ct, j)

            def pair(n, it, par, has_prev, has_next, has_then):
                ct = Count(n, last=not has_next)
                steps = plan(has_prev, has_next, has_then)
                for k in range(KK):
                    if k == 1 and has_prev:
                        read_acc(n - 1, 1)
                    if k == KT + 1:
                        read_acc(n, 0)
                    for op, j in steps[k]:
                        if op == MAXNEXT or op == MAXTHEN:
                            maxima(ct, j)
                        elif op == ROWMAX:
                            s_mr_prev[0], s_mr_prev[1] = s_mr[par], 64 * (it + 1)
                            rows_of_max(ct, n + 1)
                        elif op == OUT:
                            outputs(ct, n - j, j)

            def epilogue():
                read_acc(NP - 1, 1)
                ct = Count(NP - 1, last=True)
                ct.next(0)
                ct.next(1)
                outputs(ct, NP - 1, 1)

            every_pair(dve, prologue, pair, epilogue)


def moe_stage(nc, x1_dram, f_dram, att, woT, ln2_w, gateT, w1T, w2T, w3T, xg_dram, y_dram, out):
    B, L, _ = x1_dram.shape
    NI = L // CH
    NE, _, FI = w1T.shape
    KF = FI // P
    BT = L // P
    NT = B * BT
    SLOT_TILES = xg_dram.shape[0] // P
    assert B == 2 and NE == 8 and SLOT_TILES == slot_tiles(B * L, NE) and SLOT_TILES % 4 == 0
    ZC = 4

    with ExitStack() as ctx:
        def sb(name, shape, dt=F32):
            return ctx.enter_context(nc.sbuf_tensor(name, shape, dt))

        def ps(name, shape, dt=F32):
            return ctx.enter_context(nc.psum_tensor(name, shape, dt))

        def sem(name):
            return ctx.enter_context(nc.semaphore(name))

        w1 = sb("w1", [P, NE, KM, FI])
        w3 = sb("w3", [P, NE, KM, FI])
        w2 = sb("w2", [P, NE, KF, DM])
        ln2 = sb("ln2", [P, KM])
        ident = sb("m_ident", [P, P])
        g = sb("g", [P, NT, DM])
        sh = sb("sh", [P, 2, NT])
        pos = sb("pos", [P, 2, NT], U32)
        expert = sb("expert", [1, SLOT_TILES], U32)

        s_w = sem("m_w")
        s_we = sem("m_we")
        s_id = sem("m_id")
        s_set = sem("m_set")
        s_clear = sem("m_clear")

        with ExitStack() as ctx2:
            def sb2(name, shape, dt=F32):
                return ctx2.enter_context(nc.sbuf_tensor(name, shape, dt))

            def ps2(name, shape, dt=F32):
                return ctx2.enter_context(nc.psum_tensor(name, shape, dt))

            wo = sb2("wo", [P, KM, DM])
            gate = sb2("gate", [P, KM, NE])
            epsc = sb2("m_epsc", [P, 1])
            iota = sb2("iota", [P, NE])
            starts = sb2("starts", [P, NT])
            tiles = sb2("tiles", [1, SLOT_TILES])
            before = sb2("before", [P, P])
            ones = sb2("ones", [P, P])
            zero = sb2("zero", [P, ZC * DM])
            one = sb2("one", [P, NT])
            idf = sb2("idf", [P, 2, NT])
            dif = sb2("dif", [P, NT])

            s_f = [sem("m_f0"), sem("m_f1")]
            s_at = sem("m_at")
            s_t1 = sem("m_t1")
            s_aT = sem("m_aT")
            s_wo = sem("m_wo")
            s_h = sem("m_h")
            s_st = sem("m_st")
            s_sd = sem("m_sd_s")
            s_rs = sem("m_rs_s")
            s_g = sem("m_g")
            s_base = sem("m_base")
            s_t2 = sem("m_t2")
            s_gT = sem("m_gT")
            s_lg = sem("m_lg")
            s_lc = sem("m_lc")
            s_top = sem("m_top")
            s_ix = sem("m_ix")
            s_dif = sem("m_dif")
            s_r = sem("m_r")
            s_ex = sem("m_ex")
            s_cnt = sem("m_cnt")

            with ExitStack() as ctx3:
                def sb3(name, shape, dt=F32):
                    return ctx3.enter_context(nc.sbuf_tensor(name, shape, dt))

                def ps3(name, shape, dt=F32):
                    return ctx3.enter_context(nc.psum_tensor(name, shape, dt))

                attc = sb3("attc", [P, TT, DM])
                attT = sb3("attT", [P, KM, CH])
                gT = sb3("gT", [P, KM, CH])
                hc = sb3("hc", [P, 2, TT, DM])
                xr = sb3("xr", [P, 2, TT, DM])
                stats = sb3("m_stats", [P, TT, 6])
                mv = sb3("m_mv", [P, TT, 2])
                sd = sb3("m_sd", [P, TT])
                rs = sb3("m_rs", [P, TT])
                gs = sb3("gs", [P, 2, TT, DM])
                lgc = sb3("lgc", [P, 2, TT, NE])
                topc = sb3("topc", [P, 2, TT, 8])
                idxc = sb3("idxc", [P, 2, TT, 8], U32)
                t1_ps = ps3("t1_ps", [P, KM, CH])
                h_ps = ps3("h_ps", [P, TT, DM])
                t2_ps = ps3("t2_ps", [P, KM, CH])
                g_ps = ps3("g_ps", [P, CH])
                block = ctx3.enter_context(nc.Block())

                def every_chunk(eng, front, back):
                    front(0, 0)
                    front(0, 1)
                    back(0, 0)
                    with eng.Fori(1, NI) as i:
                        front(i, 0)
                        back(i - 1, 1)
                        front(i, 1)
                        back(i, 0)
                    back(NI - 1, 1)

                @block.sync
                def _(sp):
                    sp.dma_start(wo[:, :, :], woT.rearrange("(k p) e -> p k e", p=P)).then_inc(s_w, 16)
                    sp.dma_start(gate[:, :, :], gateT.rearrange("(k p) e -> p k e", p=P)).then_inc(s_w, 16)
                    with nc.allow_non_contiguous_dma(reason="one small vector, once"):
                        sp.dma_start(ln2[:, :], ln2_w.rearrange("(k p) -> p k", p=P)).then_inc(s_w, 16)

                    def front(i, b):
                        c = 2 * i + b
                        wait_apart(sp, s_base, c - 1, s_w)
                        wait_apart(sp, s_g, c - 1, s_w)
                        for dst, src in ((hc, f_dram), (xr, x1_dram)):
                            sp.dma_start(dst[:, b], src[b, bass.ds(i * CH, CH), :].rearrange(
                                "(t p) e -> p t e", p=P)).then_inc(s_f[b], 16)

                    def weights(i, b):
                        if isinstance(i, int) and i == 0:
                            for e in range(NE):
                                for dst, src in ((w1, w1T), (w3, w3T), (w2, w2T)):
                                    sp.dma_start(dst[:, e], src[e].rearrange("(k p) e -> p k e", p=P)
                                                 ).then_inc(s_we, 16)
                            sp.wait_ge(s_set, 6)
                            for n in range(SLOT_TILES // ZC):
                                rows = xg_dram[n * ZC * P:(n + 1) * ZC * P, :].rearrange("(p r) e -> p (r e)", r=ZC)
                                sp.dma_start(rows, zero[:, :]).then_inc(s_clear, 16)

                    front(0, 0)
                    front(0, 1)
                    weights(0, 0)
                    sp.wait_ge(s_w, 48)
                    with sp.Fori(1, NI) as i:
                        front(i, 0)
                        front(i, 1)

                @block.gpsimd
                def _(pool):
                    nc.gpsimd.memset(epsc[:, :], EPS).then_inc(s_set, 1)
                    nc.gpsimd.memset(ones[:, :], 1.0).then_inc(s_set, 1)
                    nc.gpsimd.memset(before[:, :], 1.0).then_inc(s_set, 1)
                    nc.gpsimd.memset(zero[:, :], 0.0).then_inc(s_set, 1)
                    nc.gpsimd.iota(iota[:, :], pattern=[[1, NE]], base=0, channel_multiplier=0,
                                   allow_small_or_imprecise_dtypes=True).then_inc(s_set, 1)
                    nc.gpsimd.iota(starts[:, :], pattern=[[P, NT]], base=0, channel_multiplier=0,
                                   allow_small_or_imprecise_dtypes=True).then_inc(s_set, 1)
                    nc.gpsimd.memset(ident[:, :], 0.0).then_inc(s_id, 1)
                    pool.wait_ge(s_set, 6)
                    pool.wait_ge(s_id, 1)
                    nc.gpsimd.affine_select(out=ident[:, :], in_=ident[:, :], compare_op=ALU.not_equal, fill=1.0,
                                            base=0, pattern=[[-1, P]], channel_multiplier=1).then_inc(s_id, 1)
                    nc.gpsimd.affine_select(out=before[:, :], in_=before[:, :], compare_op=ALU.is_gt, fill=0.0,
                                            base=0, pattern=[[1, P]], channel_multiplier=-1).then_inc(s_set, 1)
                    pool.wait_ge(s_set, 7)
                    nc.gpsimd.iota(tiles[:, :], pattern=[[1, SLOT_TILES]], base=0, channel_multiplier=0,
                                   allow_small_or_imprecise_dtypes=True).then_inc(s_set, 1)
                    pool.wait_ge(s_set, 8)

                    def front(i, b):
                        c = 2 * i + b
                        wait_apart(pool, s_t1, c, s_id)
                        for t in range(TT):
                            src = att[:, b * HP:(b + 1) * HP, bass.ds(i * TT + t, 1), :]
                            last = nc.gpsimd.tensor_copy(attc[:, t, :].rearrange("p (n w) -> p n w", n=HP),
                                                         src.rearrange("p n o w -> p (n o) w"))
                        last.then_inc(s_at, 1)

                    def back(i, b):
                        c = 2 * i + b
                        wait_apart(pool, s_f[b], 32 * (i + 1), s_id)
                        wait_apart(pool, s_h, 2 * (c + 1), s_id)
                        wait_apart(pool, s_at, c + 1, s_id)
                        for t in range(TT):
                            dst = att[:, b * HP:(b + 1) * HP, bass.ds(i * TT + t, 1), :]
                            last = nc.gpsimd.tensor_tensor(
                                dst.rearrange("p n o w -> p (n o) w"),
                                hc[:, b, t, :].rearrange("p (n w) -> p n w", n=HP),
                                xr[:, b, t, :].rearrange("p (n w) -> p n w", n=HP), ALU.add)
                        last.then_inc(s_base, 1)

                    every_chunk(pool, front, back)

                @block.scalar
                def _(act):
                    act.wait_ge(s_w, 48)
                    act.wait_ge(s_set, 6)

                    def front(i, b):
                        c = 2 * i + b
                        wait(act, s_t1, c + 1)
                        wait(act, s_wo, c)
                        nc.scalar.copy(attT[:, :, :], t1_ps[:, :, :]).then_inc(s_aT, 1)
                        wait(act, s_st, 4 * c + 4)
                        nc.scalar.activation(sd[:, :], mv[:, :, 1], ACT.Sqrt, bias=epsc[:, 0:1]).then_inc(s_sd, 1)

                    def back(i, b):
                        c = 2 * i + b
                        wait(act, s_t2, c + 1)
                        wait(act, s_lg, c)
                        for k in range(KM):
                            nc.scalar.activation(gT[:, k, :], t2_ps[:, k, :], ACT.Identity,
                                                 scale=ln2[:, k:k + 1]).then_inc(s_gT, 1)

                    every_chunk(act, front, back)

                @block.tensor
                def _(pe):
                    pe.wait_ge(s_w, 48)
                    pe.wait_ge(s_id, 2)

                    def turn(dst, tile):
                        for k in range(KM):
                            for t in range(TT):
                                last = nc.tensor.transpose(dst[:, k, t * P:(t + 1) * P], tile(t, k), ident[:, :])
                        return last

                    def front(i, b):
                        c = 2 * i + b
                        wait(pe, s_at, c + 1)
                        wait(pe, s_aT, c)
                        turn(t1_ps, lambda t, k: attc[:, t, k * P:(k + 1) * P]).then_inc(s_t1, 1)
                        wait(pe, s_aT, c + 1)
                        wait(pe, s_h, 2 * c)
                        for t in range(TT):
                            for k in range(KM):
                                last = nc.tensor.matmul(h_ps[:, t, :], attT[:, k, t * P:(t + 1) * P], wo[:, k, :],
                                                        start=(k == 0), stop=(k == KM - 1))
                        last.then_inc(s_wo, 1)

                    def back(i, b):
                        c = 2 * i + b
                        wait(pe, s_g, c + 1)
                        wait(pe, s_gT, KM * c)
                        turn(t2_ps, lambda t, k: gs[:, b, t, k * P:(k + 1) * P]).then_inc(s_t2, 1)
                        wait(pe, s_gT, KM * (c + 1))
                        wait(pe, s_lc, c)
                        for t in range(TT):
                            for k in range(KM):
                                last = nc.tensor.matmul(g_ps[:, t * NE:(t + 1) * NE], gT[:, k, t * P:(t + 1) * P],
                                                        gate[:, k, :], start=(k == 0), stop=(k == KM - 1))
                        last.then_inc(s_lg, 1)

                    every_chunk(pe, front, back)

                @block.vector
                def _(dve):
                    dve.wait_ge(s_w, 48)
                    dve.wait_ge(s_set, 8)

                    def front(i, b):
                        c = 2 * i + b
                        wait(dve, s_f[b], 32 * (i + 1))
                        wait(dve, s_wo, c + 1)
                        for half in range(2):
                            part = flat(hc[:, b, 2 * half:2 * half + 2, :])
                            nc.vector.tensor_tensor(part, flat(h_ps[:, 2 * half:2 * half + 2, :]), part, ALU.add
                                                    ).then_inc(s_h, 1)
                        wait(dve, s_h, 2 * (c + 1))
                        for t in range(TT):
                            last = nc.vector.bn_stats(stats[:, t, :], hc[:, b, t, :])
                        last.then_inc(s_st, 1)
                        wait_apart(dve, s_st, 4 * c + 1, s_w)
                        for t in range(TT):
                            last = nc.vector.bn_aggr(mv[:, t, :], stats[:, t, :])
                        last.then_inc(s_st, 1)
                        wait(dve, s_st, 4 * c + 2)
                        nc.vector.tensor_tensor(mv[:, :, 0], mv[:, :, 0], mv[:, :, 0], ALU.mult).then_inc(s_st, 1)
                        wait(dve, s_st, 4 * c + 3)
                        nc.vector.tensor_tensor(mv[:, :, 1], mv[:, :, 1], mv[:, :, 0], ALU.add).then_inc(s_st, 1)
                        wait(dve, s_sd, c + 1)
                        nc.vector.reciprocal(rs[:, :], sd[:, :]).then_inc(s_rs, 1)
                        wait(dve, s_rs, c + 1)
                        wait(dve, s_t2, c - 1)
                        for t in range(TT):
                            nc.vector.tensor_scalar(gs[:, b, t, :], hc[:, b, t, :], rs[:, t:t + 1], None, ALU.mult)
                            last = nc.vector.tensor_scalar(
                                g[:, bass.ds(i * TT + (b * BT + t), 1), :].rearrange("p o e -> p (o e)"),
                                hc[:, b, t, :], rs[:, t:t + 1], None, ALU.mult)
                        last.then_inc(s_g, 1)

                    def back(i, b):
                        c = 2 * i + b
                        wait_apart(dve, s_lg, c + 1, s_w)
                        nc.vector.tensor_copy(lgc[:, b].rearrange("p t e -> p (t e)"), g_ps[:, 0:TT * NE]
                                              ).then_inc(s_lc, 1)
                        wait_apart(dve, s_lc, c + 1, s_w)
                        for t in range(TT):
                            last = nc.vector.max(topc[:, b, t, :], lgc[:, b, t, :])
                        last.then_inc(s_top, 1)
                        wait_apart(dve, s_top, c + 1, s_w)
                        for t in range(TT):
                            last = nc.vector.max_index(idxc[:, b, t, :], topc[:, b, t, :], lgc[:, b, t, :])
                        last.then_inc(s_ix, 1)
                        wait_apart(dve, s_ix, c + 1, s_w)
                        at = bass.ds(i * TT + b * BT, TT)
                        nc.vector.tensor_copy(idf[:, 0, at], idxc[:, b, :, 0])
                        nc.vector.tensor_copy(idf[:, 1, at], idxc[:, b, :, 1])
                        nc.vector.tensor_tensor(dif[:, at], topc[:, b, :, 1], topc[:, b, :, 0], ALU.subtract
                                                ).then_inc(s_dif, 1)

                    every_chunk(dve, front, back)

            ex = sb2("ex", [P, NT])
            den = sb2("den", [P, NT])
            hot = sb2("hot", [P, 2, NT, NE])
            both = sb2("both", [P, NT, NE])
            tot = sb2("tot", [P, NT, NE])
            run = sb2("run", [P, NT, NE])
            cmp_ = sb2("cmp", [P, NE, NT])
            nt = sb2("nt", [P, NE])
            upto = sb2("upto", [P, NE])
            base = sb2("base", [P, NE])
            place = sb2("place", [P, NT, NE])
            pick = sb2("pick", [P, 2, NT, NE])
            posf = sb2("posf", [P, 2, NT])
            le = sb2("le", [1, SLOT_TILES, NE])
            exf = sb2("exf", [1, SLOT_TILES])
            r_ps = ps2("r_ps", [P, 2, NT, NE])
            block = ctx2.enter_context(nc.Block())

            @block.scalar
            def _(act):
                nc.scalar.activation(ex[:, :], dif[:, :], ACT.Exp).then_inc(s_ex, 1)

            @block.tensor
            def _(pe):
                pe.wait_ge(s_r, 4)
                pe.wait_ge(s_set, 7)
                nc.tensor.matmul(r_ps[:, 0].rearrange("p t e -> p (t e)"), before[:, :],
                                 both[:, :, :].rearrange("p t e -> p (t e)"), start=True, stop=True)
                nc.tensor.matmul(r_ps[:, 1].rearrange("p t e -> p (t e)"), ones[:, :],
                                 both[:, :, :].rearrange("p t e -> p (t e)"), start=True, stop=True
                                 ).then_inc(s_cnt, 1)

            @block.vector
            def _(dve):
                step = [0]

                def then(ins):
                    step[0] += 1
                    ins.then_inc(s_r, 1)
                    dve.wait_ge(s_r, step[0])

                def te(ap):
                    return ap.rearrange("p t e -> p (t e)")

                then(nc.vector.memset(one[:, :], 1.0))
                for k in range(2):
                    then(nc.vector.tensor_tensor(hot[:, k], iota[:, None, :].to_broadcast([P, NT, NE]),
                                                 idf[:, k, :, None].to_broadcast([P, NT, NE]), ALU.is_equal))
                then(nc.vector.tensor_tensor(te(both[:, :, :]), te(hot[:, 0]), te(hot[:, 1]), ALU.add))
                dve.wait_ge(s_ex, 1)
                then(nc.vector.tensor_scalar(den[:, :], ex[:, :], 1.0, None, ALU.add))
                then(nc.vector.reciprocal(sh[:, 0, :], den[:, :]))
                then(nc.vector.tensor_tensor(sh[:, 1, :], sh[:, 0, :], ex[:, :], ALU.mult))
                dve.wait_ge(s_cnt, 1)
                then(nc.vector.tensor_copy(te(tot[:, :, :]), te(r_ps[:, 1])))
                for e in range(NE):
                    last = nc.vector.tensor_tensor_scan(run[:, :, e], one[:, 0:NT], tot[:, :, e], 0.0,
                                                        ALU.mult, ALU.add)
                then(last)
                then(nc.vector.tensor_tensor(cmp_[:, :, :], run[:, NT - 1, :, None].to_broadcast([P, NE, NT]),
                                             starts[:, None, :].to_broadcast([P, NE, NT]), ALU.is_gt))
                then(nc.vector.tensor_reduce(nt[:, :], cmp_[:, :, :], AX.X, ALU.add))
                then(nc.vector.tensor_tensor_scan(upto[:, :], one[:, 0:NE], nt[:, :], 0.0, ALU.mult, ALU.add))
                then(nc.vector.tensor_tensor(base[:, :], upto[:, :], nt[:, :], ALU.subtract))
                then(nc.vector.tensor_scalar(base[:, :], base[:, :], float(P), None, ALU.mult))
                then(nc.vector.tensor_tensor(te(run[:, :, :]), te(run[:, :, :]), te(tot[:, :, :]), ALU.subtract))
                then(nc.vector.tensor_tensor(te(place[:, :, :]), te(run[:, :, :]), te(r_ps[:, 0]), ALU.add))
                then(nc.vector.tensor_tensor(place[:, :, :], place[:, :, :],
                                             base[:, None, :].to_broadcast([P, NT, NE]), ALU.add))
                for k in range(2):
                    then(nc.vector.tensor_tensor(te(pick[:, k]), te(hot[:, k]), te(place[:, :, :]), ALU.mult))
                    then(nc.vector.tensor_reduce(posf[:, k, :], pick[:, k], AX.X, ALU.add))
                    then(nc.vector.tensor_copy(pos[:, k, :], posf[:, k, :]))
                then(nc.vector.tensor_tensor(le[:, :, :], upto[0:1, None, :].to_broadcast([1, SLOT_TILES, NE]),
                                             tiles[:, :, None].to_broadcast([1, SLOT_TILES, NE]), ALU.is_le))
                then(nc.vector.tensor_reduce(exf[:, :], le[:, :, :], AX.X, ALU.add))
                then(nc.vector.tensor_scalar(exf[:, :], exf[:, :], float(NE - 1), None, ALU.min))
                then(nc.vector.tensor_copy(expert[:, :], exf[:, :]))

        with ExitStack() as ctx2:
            def sb3(name, shape, dt=F32):
                return ctx2.enter_context(nc.sbuf_tensor(name, shape, dt))

            def ps3(name, shape, dt=F32):
                return ctx2.enter_context(nc.psum_tensor(name, shape, dt))

            xt = sb3("xt", [P, 4, DM])
            xT = sb3("m_xT", [P, 2, KM, P])
            sl = sb3("sl", [P, 2, FI])
            mid = sb3("mid", [P, 2, FI])
            midT = sb3("midT", [P, 2, KF, P])
            yt = sb3("yt", [P, 4, DM])
            a_ps = ps3("a_ps", [P, 2, FI])
            c_ps = ps3("c3_ps", [P, 2, FI])
            x_ps = ps3("x_ps", [P, FI])
            m_ps = ps3("m_ps", [P, KF, P])
            o_ps = ps3("o_ps", [P, 2, FI])

            s_sc = sem("m_sc")
            s_xt = [sem(f"m_xt{r}") for r in range(4)]
            s_xp = sem("m_xp")
            s_xT = sem("m_xTs")
            s_up = sem("m_up")
            s_sl = sem("m_sl")
            s_mid = sem("m_mid")
            s_mp = sem("m_mp")
            s_mT = sem("m_mT")
            s_dn = sem("m_dn")
            s_yt = sem("m_yt")
            s_y = [sem(f"m_y{r}") for r in range(4)]

            NJ = SLOT_TILES
            block = ctx2.enter_context(nc.Block())

            def every_tile(eng, step):
                for j in range(8):
                    step(j, j % 4, j // 4)
                with eng.Fori(2, NJ // 4 - 1) as n:
                    for q in range(4):
                        step(4 * n + q, q, n)
                for j in range(NJ - 4, NJ + 2):
                    step(j, j % 4, j // 4)

            def there(j, back):
                return not isinstance(j, int) or 0 <= j - back < NJ

            def at(q, n, back):
                return (q - back) % 4, n + (q - back) // 4

            @block.gpsimd
            def _(pool):
                pool.wait_ge(s_clear, 16 * (SLOT_TILES // ZC))
                for k in range(2):
                    for t in range(NT):
                        nc.gpsimd.indirect_dma_start(
                            out=xg_dram[:, :], out_offset=bass.IndirectOffsetOnAxis(ap=pos[:, k, t:t + 1], axis=0),
                            in_=g[:, t, :], in_offset=None).then_inc(s_sc, 16)

            @block.sync
            def _(sp):
                sp.wait_ge(s_sc, 16 * 2 * NT)

                def load(j, slot, i):
                    wait_apart(sp, s_xp, j - 3, s_sc)
                    sp.dma_start(xt[:, slot, :], xg_dram[bass.ds(j * P, P), :]).then_inc(s_xt[slot], 16)

                def store(j, slot):
                    wait_apart(sp, s_yt, j + 1, s_sc)
                    sp.dma_start(y_dram[bass.ds(j * P, P), :], yt[:, slot, :]).then_inc(s_y[slot], 16)

                for j in range(8):
                    load(j, j % 4, j // 4)
                    if j >= 4:
                        store(j - 4, j % 4)
                with sp.Fori(2, NJ // 4) as n:
                    for q in range(4):
                        load(4 * n + q, q, n)
                        store(4 * n + q - 4, q)
                for j in range(NJ - 4, NJ):
                    store(j, j % 4)
                for slot in range(4):
                    sp.wait_ge(s_y[slot], 16 * (NJ // 4))

            @block.scalar
            def _(act):
                def rows(j, q, n):
                    wait(act, s_xp, j + 1)
                    wait(act, s_up, j - 1)
                    for k in range(KM):
                        nc.scalar.activation(xT[:, q % 2, k, :], x_ps[:, k * P:(k + 1) * P], ACT.Identity,
                                             scale=ln2[:, k:k + 1]).then_inc(s_xT, 1)

                def step(j, q, n):
                    if isinstance(j, int) and j == 0:
                        rows(0, 0, 0)
                    if there(j, -1):
                        rows(j + 1, (q + 1) % 4, 0)
                    if there(j, 1):
                        wait(act, s_mp, j)
                        wait(act, s_dn, j - 2)
                        nc.scalar.copy(midT[:, (q - 1) % 2], m_ps[:, :, :]).then_inc(s_mT, 1)
                    if there(j, 0):
                        wait(act, s_up, j + 1)
                        wait(act, s_mid, j - 1)
                        nc.scalar.activation(sl[:, q % 2, :], a_ps[:, q % 2, :], ACT.Silu).then_inc(s_sl, 1)

                every_tile(act, step)

            @block.vector
            def _(dve):
                def step(j, q, n):
                    if there(j, 2):
                        slot, taken = at(q, n, 2)
                        wait(dve, s_dn, j - 1)
                        wait(dve, s_y[slot], 16 * taken)
                        nc.vector.tensor_copy(yt[:, slot, :], o_ps[:, q % 2, 0:DM]).then_inc(s_yt, 1)
                    if there(j, 0):
                        wait(dve, s_sl, j + 1)
                        wait(dve, s_mp, j - 1)
                        nc.vector.tensor_tensor(mid[:, q % 2, :], sl[:, q % 2, :], c_ps[:, q % 2, :], ALU.mult
                                                ).then_inc(s_mid, 1)

                every_tile(dve, step)

            @block.tensor
            def _(pe):
                pe.wait_ge(s_we, 16 * 3 * NE)

                def turn_rows(j, slot, taken):
                    wait(pe, s_xt[slot], 16 * (taken + 1))
                    wait(pe, s_xT, KM * j)
                    for k in range(KM):
                        last = nc.tensor.transpose(x_ps[:, k * P:(k + 1) * P], xt[:, slot, k * P:(k + 1) * P],
                                                   ident[:, :])
                    last.then_inc(s_xp, 1)

                def of_expert(w, e, k):
                    return w[:, bass.ds(e, 1), k, :].rearrange("p o n -> p (o n)")

                def load_expert(j):
                    return pe.value_load(expert[0:1, bass.ds(j, 1)], min_val=0, max_val=NE - 1)

                def step(j, q, n):
                    if isinstance(j, int) and j == 0:
                        turn_rows(0, 0, 0)
                    if there(j, -1):
                        turn_rows(j + 1, *at(q, n, -1))
                    if there(j, 2):
                        e = load_expert(j - 2)
                        wait(pe, s_mT, j - 1)
                        wait(pe, s_yt, j - 3)
                        for m in range(KF):
                            last = nc.tensor.matmul(o_ps[:, q % 2, 0:DM], midT[:, q % 2, m, :],
                                                    of_expert(w2, e, m), start=(m == 0), stop=(m == KF - 1))
                        last.then_inc(s_dn, 1)
                    if there(j, 1):
                        wait(pe, s_mid, j)
                        wait(pe, s_mT, j - 1)
                        for m in range(KF):
                            last = nc.tensor.transpose(m_ps[:, m, :], mid[:, (q - 1) % 2, m * P:(m + 1) * P],
                                                       ident[:, :])
                        last.then_inc(s_mp, 1)
                    if there(j, 0):
                        e = load_expert(j)
                        wait(pe, s_xT, KM * (j + 1))
                        wait(pe, s_mid, j - 1)
                        for w, dst in ((w1, a_ps), (w3, c_ps)):
                            for k in range(KM):
                                last = nc.tensor.matmul(dst[:, q % 2, :], xT[:, q % 2, k, :],
                                                        of_expert(w, e, k), start=(k == 0), stop=(k == KM - 1))
                        last.then_inc(s_up, 1)

                every_tile(pe, step)

        with ExitStack() as ctx2:
            RG = 4
            ya = ctx2.enter_context(nc.sbuf_tensor("ya", [P, RG, 2, DM], F32))
            res = ctx2.enter_context(nc.sbuf_tensor("res", [P, RG, DM], F32))
            s_ya = [sem(f"m_ya{r}") for r in range(RG)]
            s_res = [sem("m_res0"), sem("m_res1")]
            s_out = [sem(f"m_out{r}") for r in range(RG)]
            block = ctx2.enter_context(nc.Block())

            @block.gpsimd
            def _(pool):
                for t in range(NT):
                    wait(pool, s_res[1], t - RG + 1)
                    for k in range(2):
                        nc.gpsimd.indirect_dma_start(
                            out=ya[:, t % RG, k, :], out_offset=None, in_=y_dram[:, :],
                            in_offset=bass.IndirectOffsetOnAxis(ap=pos[:, k, t:t + 1], axis=0)
                        ).then_inc(s_ya[t % RG], 16)

            @block.vector
            def _(dve):
                def rows(ap):
                    return ap.rearrange("p (n w) -> p n w", n=HP)

                def add(t, k):
                    b, tb = t // BT, t % BT
                    r = t % RG
                    if k == 0:
                        dve.wait_ge(s_ya[r], 32 * (t // RG + 1))
                        wait(dve, s_out[r], 16 * (t // RG))
                        src = att[:, b * HP:(b + 1) * HP, tb, :]
                    else:
                        dve.wait_ge(s_res[0], t + 1)
                        src = rows(res[:, r, :])
                    nc.vector.scalar_tensor_tensor(
                        out=rows(res[:, r, :]), in0=rows(ya[:, r, k, :]), scalar=sh[:, k, t:t + 1],
                        in1=src, op0=ALU.mult, op1=ALU.add).then_inc(s_res[k], 1)

                for t in range(NT):
                    add(t, 0)
                    add(t, 1)

            @block.sync
            def _(sp):
                for t in range(NT):
                    b, tb = t // BT, t % BT
                    sp.wait_ge(s_res[1], t + 1)
                    sp.dma_start(out[b, tb * P:(tb + 1) * P, :], res[:, t % RG, :]).then_inc(s_out[t % RG], 16)
                for r in range(RG):
                    sp.wait_ge(s_out[r], 16 * (NT // RG))


def slot_tiles(tokens, experts):
    most = (2 * tokens + experts * (P - 1)) // P
    return -(-most // 4) * 4


def build(nc, a, out):
    B, L, _ = a["x"].shape
    x1 = nc.dram_tensor("x1_scratch", [B, L, DM], F32, kind="Internal").ap()
    f = nc.dram_tensor("f_scratch", [B, L, DM], F32, kind="Internal").ap()
    b_rows = nc.dram_tensor("b_rows", [2, NS, CH], F32, kind="Internal").ap()
    slots = P * slot_tiles(B * L, a["gateT"].shape[1])
    xg = nc.dram_tensor("slots_in", [slots, DM], F32, kind="Internal").ap()
    y = nc.dram_tensor("slots_out", [slots, DM], F32, kind="Internal").ap()
    parts = nc.dram_tensor("parts", [2, 3, B * DM, L], BF16, kind="Internal").ap()

    ssm_stage(nc, a["x"], a["W_inT"], a["conv_w"], a["conv_b"], a["W_xT"], a["dt_w"], a["dt_b"],
              a["A_log"], a["D_param"], a["W_outT"], x1, b_rows)
    with nc.sbuf_tensor("att", [P, B * HP, L // P, 2 * HD], F32) as att:
        with nc.sbuf_tensor("v_all", [P, B * HP, L // P, VW], F32) as v_all:
            qkv_stage(nc, x1, a["ln1_w"], a["wqT"], a["wkT"], a["wvT"], f, parts, v_all)
            attention_stage(nc, parts, v_all, att, B, L)
        moe_stage(nc, x1, f, att, a["woT"], a["ln2_w"], a["gateT"], a["w1T"], a["w2T"], a["w3T"], xg, y, out)


def kernel(**inputs):
    import numpy as np
    import concourse.bacc as bacc
    from concourse.bass_utils import run_bass_kernel_spmd

    a = {k.replace("L0_attn_", "").replace("L0_ffn_", ""): np.asarray(v) for k, v in inputs.items()}
    W_x = a["W_x"]
    laid = dict(
        x=a["x"], W_inT=a["W_in"].T, conv_w=a["conv_w"], conv_b=a["conv_b"],
        W_xT=np.concatenate([W_x[1:], W_x[:1]], axis=0).T, dt_w=a["dt_w"][:, 0], dt_b=a["dt_b"],
        A_log=a["A_log"], D_param=a["D_param"], W_outT=a["W_out"].T,
        ln1_w=a["ln1_w"], ln2_w=a["ln2_w"], wqT=a["wq"].T, wkT=a["wk"].T, wvT=a["wv"].T, woT=a["wo"].T,
        gateT=a["gate_w"].T, w1T=a["w1"].transpose(0, 2, 1), w2T=a["w2"].transpose(0, 2, 1),
        w3T=a["w3"].transpose(0, 2, 1))
    nc = bacc.Bacc("TRN2", target_bir_lowering=False, num_devices=1)
    arrays, aps = {}, {}
    for name, v in laid.items():
        v = np.ascontiguousarray(v)
        arrays[f"in_{name}"] = v
        aps[name] = nc.dram_tensor(f"in_{name}", v.shape, mybir.dt.from_np(v.dtype), kind="ExternalInput").ap()
    out = nc.dram_tensor("out_x", a["x"].shape, F32, kind="ExternalOutput").ap()
    build(nc, aps, out)
    r = run_bass_kernel_spmd(nc, [arrays], core_ids=[0])
    return r.results[0]["out_x"]
```

```python
from contextlib import ExitStack

import concourse.bass as bass
from concourse import mybir

ALU = mybir.AluOpType
ACT = mybir.ActivationFunctionType
AX = mybir.AxisListType
F32 = mybir.dt.float32
BF16 = mybir.dt.bfloat16
U32 = mybir.dt.uint32

P = 128
CH = 512
TT = CH // P
DM = 256
KM = DM // P
DI = 512
KI = DI // P
NS = 16
TAPS = 4
EPS = 1e-5


def wait(eng, sem, value):
    if isinstance(value, int) and value <= 0:
        return
    eng.wait_ge(sem, value)


def wait_apart(eng, sem, value, met):
    if isinstance(value, int):
        wait(eng, sem, value)
    else:
        eng.compute_val(value)
        eng.wait_ge(met, 1)
        eng.wait_ge(sem, value)


def flat(ap):
    return ap.rearrange("p a b -> p (a b)")


def ssm_stage(nc, x, W_inT, conv_w, conv_b, W_xT, dt_w, dt_b, A_log, D_param, W_outT, x1_dram, b_dram):
    B, L, _ = x.shape
    NI = L // CH
    assert B == 2 and L % CH == 0 and NI >= 2
    HR = 4
    BR = 4
    RB = 4
    NR = NS + 1

    with ExitStack() as ctx:
        def sb(name, shape, dt=F32):
            return ctx.enter_context(nc.sbuf_tensor(name, shape, dt))

        def ps(name, shape, dt=F32):
            return ctx.enter_context(nc.psum_tensor(name, shape, dt))

        def sem(name):
            return ctx.enter_context(nc.semaphore(name))

        w_in = sb("w_in", [P, KM, 2 * DI])
        w_x = sb("w_x", [P, KI, 2 * NS + 1])
        w_out = sb("w_out", [P, KI, DM])
        cw = sb("cw", [P, KI, TAPS])
        cb = sb("cb", [P, KI])
        dtw = sb("dtw", [P, KI])
        dtb = sb("dtb", [P, KI])
        dpar = sb("dpar", [P, KI])
        alog = sb("alog", [P, KI, NS])
        aneg = sb("aneg", [P, KI, NS])
        ident = sb("ident", [P, P])
        diag = sb("diag", [P, KI, P])
        sel_f = sb("sel_f", [96, NR])
        sel = sb("sel", [96, NR], BF16)
        epsc = sb("epsc", [P, 1])
        xn = sb("xn", [P, TT, DM])
        stats = sb("stats", [P, TT, 6])
        mv = sb("mv", [P, TT, 2])
        sd = sb("sd", [P, TT])
        rs = sb("rs", [P, TT])
        xT = sb("xT", [P, KM, CH])
        HALO = TAPS - 1
        xs = sb("xs", [P, KI, HALO + CH])
        halo = sb("halo", [P, 2, KI, HALO])
        tA = xs[:, :, 0:CH]
        tB = sb("tB", [P, KI, CH])
        xc = sb("xc", [P, KI, CH])
        pr = sb("pr", [2 * NS + 1, CH])
        r1 = sb("r1", [NR, CH])
        p1 = sb("p1", [NR, CH], BF16)
        zs = sb("zs", [P, 2, KI, CH])
        dt = sb("dt", [P, 2, KI, CH])
        u = sb("u", [P, 2, KI, CH])
        parts = sb("c_parts", [96, 2, CH], BF16)
        state = sb("state", [P, 2, NS, KI])
        dA = sb("dA", [P, 2, KI, CH])
        h = sb("h", [P, HR, KI, CH])
        bx = sb("bx", [P, BR, KI, CH])
        bb = sb("bb", [P, RB, CH])
        xres = sb("xres", [P, TT, DM])

        y_ps = ps("y_ps", [P, KI, CH])
        c_ps = ps("c_ps", [P, 2, CH])
        fill = ps("fill", [P, 2, CH])

        s_w = sem("s_w")
        s_id = sem("s_id")
        s_set = sem("s_set")
        s_aexp = sem("s_aexp")
        s_an = sem("s_an")
        s_x = sem("s_x")
        s_xr = sem("s_xr")
        s_st1 = sem("s_st1")
        s_mv = sem("s_mv")
        s_sd = sem("s_sd")
        s_rs = sem("s_rs")
        s_xn = sem("s_xn")
        s_xT = sem("s_xT")
        s_full = [sem("s_full0"), sem("s_full1")]
        s_free = [sem("s_free0"), sem("s_free1")]
        s_halo = sem("s_halo")
        s_hsave = sem("s_hsave")
        s_tap = sem("s_tap")
        s_cv = sem("s_cv")
        s_xc = sem("s_xc")
        s_zs = sem("s_zs")
        s_prst = sem("s_prst")
        s_b = [sem(f"s_b{k}") for k in range(RB)]
        s_abs = sem("s_abs")
        s_e = sem("s_e")
        s_ln = sem("s_ln")
        s_q = sem("s_q")
        s_sp = sem("s_sp")
        s_dt = sem("s_dt")
        s_u = sem("s_u")
        s_da = sem("s_da")
        s_bx = sem("s_bx")
        s_h = sem("s_h")
        s_sv = sem("s_sv")
        s_dx = sem("s_dx")
        s_sel = sem("s_sel")
        s_r1 = sem("s_r1")
        s_p0 = sem("s_p0")
        s_p1 = sem("s_p1")
        s_p2 = sem("s_p2")
        s_cb = sem("s_cb")
        s_hc = sem("s_hc")
        s_ys = sem("s_ys")
        s_g = sem("s_g")
        s_x1st = sem("s_x1st")

        NW = 10
        FA = 6

        def known_below(c, value):
            return isinstance(c, int) and c < value

        def prep_fill(c):
            return FA * c if known_below(c, 2) else (FA + 1) * c - 2

        CONV = 1

        def late_fill(c, k):
            return prep_fill(c) + (3 if known_below(c, 2) else 4) + k

        def out_fill(c, last_but_one=False, last=False):
            if last:
                return prep_fill(c + 1) + 1
            return prep_fill(c + 2) + (0 if last_but_one else 3)

        def tokens(c, i, b):
            return b, bass.ds(i * CH, CH)

        def nxt(i, b):
            return (i, 1) if b == 0 else (i + 1, 0)

        def prv(i, b):
            return (i, 0) if b == 1 else (i - 1, 1)

        def has_two(i):
            return not (isinstance(i, int) and i == NI - 1)

        def every_chunk(eng, prologue, chunk):
            prologue()
            for b in range(2):
                chunk(0, b, b > 0, True)
            if NI > 2:
                with eng.Fori(1, NI - 1) as i:
                    for b in range(2):
                        chunk(i, b, True, True)
            for b in range(2):
                chunk(NI - 1, b, True, b == 0)

        block = ctx.enter_context(nc.Block())

        @block.sync
        def _(sp):
            sp.dma_start(w_in[:, :, :], W_inT.rearrange("(k p) e -> p k e", p=P)).then_inc(s_w, 16)
            sp.dma_start(w_x[:, :, :], W_xT.rearrange("(k p) e -> p k e", p=P)).then_inc(s_w, 16)
            sp.dma_start(w_out[:, :, :], W_outT.rearrange("(k p) e -> p k e", p=P)).then_inc(s_w, 16)
            sp.dma_start(cw[:, :, :], conv_w.rearrange("(k p) e -> p k e", p=P)).then_inc(s_w, 16)
            sp.dma_start(alog[:, :, :], A_log.rearrange("(k p) e -> p k e", p=P)).then_inc(s_w, 16)
            with nc.allow_non_contiguous_dma(reason="five small vectors, once"):
                for dst, src in ((cb, conv_b), (dtw, dt_w), (dtb, dt_b), (dpar, D_param)):
                    sp.dma_start(dst[:, :], src.rearrange("(k p) -> p k", p=P)).then_inc(s_w, 16)

            def load_x(i, b):
                c = 2 * i + b
                bt, ts = tokens(c, i, b)
                wait_apart(sp, s_full[1], prep_fill(c - 1) + 1 if not (isinstance(c, int) and c == 0) else 0, s_w)
                sp.dma_start(xn[:, :, :], x[bt, ts, :].rearrange("(t p) e -> p t e", p=P)).then_inc(s_x, 16)

            def load_b(i, b, n):
                c = 2 * i + b
                wait_apart(sp, s_prst, 16 * (c + 1), s_w)
                wait_apart(sp, s_bx, NS * c + n - RB + 1, s_w)
                sp.dma_start(bb[:, n % RB, :], b_dram[b, n:n + 1, :].partition_broadcast(P)
                             ).then_inc(s_b[n % RB], 16)

            def store_rows(i, b):
                c = 2 * i + b
                wait_apart(sp, s_free[0], late_fill(c, 0) + 1, s_w)
                sp.dma_start(b_dram[b, :, :], pr[NR:NR + NS, :]).then_inc(s_prst, 16)

            def wait_x1(c, *place):
                for bank in range(2):
                    wait_apart(sp, s_free[bank], out_fill(c, *place) + 1, s_w)

            def store_x1(i, b, *place):
                c = 2 * i + b
                bt, ts = tokens(c, i, b)
                wait_x1(c, *place)
                sp.dma_start(x1_dram[bt, ts, :].rearrange("(t p) e -> p t e", p=P), xres[:, :, :]
                             ).then_inc(s_x1st, 16)

            def load_res(i, b):
                c = 2 * i + b
                bt, ts = tokens(c, i, b)
                wait_apart(sp, s_x1st, 16 * c, s_w)
                sp.dma_start(xres[:, :, :], x[bt, ts, :].rearrange("(t p) e -> p t e", p=P)).then_inc(s_xr, 16)

            def prologue():
                load_x(0, 0)
                store_rows(0, 0)
                load_b(0, 0, 0)
                load_b(0, 0, 1)
                load_b(0, 0, 2)
                load_x(0, 1)

            def chunk(i, b, has_prev, has_next):
                for n in range(NS):
                    if n + 3 < NS:
                        load_b(i, b, n + 3)
                    if n == 12 and has_prev:
                        store_x1(*prv(i, b), not has_next)
                    if n == 3 and has_two(i):
                        load_x(*nxt(*nxt(i, b)))
                    if n == 14:
                        load_res(i, b)
                    if n == 13 and has_next:
                        store_rows(*nxt(i, b))
                    if n == 15 and has_next:
                        load_b(*nxt(i, b), 0)
                        load_b(*nxt(i, b), 1)
                        load_b(*nxt(i, b), 2)

            every_chunk(sp, prologue, chunk)
            store_x1(NI - 1, 1, False, True)
            sp.wait_ge(s_x1st, 16 * 2 * NI)

        @block.gpsimd
        def _(pool):
            nc.gpsimd.memset(ident[:, :], 0.0).then_inc(s_id, 1)
            nc.gpsimd.memset(epsc[:, :], EPS).then_inc(s_set, 1)
            nc.gpsimd.memset(halo[:, :, :, :], 0.0).then_inc(s_set, 1)
            nc.gpsimd.memset(state[:, :, :, :], 0.0).then_inc(s_set, 1)
            nc.gpsimd.memset(parts[:, :, :], 0.0).then_inc(s_set, 1)
            pool.wait_ge(s_id, 1)
            nc.gpsimd.affine_select(out=ident[:, :], in_=ident[:, :], compare_op=ALU.not_equal, fill=1.0,
                                    base=0, pattern=[[-1, P]], channel_multiplier=1).then_inc(s_id, 1)
            pool.wait_ge(s_aexp, 1)
            nc.gpsimd.tensor_scalar(aneg[:, :, :], aneg[:, :, :], -1.0, None, ALU.mult).then_inc(s_an, 1)

            def step_sizes(c, b, k):
                if k == 0:
                    wait(pool, s_ln, 2 * (c + 1))
                    wait(pool, s_q, c + 1)
                    nc.gpsimd.tensor_tensor(u[:, b], u[:, b], tB[:, :, :], ALU.subtract).then_inc(s_sp, 1)
                if k == 1:
                    wait(pool, s_sp, c + 1)
                    nc.gpsimd.tensor_tensor(dt[:, b], dt[:, b], u[:, b], ALU.add).then_inc(s_dt, 1)
                if k == 2:
                    wait(pool, s_dt, c + 1)
                    nc.gpsimd.tensor_tensor(u[:, b], dt[:, b], xc[:, :, :], ALU.mult).then_inc(s_u, 1)

            def prologue():
                for k in range(3):
                    step_sizes(0, 0, k)

            def chunk(i, b, has_prev, has_next):
                c = 2 * i + b
                wait(pool, s_u, c + 1)
                for n in range(NS):
                    wait(pool, s_b[n % RB], 16 * ((NS // RB) * c + n // RB + 1))
                    wait(pool, s_h, NS * c + n - BR + 1)
                    nc.gpsimd.tensor_tensor(
                        bx[:, n % BR], u[:, b],
                        bb[:, n % RB, None, :].to_broadcast([P, KI, CH]), ALU.mult).then_inc(s_bx, 1)
                if has_next:
                    for k in range(3):
                        step_sizes(c + 1, 1 - b, k)

            every_chunk(pool, prologue, chunk)

        @block.scalar
        def _(act):
            act.wait_ge(s_w, 16 * (NW - 1))
            act.wait_ge(s_set, 4)
            nc.scalar.activation(aneg[:, :, :], alog[:, :, :], ACT.Exp).then_inc(s_aexp, 1)

            def root(c):
                wait(act, s_mv, c + 1)
                nc.scalar.activation(sd[:, :], mv[:, :, 1], ACT.Sqrt, bias=epsc[:, 0:1]).then_inc(s_sd, 1)

            def take_xT(c):
                f = prep_fill(c)
                for k in range(KM):
                    wait(act, s_full[k], f + 1)
                    nc.scalar.copy(xT[:, k, :], fill[:, k, :]).then_inc(s_free[k], 1)

            def place_halo(c, b):
                wait(act, s_dt, c)
                wait(act, s_hsave, c - 1)
                nc.scalar.copy(xs[:, :, 0:HALO], halo[:, b]).then_inc(s_halo, 1)

            def take_conv_in(c, b, d):
                bank, f = d % 2, prep_fill(c) + CONV + d // 2
                wait(act, s_full[bank], f + 1)
                nc.scalar.copy(xs[:, d, HALO:], fill[:, bank, :]).then_inc(s_tap, 1)
                if d == 0:
                    wait(act, s_u, c)
                    wait(act, s_dx, c)
                nc.scalar.activation(xc[:, d, :], fill[:, bank, :], ACT.Identity,
                                     bias=cb[:, d:d + 1], scale=cw[:, d, HALO:HALO + 1]
                                     ).then_inc(s_free[bank], 1)

            def take_z(c, b, d):
                bank, f = d % 2, late_fill(c, 1 + d // 2)
                wait(act, s_full[bank], f + 1)
                nc.scalar.copy(zs[:, b, d, :], fill[:, bank, :]).then_inc(s_free[bank], 1)

            def silu_xc(c, b):
                wait(act, s_cv, KI * HALO * (c + 1))
                nc.scalar.copy(halo[:, b], xs[:, :, CH:CH + HALO]).then_inc(s_hsave, 1)
                nc.scalar.activation(flat(xc[:, :, :]), flat(xc[:, :, :]), ACT.Silu).then_inc(s_xc, 1)

            def silu_z(c, b):
                for k in range(2):
                    wait(act, s_free[k], late_fill(c, 2) + 1)
                nc.scalar.activation(flat(zs[:, b]), flat(zs[:, b]), ACT.Silu).then_inc(s_zs, 1)

            def take_rows(c, b):
                wait(act, s_full[0], late_fill(c, 0) + 1)
                wait(act, s_prst, 16 * c)
                nc.scalar.copy(parts[0:NR, b, :], fill[0:NR, 0, :]).then_inc(s_p0, 1)
                nc.scalar.copy(pr[:, :], fill[0:NR + NS, 0, :]).then_inc(s_free[0], 1)

            def second_part(c, b):
                wait(act, s_r1, c + 1)
                nc.scalar.copy(p1[:, :], r1[:, :]).then_inc(s_p1, 1)
                nc.scalar.copy(parts[32:32 + NR, b, :], r1[:, :]).then_inc(s_p1, 1)

            def softplus_in(c, b, half):
                wait(act, s_full[1], late_fill(c, 0) + 1)
                wait(act, s_hsave, c + 1)
                for d in (2 * half, 2 * half + 1):
                    nc.scalar.activation(tA[:, d, :], fill[:, 1, :], ACT.Abs,
                                         bias=dtb[:, d:d + 1], scale=dtw[:, d:d + 1]).then_inc(s_abs, 1)
                    last = nc.scalar.activation(dt[:, b, d, :], fill[:, 1, :], ACT.Relu,
                                                bias=dtb[:, d:d + 1], scale=dtw[:, d:d + 1])
                if half:
                    last.then_inc(s_free[1], 1)

            def softplus_exp(c):
                wait(act, s_abs, KI * (c + 1))
                nc.scalar.activation(tA, tA, ACT.Exp, scale=-1.0).then_inc(s_e, 1)
                wait(act, s_e, c + 1)
                nc.scalar.activation(tB[:, :, :], tA, ACT.Identity, bias=1.0).then_inc(s_ln, 1)

            def softplus_ln(c, b):
                nc.scalar.activation(u[:, b], tA, ACT.Ln, bias=1.0).then_inc(s_ln, 1)

            def prep(c, b, n):
                if n == 1:
                    place_halo(c, b)
                if n in (3, 4):
                    take_conv_in(c, b, 2 * n - 6)
                    take_conv_in(c, b, 2 * n - 5)
                if n == 6:
                    silu_xc(c, b)
                if n == 7:
                    take_rows(c, b)
                if n == 8:
                    second_part(c, b)
                if n in (10, 11):
                    softplus_in(c, b, n - 10)
                if n == 12:
                    softplus_exp(c)
                if n == 13:
                    softplus_ln(c, b)
                if n in (13, 15):
                    take_z(c, b, n - 13)
                    take_z(c, b, n - 12)

            def prologue():
                root(0)
                take_xT(0)
                for n in range(NS):
                    prep(0, 0, n)
                root(1)
                act.wait_ge(s_an, 1)

            def chunk(i, b, has_prev, has_next):
                c = 2 * i + b
                wait(act, s_dt, c + 1)
                for n in range(NS):
                    wait(act, s_h, NS * c + n - 1)
                    for d in range(KI):
                        nc.scalar.activation(dA[:, n % 2, d, :], dt[:, b, d, :], ACT.Exp,
                                             scale=aneg[:, d, n:n + 1]).then_inc(s_da, 1)
                    if has_next:
                        prep(c + 1, 1 - b, n)
                    if n == 0 and has_next:
                        take_xT(c + 1)
                    if n == 6:
                        silu_z(c, b)
                    if n == 13 and has_two(i):
                        root(c + 2)

            every_chunk(act, prologue, chunk)

        @block.tensor
        def _(pe):
            pe.wait_ge(s_w, 16 * (NW - 1))
            pe.wait_ge(s_id, 2)
            pe.wait_ge(s_sel, 4)

            def transposes(c):
                wait(pe, s_xn, c + 1)
                for k in range(KM):
                    wait(pe, s_free[k], prep_fill(c))
                    for t in range(TT):
                        last = nc.tensor.transpose(fill[:, k, t * P:(t + 1) * P],
                                                   xn[:, t, k * P:(k + 1) * P], ident[:, :])
                    last.then_inc(s_full[k], 1)

            def project_in(c, e):
                bank, f = e % 2, (prep_fill(c) + CONV + e // 2 if e < 4 else late_fill(c, e // 2 - 1))
                if e == 0:
                    wait(pe, s_free[1], f)
                wait(pe, s_free[bank], f)
                for k in range(KM):
                    last = nc.tensor.matmul(fill[:, bank, :], w_in[:, k, e * P:(e + 1) * P], xT[:, k, :],
                                            start=(k == 0), stop=(k == KM - 1))
                last.then_inc(s_full[bank], 1)

            def project_rows(c):
                wait(pe, s_xc, c + 1)
                wait(pe, s_free[0], late_fill(c, 0))
                for k in range(KI):
                    last = nc.tensor.matmul(fill[0:NR + NS, 0, :], w_x[:, k, :], xc[:, k, :],
                                            start=(k == 0), stop=(k == KI - 1))
                last.then_inc(s_full[0], 1)

            def spread(dst, b, r):
                return nc.tensor.matmul(dst, sel[:, r:r + 1].to_broadcast([96, P]), parts[:, b, :],
                                        start=True, stop=True)

            def spread_dt(c, b):
                wait(pe, s_p0, c + 1)
                wait(pe, s_p1, 2 * (c + 1))
                wait(pe, s_p2, c + 1)
                wait(pe, s_free[1], late_fill(c, 0))
                spread(fill[:, 1, :], b, NS).then_inc(s_full[1], 1)

            def spread_c(c, b, n):
                wait(pe, s_hc, NS * c + n - 1)
                spread(c_ps[:, n % 2, :], b, n).then_inc(s_cb, 1)

            def project_out(c, b, bank, *place):
                f = out_fill(c, *place)
                wait(pe, s_free[bank], f)
                for t in (2 * bank, 2 * bank + 1):
                    for d in range(KI):
                        last = nc.tensor.matmul(fill[:, bank, (t % 2) * DM:(t % 2 + 1) * DM],
                                                zs[:, b, d, t * P:(t + 1) * P], w_out[:, d, :],
                                                start=(d == 0), stop=(d == KI - 1))
                last.then_inc(s_full[bank], 1)

            def prep(c, b, n):
                if n in (2, 3):
                    project_in(c, 2 * n - 4)
                    project_in(c, 2 * n - 3)
                if n == 7:
                    project_rows(c)
                if n == 9:
                    spread_dt(c, b)
                    project_in(c, 4)
                if n >= 11 and n < 14:
                    project_in(c, n - 6)

            def prologue():
                transposes(0)
                for n in range(NS):
                    prep(0, 0, n)
                transposes(1)
                spread_c(0, 0, 0)
                spread_c(0, 0, 1)

            def chunk(i, b, has_prev, has_next):
                c = 2 * i + b
                for n in range(NS):
                    if n == 0:
                        if has_next:
                            prep(c + 1, 1 - b, 2)
                        wait(pe, s_g, c)
                        for d in range(KI):
                            last = nc.tensor.matmul(y_ps[:, d, :], diag[:, d, :], xc[:, d, :],
                                                    start=True, stop=False)
                        last.then_inc(s_dx, 1)
                    if n == NS - 1 and has_next:
                        spread_c(c + 1, 1 - b, 0)
                    wait(pe, s_hc, NS * c + n + 1)
                    for d in range(KI):
                        last = nc.tensor.matmul(y_ps[:, d, :], ident[:, :], h[:, n % HR, d, :],
                                                start=False, stop=(n == NS - 1))
                    last.then_inc(s_ys, 1)
                    if n + 2 < NS:
                        spread_c(c, b, n + 2)
                    if n in (3, 4) and has_prev:
                        project_out(c - 1, 1 - b, n - 3, not has_next)
                    if has_next and 0 < n < NS - 2:
                        prep(c + 1, 1 - b, n + 2)
                    if n == NS - 3 and has_two(i):
                        transposes(c + 2)
                if has_next:
                    spread_c(c + 1, 1 - b, 1)

            every_chunk(pe, prologue, chunk)
            pe.wait_ge(s_g, 2 * NI)
            for bank in range(2):
                project_out(2 * NI - 1, 1, bank, False, True)

        @block.vector
        def _(dve):
            def norm_stats(c):
                wait(dve, s_x, 16 * (c + 1))
                for t in range(TT):
                    last = nc.vector.bn_stats(stats[:, t, :], xn[:, t, :])
                last.then_inc(s_st1, 1)
                wait_apart(dve, s_st1, c + 1, s_w)
                for t in range(TT):
                    last = nc.vector.bn_aggr(mv[:, t, :], stats[:, t, :])
                last.then_inc(s_mv, 1)

            def norm_apply(c):
                wait(dve, s_sd, c + 1)
                nc.vector.reciprocal(rs[:, :], sd[:, :]).then_inc(s_rs, 1)
                wait(dve, s_rs, c + 1)
                for t in range(TT):
                    last = nc.vector.tensor_scalar(xn[:, t, :], xn[:, t, :], mv[:, t, 0:1], rs[:, t:t + 1],
                                                   ALU.subtract, ALU.mult)
                last.then_inc(s_xn, 1)

            def add_taps(c, d):
                wait(dve, s_free[d % 2], prep_fill(c) + 2 + d // 2)
                wait(dve, s_halo, c + 1)
                for k in range(HALO):
                    if k:
                        wait(dve, s_cv, HALO * (KI * c + d) + k)
                    nc.vector.scalar_tensor_tensor(
                        out=xc[:, d, :], in0=xs[:, d, k:k + CH], scalar=cw[:, d, k:k + 1],
                        in1=xc[:, d, :], op0=ALU.mult, op1=ALU.add).then_inc(s_cv, 1)

            def rounding(c):
                wait(dve, s_ln, 2 * c + 1)
                nc.vector.scalar_tensor_tensor(out=tB[:, :, :], in0=tB[:, :, :], scalar=-1.0, in1=tA,
                                               op0=ALU.add, op1=ALU.subtract).then_inc(s_q, 1)

            def rest(c, b):
                wait(dve, s_free[0], late_fill(c, 0) + 1)
                wait(dve, s_p0, c + 1)
                nc.vector.tensor_tensor(r1[:, :], pr[0:NR, :], parts[0:NR, b, :], ALU.subtract
                                        ).then_inc(s_r1, 1)

            def third_part(c, b):
                wait(dve, s_p1, 2 * (c + 1))
                nc.vector.tensor_tensor(parts[64:64 + NR, b, :], r1[:, :], p1[:, :], ALU.subtract
                                        ).then_inc(s_p2, 1)

            def residual(c, *place):
                wait(dve, s_xr, 16 * (c + 1))
                f = out_fill(c, *place)
                for bank in range(2):
                    wait(dve, s_full[bank], f + 1)
                    nc.vector.tensor_tensor(flat(xres[:, 2 * bank:2 * bank + 2, :]), fill[:, bank, :],
                                            flat(xres[:, 2 * bank:2 * bank + 2, :]), ALU.add
                                            ).then_inc(s_free[bank], 1)

            def prep(c, b, n):
                if n in (4, 5):
                    add_taps(c, 2 * n - 8)
                    add_taps(c, 2 * n - 7)
                if n == 7:
                    rest(c, b)
                if n == 8:
                    third_part(c, b)
                if n == 12:
                    rounding(c)

            def scans(c, b, n, half):
                if half == 0:
                    wait(dve, s_bx, NS * c + n + 1)
                    wait(dve, s_ys, NS * c + n - HR + 1)
                for d in (2 * half, 2 * half + 1):
                    wait(dve, s_da, KI * (NS * c + n) + d + 1)
                    last = nc.vector.tensor_tensor_scan(
                        h[:, n % HR, d, :], dA[:, n % 2, d, :], bx[:, n % BR, d, :],
                        state[:, b, n, d:d + 1], ALU.mult, ALU.add)
                if half == 1:
                    last.then_inc(s_h, 1)

            def save_state(c, b, n):
                wait(dve, s_h, NS * c + n + 1)
                nc.vector.tensor_copy(state[:, b, n, :], h[:, n % HR, :, CH - 1]).then_inc(s_sv, 1)

            def times_c(c, b, n):
                wait(dve, s_sv, NS * c + n + 1)
                wait(dve, s_cb, NS * c + n + 1)
                nc.vector.tensor_tensor(h[:, n % HR], h[:, n % HR],
                                        c_ps[:, n % 2, None, :].to_broadcast([P, KI, CH]), ALU.mult
                                        ).then_inc(s_hc, 1)

            def gate(c, b):
                wait(dve, s_ys, NS * (c + 1))
                wait(dve, s_zs, c + 1)
                nc.vector.tensor_tensor(zs[:, b], y_ps[:, :, :], zs[:, b], ALU.mult).then_inc(s_g, 1)

            def prologue():
                dve.wait_ge(s_w, 16 * (NW - 1))
                dve.wait_ge(s_set, 4)
                dve.wait_ge(s_id, 2)
                nc.vector.tensor_tensor(sel_f[:, :], ident[0:96, 0:NR], ident[0:96, 32:32 + NR], ALU.add
                                        ).then_inc(s_sel, 1)
                dve.wait_ge(s_sel, 1)
                nc.vector.tensor_tensor(sel_f[:, :], sel_f[:, :], ident[0:96, 64:64 + NR], ALU.add
                                        ).then_inc(s_sel, 1)
                dve.wait_ge(s_sel, 2)
                nc.vector.tensor_copy(sel[:, :], sel_f[:, :]).then_inc(s_sel, 1)
                for d in range(KI):
                    last = nc.vector.tensor_scalar(diag[:, d, :], ident[:, :], dpar[:, d:d + 1], None, ALU.mult)
                last.then_inc(s_sel, 1)
                norm_stats(0)
                norm_apply(0)
                for n in range(NS):
                    prep(0, 0, n)
                norm_stats(1)
                norm_apply(1)

            def chunk(i, b, has_prev, has_next):
                c = 2 * i + b
                for n in range(NS):
                    scans(c, b, n, 0)
                    before = (c, b, n - 1) if n > 0 else (c - 1, 1 - b, NS - 1)
                    if n > 0 or has_prev:
                        save_state(*before)
                    scans(c, b, n, 1)
                    if n > 0 or has_prev:
                        times_c(*before)
                    if n == 1 and has_prev:
                        gate(c - 1, 1 - b)
                    if n == 6 and has_prev:
                        residual(c - 1, not has_next)
                    if has_next:
                        prep(c + 1, 1 - b, n)
                    if n == 12 and has_two(i):
                        norm_stats(c + 2)
                    if n == 13 and has_two(i):
                        norm_apply(c + 2)

            every_chunk(dve, prologue, chunk)
            save_state(2 * NI - 1, 1, NS - 1)
            times_c(2 * NI - 1, 1, NS - 1)
            gate(2 * NI - 1, 1)
            residual(2 * NI - 1, False, True)


NH = 16
HD = DM // NH
HP = NH // 2
VW = 2 * (HD + 1)


def qkv_stage(nc, x1_dram, ln1_w, wqT, wkT, wvT, f_dram, parts_dram, v_all):
    B, L, _ = x1_dram.shape
    NI = L // CH
    NC = B * NI
    assert B == 2

    with ExitStack() as ctx:
        def sb(name, shape, dt=F32):
            return ctx.enter_context(nc.sbuf_tensor(name, shape, dt))

        def ps(name, shape, dt=F32):
            return ctx.enter_context(nc.psum_tensor(name, shape, dt))

        def sem(name):
            return ctx.enter_context(nc.semaphore(name))

        wq = sb("wq", [P, KM, DM])
        wk = sb("wk", [P, KM, DM])
        wv = sb("wv", [P, KM, DM])
        ln1 = sb("ln1", [P, KM])
        ident = sb("q_ident", [P, P])
        epsc = sb("q_epsc", [P, 1])
        xa = sb("xa", [P, 2, TT, DM])
        fo = sb("fo", [P, 2, TT, DM])
        an = sb("an", [P, 2, TT, DM])
        stats = sb("q_stats", [P, TT, 6])
        mv = sb("q_mv", [P, 2, TT, 2])
        sd = sb("q_sd", [P, 2, TT])
        rs = sb("q_rs", [P, 2, TT])
        ms = sb("q_ms", [P, 2, TT])
        rr = sb("q_rr", [P, 2, TT])
        aT = sb("aT", [P, 2, KM, CH])
        part = sb("part", [P, 2, 3, 2 * KM, CH], BF16)
        rest = sb("rest", [P, 2 * KM, CH])
        tr_ps = ps("tr_ps", [P, KM, CH])
        qk_ps = ps("qk_ps", [P, 2 * KM, CH])
        v_ps = ps("v_ps", [P, TT, DM])

        s_w = sem("q_w")
        s_id = sem("q_id")
        s_set = sem("q_set")
        s_x = [sem("q_x0"), sem("q_x1")]
        s_st = sem("q_st")
        s_sd = sem("q_sd_s")
        s_rs = sem("q_rs_s")
        s_ms = sem("q_ms_s")
        s_f = sem("q_f")
        s_a = sem("q_a")
        s_fst = [sem("q_fst0"), sem("q_fst1")]
        s_tr = sem("q_tr")
        s_aT = sem("q_aT")
        s_qk = sem("q_qk")
        s_v = sem("q_v")
        s_p1 = sem("q_p1")
        s_r = sem("q_r")
        s_p2 = sem("q_p2")
        s_p3 = sem("q_p3")
        s_pst = [sem("q_pst0"), sem("q_pst1")]
        s_vout = sem("q_vout")

        block = ctx.enter_context(nc.Block())

        def every_chunk(front, step, eng):
            front(0, 0)
            step(0, 0, 0, 1)
            with eng.Fori(1, NI) as i:
                step(i - 1, 1, i, 0)
                step(i, 0, i, 1)
            step(NI - 1, 1, None, None)

        @block.sync
        def _(sp):
            for dst, src in ((wq, wqT), (wk, wkT), (wv, wvT)):
                sp.dma_start(dst[:, :, :], src.rearrange("(k p) e -> p k e", p=P)).then_inc(s_w, 16)
            with nc.allow_non_contiguous_dma(reason="one small vector, once"):
                sp.dma_start(ln1[:, :], ln1_w.rearrange("(k p) -> p k", p=P)).then_inc(s_w, 16)

            def tokens(dram, i, b):
                return dram[b, bass.ds(i * CH, CH), :].rearrange("(t p) e -> p t e", p=P)

            def load(i, b):
                sp.dma_start(xa[:, b], tokens(x1_dram, i, b)).then_inc(s_x[b], 16)

            def store(i, b):
                wait_apart(sp, s_f, 2 * i + b + 1, s_w)
                sp.dma_start(tokens(f_dram, i, b), fo[:, b]).then_inc(s_fst[b], 16)

            load(0, 0)
            load(0, 1)
            with sp.Fori(1, NI) as i:
                for b in range(2):
                    store(i - 1, b)
                    load(i, b)
            store(NI - 1, 0)
            store(NI - 1, 1)
            for b in range(2):
                sp.wait_ge(s_fst[b], 16 * NI)

        @block.gpsimd
        def _(pool):
            nc.gpsimd.memset(ident[:, :], 0.0).then_inc(s_id, 1)
            nc.gpsimd.memset(epsc[:, :], EPS).then_inc(s_set, 1)
            for hh in range(2):
                col = hh * (HD + 1) + HD
                nc.gpsimd.memset(v_all[:, :, :, col:col + 1], 1.0).then_inc(s_set, 1)
            pool.wait_ge(s_id, 1)
            nc.gpsimd.affine_select(out=ident[:, :], in_=ident[:, :], compare_op=ALU.not_equal, fill=1.0,
                                    base=0, pattern=[[-1, P]], channel_multiplier=1).then_inc(s_id, 1)

            def store(i, b):
                c = 2 * i + b
                for s, ready in enumerate((s_p1, s_p2, s_p3)):
                    wait_apart(pool, ready, c + 1, s_id)
                    for m in range(2):
                        dst = parts_dram[m, s, b * DM:(b + 1) * DM, bass.ds(i * CH, CH)]
                        nc.gpsimd.dma_start(dst.rearrange("(k p) l -> p k l", p=P),
                                            part[:, b, s, m * KM:(m + 1) * KM, :]).then_inc(s_pst[b], 16)

            store(0, 0)
            store(0, 1)
            with pool.Fori(1, NI) as i:
                store(i, 0)
                store(i, 1)
            for b in range(2):
                pool.wait_ge(s_pst[b], 16 * 6 * NI)

        @block.scalar
        def _(act):
            act.wait_ge(s_w, 64)
            act.wait_ge(s_set, 3)

            def roots(i, b):
                c = 2 * i + b
                wait(act, s_st, 2 * c + 2)
                nc.scalar.activation(sd[:, b, :], mv[:, b, :, 1], ACT.Sqrt, bias=epsc[:, 0:1]
                                     ).then_inc(s_sd, 1)
                wait(act, s_ms, 2 * c + 2)
                nc.scalar.activation(sd[:, b, :], ms[:, b, :], ACT.Sqrt, bias=epsc[:, 0:1]
                                     ).then_inc(s_sd, 1)

            def take_aT(i, b):
                c = 2 * i + b
                wait(act, s_tr, c + 1)
                wait(act, s_v, c - 1)
                for k in range(KM):
                    nc.scalar.activation(aT[:, b, k, :], tr_ps[:, k, :], ACT.Identity,
                                         scale=ln1[:, k:k + 1]).then_inc(s_aT, 1)

            def front(i, b):
                roots(i, b)
                take_aT(i, b)

            def step(i, b, i2, b2):
                c = 2 * i + b
                if b2 is not None:
                    roots(i2, b2)
                wait(act, s_qk, c + 1)
                wait(act, s_pst[b], 16 * 6 * i)
                nc.scalar.copy(part[:, b, 0], qk_ps[:, :, :]).then_inc(s_p1, 1)
                if b2 is not None:
                    take_aT(i2, b2)
                wait(act, s_r, c + 1)
                nc.scalar.copy(part[:, b, 1], rest[:, :, :]).then_inc(s_p2, 1)

            every_chunk(front, step, act)

        @block.tensor
        def _(pe):
            pe.wait_ge(s_w, 64)
            pe.wait_ge(s_id, 2)

            def front(i, b):
                c = 2 * i + b
                wait(pe, s_a, c + 1)
                wait(pe, s_aT, 2 * c)
                for k in range(KM):
                    for t in range(TT):
                        last = nc.tensor.transpose(tr_ps[:, k, t * P:(t + 1) * P],
                                                   an[:, b, t, k * P:(k + 1) * P], ident[:, :])
                last.then_inc(s_tr, 1)

            def step(i, b, i2, b2):
                c = 2 * i + b
                wait(pe, s_aT, 2 * c + 2)
                wait(pe, s_r, c)
                for m, w in enumerate((wq, wk)):
                    for o in range(KM):
                        for k in range(KM):
                            last = nc.tensor.matmul(qk_ps[:, m * KM + o, :], w[:, k, o * P:(o + 1) * P],
                                                    aT[:, b, k, :], start=(k == 0), stop=(k == KM - 1))
                last.then_inc(s_qk, 1)
                if b2 is not None:
                    front(i2, b2)
                wait(pe, s_vout, c)
                for t in range(TT):
                    for k in range(KM):
                        last = nc.tensor.matmul(v_ps[:, t, :], aT[:, b, k, t * P:(t + 1) * P], wv[:, k, :],
                                                start=(k == 0), stop=(k == KM - 1))
                last.then_inc(s_v, 1)

            every_chunk(front, step, pe)

        @block.vector
        def _(dve):
            dve.wait_ge(s_set, 3)

            def front(i, b):
                c = 2 * i + b
                wait(dve, s_x[b], 16 * (i + 1))
                for t in range(TT):
                    last = nc.vector.bn_stats(stats[:, t, :], xa[:, b, t, :])
                last.then_inc(s_st, 1)
                wait_apart(dve, s_st, 2 * c + 1, s_w)
                for t in range(TT):
                    last = nc.vector.bn_aggr(mv[:, b, t, :], stats[:, t, :])
                last.then_inc(s_st, 1)
                wait(dve, s_sd, 2 * c + 1)
                nc.vector.reciprocal(rs[:, b, :], sd[:, b, :]).then_inc(s_rs, 1)
                wait(dve, s_rs, 2 * c + 1)
                nc.vector.tensor_tensor(ms[:, b, :], mv[:, b, :, 1], rs[:, b, :], ALU.mult).then_inc(s_ms, 1)
                wait(dve, s_fst[b], 16 * i)
                for t in range(TT):
                    last = nc.vector.tensor_scalar(fo[:, b, t, :], xa[:, b, t, :], mv[:, b, t, 0:1],
                                                   rs[:, b, t:t + 1], ALU.subtract, ALU.mult)
                last.then_inc(s_f, 1)
                wait(dve, s_ms, 2 * c + 1)
                nc.vector.tensor_tensor(ms[:, b, :], ms[:, b, :], rs[:, b, :], ALU.mult).then_inc(s_ms, 1)
                wait(dve, s_sd, 2 * c + 2)
                nc.vector.reciprocal(rr[:, b, :], sd[:, b, :]).then_inc(s_rs, 1)
                wait(dve, s_rs, 2 * c + 2)
                wait(dve, s_f, c + 1)
                wait(dve, s_tr, c - 1)
                for t in range(TT):
                    last = nc.vector.tensor_scalar(an[:, b, t, :], fo[:, b, t, :], rr[:, b, t:t + 1],
                                                   None, ALU.mult)
                last.then_inc(s_a, 1)

            def step(i, b, i2, b2):
                c = 2 * i + b
                if b2 is not None:
                    front(i2, b2)
                wait(dve, s_p1, c + 1)
                wait(dve, s_p3, c)
                nc.vector.tensor_tensor(rest[:, :, :], qk_ps[:, :, :], part[:, b, 0], ALU.subtract).then_inc(s_r, 1)
                wait_apart(dve, s_v, c + 1, s_w)
                for t in range(TT):
                    dst = v_all[:, b * HP:(b + 1) * HP, bass.ds(i * TT + t, 1), :]
                    dst = dst.rearrange("p a o (h w) -> p (a o) h w", h=2)[:, :, :, 0:HD]
                    src = v_ps[:, t, :].rearrange("p (a h w) -> p a h w", h=2, w=HD)
                    last = nc.vector.tensor_copy(dst, src)
                last.then_inc(s_vout, 1)
                wait(dve, s_p2, c + 1)
                wait(dve, s_r, c + 1)
                nc.vector.tensor_tensor(part[:, b, 2], rest[:, :, :], part[:, b, 1], ALU.subtract
                                        ).then_inc(s_p3, 1)

            every_chunk(front, step, dve)


def attention_stage(nc, parts_dram, v_all, att, B, L):
    NP = B * HP
    QC = L // CH
    KT = L // P
    KK = 2 * KT
    LEAD = 4
    HW = 2 * CH
    NHALF = L // HW
    NMAX = KT * NHALF
    assert NMAX == KK and QC == 4 and NP % 2 == 0 and NP >= 6
    ROWS = 6 * HD + 2
    SC = float(HD) ** -0.5
    SR = 3
    PR = 4

    with ExitStack() as ctx:
        def sb(name, shape, dt=F32):
            return ctx.enter_context(nc.sbuf_tensor(name, shape, dt))

        def ps(name, shape, dt=F32):
            return ctx.enter_context(nc.psum_tensor(name, shape, dt))

        def sem(name):
            return ctx.enter_context(nc.semaphore(name))

        qs = sb("qs", [ROWS, 2, 2, L], BF16)
        ks = sb("ks", [ROWS, 2, 2, L], BF16)
        q4 = sb("q4", [P, 2, L], BF16)
        k4 = sb("k4", [P, 2, L], BF16)
        vst = sb("vst", [P, 2, KT, 64])
        prob = sb("prob", [P, PR, QC, CH])
        osb = sb("osb", [P, 2, CH])
        nmh = sb("nmh", [P, 2, KT, NHALF])
        nm = sb("nm", [P, 2 * KT])
        nmr = sb("nmr", [2 * KT, 2, P], BF16)
        rec = sb("rec", [P, 2, QC * TT])
        ident = sb("a_ident", [P, P])
        s_ps = ps("s_ps", [P, SR, CH])
        acc = ps("acc", [P, CH])
        ring = ps("ring", [P, 2, HW])

        s_id = sem("a_id")
        s_one = sem("a_one")
        s_op = [sem("a_op0"), sem("a_op1")]
        s_op4 = [sem("a_op40"), sem("a_op41")]
        s_mr = [sem("a_mr0"), sem("a_mr1")]
        s_vst = sem("a_vst")
        s_S = sem("a_S")
        s_exp = sem("a_exp")
        s_pv = sem("a_pv")
        s_o = sem("a_o")
        s_full = [sem("a_full0"), sem("a_full1")]
        s_free = [sem("a_free0"), sem("a_free1")]
        s_comb = sem("a_comb")
        s_nmr1 = sem("a_nmr1")
        s_rec = sem("a_rec")

        Q_PARTS = (0, 0, 1, 1, 0, 2)
        K_PARTS = (0, 1, 0, 1, 2, 0)
        LOADS = 16 * 2 * 2 * 6
        LOADS4 = 16 * 2 * 2 * 4

        MAXNEXT, MAXTHEN, ROWMAX, OUT = "maximum, next pair", "maximum, pair after", "rows of the maximum", "output"

        def plan(has_prev, has_next, has_then):
            steps = [[] for _ in range(KK)]
            if has_prev:
                steps[2].append((OUT, 1))
            steps[KT + 2].append((OUT, 0))
            if has_next:
                for j in range(LEAD, NMAX):
                    steps[j - LEAD].append((MAXNEXT, j))
                steps[NMAX - LEAD].append((ROWMAX, 0))
            if has_then:
                for j in range(LEAD):
                    steps[NMAX - LEAD + j].append((MAXTHEN, j))
            return steps

        def fills_before(pair, s):
            first = (NMAX + 1 + LEAD, NMAX + LEAD)[s]
            return first + (NMAX + 2 - s) * pair - (1 if s == 0 and not (isinstance(pair, int) and pair == 0) else 0)

        class Count:
            def __init__(self, pair, last=False, start=False):
                if start:
                    self.n = [0, 0]
                else:
                    self.n = [fills_before(pair, s) - (LEAD if last else 0) for s in range(2)]

            def next(self, s):
                self.n[s] = self.n[s] + 1
                return self.n[s]

        def every_pair(eng, prologue, pair, epilogue=None):
            prologue()
            pair(0, 0, 0, False, True, True)
            pair(1, 0, 1, True, True, True)
            with eng.Fori(1, NP // 2 - 1) as it:
                for par in range(2):
                    pair(2 * it + par, it, par, True, True, True)
            pair(NP - 2, NP // 2 - 1, 0, True, True, False)
            pair(NP - 1, NP // 2 - 1, 1, True, False, False)
            if epilogue:
                epilogue()

        block = ctx.enter_context(nc.Block())

        @block.sync
        def _(sp):
            def load(dst, at, par_hh, m, order, n, s):
                for g, part in enumerate(order):
                    src = parts_dram[m, part, bass.ds(n * 2 * HD + par_hh[-1] * HD, HD), :]
                    rows = slice(at + g * HD, at + (g + 1) * HD)
                    out = dst[rows, par_hh[0], par_hh[1], :] if dst is qs or dst is ks else dst[rows, par_hh[0], :]
                    sp.dma_start(out, src).then_inc(s, 16)

            def load_stack(n, par):
                wait_apart(sp, s_S, KK * QC * (n - 1), s_one)
                for hh in range(2):
                    load(qs, 0, (par, hh), 0, Q_PARTS, n, s_op[par])
                    load(ks, 0, (par, hh), 1, K_PARTS, n, s_op[par])

            def load_lead(n, par):
                if not isinstance(n, int) or n > 1:
                    for s in range(2):
                        wait_apart(sp, s_free[s], fills_before(n - 2, s), s_one)
                for hh in range(2):
                    load(q4, 64 * hh, (par, hh), 0, Q_PARTS[0:4], n, s_op4[par])
                    load(k4, 64 * hh, (par, hh), 1, K_PARTS[0:4], n, s_op4[par])

            def max_rows(n, par, fills):
                wait_apart(sp, s_free[0], fills, s_one)
                for hh in range(2):
                    for s in range(2):
                        sp.dma_start(qs[6 * HD + s:6 * HD + s + 1, par, hh, :],
                                     nmr[hh * KT:(hh + 1) * KT, s, :]).then_inc(s_mr[par], 16)

            def prologue():
                load_lead(0, 0)
                load_stack(0, 0)
                load_lead(1, 1)
                load_stack(1, 1)
                max_rows(0, 0, NMAX + 1)

            def pair(n, it, par, has_prev, has_next, has_then):
                if has_prev and has_next:
                    load_stack(n + 1, 1 - par)
                if has_then:
                    load_lead(n + 2, par)
                if has_next:
                    ct = Count(n)
                    for ops in plan(has_prev, has_next, has_then):
                        for op, j in ops:
                            if op == ROWMAX:
                                max_rows(n + 1, 1 - par, ct.next(0))
                            elif op == OUT:
                                ct.next(1 - j)
                            elif op == MAXNEXT or op == MAXTHEN:
                                ct.next(0)
                                ct.next(1)

            every_pair(sp, prologue, pair)

        @block.gpsimd
        def _(pool):
            nc.gpsimd.memset(ident[:, :], 0.0).then_inc(s_id, 1)
            nc.gpsimd.memset(vst[:, :, :, :], 0.0).then_inc(s_one, 1)
            for par in range(2):
                pool.wait_ge(s_one, par + 1)
                nc.gpsimd.memset(ks[6 * HD:6 * HD + 2, par, :, :], 1.0).then_inc(s_one, 1)
            pool.wait_ge(s_id, 1)
            pool.wait_ge(s_one, 3)
            nc.gpsimd.affine_select(out=ident[:, :], in_=ident[:, :], compare_op=ALU.not_equal, fill=1.0,
                                    base=0, pattern=[[-1, P]], channel_multiplier=1).then_inc(s_id, 1)

            def pair(n, it, par, has_prev, has_next, has_then):
                wait_apart(pool, s_pv, KK * (n - 1), s_id)
                src = v_all[:, bass.ds(n, 1), :, :].rearrange("p a t w -> p (a t) w")
                nc.gpsimd.tensor_copy(vst[:, par, :, 0:VW], src).then_inc(s_vst, 1)

            every_pair(pool, lambda: None, pair)

        @block.scalar
        def _(act):
            def pair(n, it, par, has_prev, has_next, has_then):
                for k in range(KK):
                    wait(act, s_pv, KK * n + k - PR + 1)
                    for j in range(QC):
                        m = QC * k + j
                        wait(act, s_S, KK * QC * n + m + 1)
                        nc.scalar.activation(prob[:, k % PR, j, :], s_ps[:, m % SR, :], ACT.Exp,
                                             scale=SC).then_inc(s_exp, 1)

            every_pair(act, lambda: None, pair)

        @block.tensor
        def _(pe):
            pe.wait_ge(s_id, 2)
            pe.wait_ge(s_one, 3)
            NU = KK * QC

            def maxima(ct, par, j, hh):
                t, half = j // NHALF, j % NHALF
                wait(pe, s_free[hh], ct.next(hh) - 1)
                r = slice(64 * hh, 64 * hh + 64)
                for b in range(2):
                    at = half * HW + b * CH
                    ins = nc.tensor.matmul(ring[:, hh, b * CH:(b + 1) * CH],
                                           q4[r, par, t * P:(t + 1) * P], k4[r, par, at:at + CH],
                                           start=True, stop=True)
                ins.then_inc(s_full[hh], 1)

            def rows_of_max(ct, n):
                wait(pe, s_free[0], ct.next(0) - 1)
                wait(pe, s_comb, n + 1)
                nc.tensor.transpose(ring[0:2 * KT, 0, 0:P], nm[:, :], ident[:, :]).then_inc(s_full[0], 1)

            def outputs(ct, n, hh):
                s = 1 - hh
                wait(pe, s_free[s], ct.next(s) - 1)
                wait(pe, s_o, 2 * n + hh + 1)
                for t in range(TT):
                    last = nc.tensor.transpose(ring[:, s, t * P:(t + 1) * P], osb[:, hh, t * P:(t + 1) * P],
                                               ident[:, :])
                last.then_inc(s_full[s], 1)

            def scores(n, par, k, j):
                m = QC * k + j
                hh, t = k // KT, k % KT
                back = m - SR if m >= SR else max(x for x in range(NU) if x % SR == m % SR) - NU
                wait(pe, s_exp, NU * n + back + 1)
                nc.tensor.matmul(s_ps[:, m % SR, :], ks[:, par, hh, t * P:(t + 1) * P],
                                 qs[:, par, hh, j * CH:(j + 1) * CH], start=True, stop=True).then_inc(s_S, 1)

            def values(n, par, k):
                hh, t = k // KT, k % KT
                if t == 0:
                    wait(pe, s_o, 2 * n + hh)
                if k == 0:
                    wait(pe, s_vst, n + 1)
                wait(pe, s_exp, NU * n + QC * (k + 1))
                for j in range(QC):
                    v0 = hh * (HD + 1)
                    last = nc.tensor.matmul(acc[32 * j:32 * j + 32, :], vst[:, par, t, v0:v0 + 32],
                                            prob[:, k % PR, j, :], start=(t == 0), stop=(t == KT - 1))
                last.then_inc(s_pv, 1)

            def prologue():
                ct = Count(0, start=True)
                pe.wait_ge(s_op4[0], LOADS4)
                for j in range(NMAX):
                    for s in range(2):
                        maxima(ct, 0, j, s)
                rows_of_max(ct, 0)
                pe.wait_ge(s_op4[1], LOADS4)
                for j in range(LEAD):
                    for s in range(2):
                        maxima(ct, 1, j, s)

            def pair(n, it, par, has_prev, has_next, has_then):
                ct = Count(n, last=not has_next)
                wait(pe, s_op[par], LOADS * (it + 1))
                wait(pe, s_mr[par], 64 * (it + 1))
                steps = plan(has_prev, has_next, has_then)

                def use_ring(k, s):
                    for op, j in steps[k]:
                        if op == MAXNEXT:
                            maxima(ct, 1 - par, j, s)
                        elif op == MAXTHEN:
                            if j == 0 and s == 0:
                                wait(pe, s_op4[par], LOADS4 * (it + 2))
                            maxima(ct, par, j, s)
                        elif op == ROWMAX and s == 0:
                            rows_of_max(ct, n + 1)
                        elif op == OUT and s == 1 - j:
                            outputs(ct, n - j, j)

                for k in range(KK):
                    scores(n, par, k, 0)
                    scores(n, par, k, 1)
                    use_ring(k, 0)
                    scores(n, par, k, 2)
                    scores(n, par, k, 3)
                    use_ring(k, 1)
                    if k > 0:
                        values(n, par, k - 1)
                    elif has_prev:
                        values(n - 1, 1 - par, KK - 1)

            def epilogue():
                values(NP - 1, 1, KK - 1)
                ct = Count(NP - 1, last=True)
                ct.next(0)
                ct.next(1)
                outputs(ct, NP - 1, 1)

            every_pair(pe, prologue, pair, epilogue)

        @block.vector
        def _(dve):
            def maxima(ct, j, s):
                t, half = j // NHALF, j % NHALF
                wait(dve, s_full[s], ct.next(s))
                nc.vector.tensor_reduce(nmh[:, s, t, half:half + 1], ring[:, s, :], AX.X, ALU.max,
                                        negate=True).then_inc(s_free[s], 1)

            def rows_of_max(ct, n):
                for s in range(2):
                    wait(dve, s_free[s], ct.n[s])
                nc.vector.tensor_tensor(nm[:, :], nmh[:, :, :, 0].rearrange("p h t -> p (h t)"),
                                        nmh[:, :, :, 1].rearrange("p h t -> p (h t)"), ALU.min
                                        ).then_inc(s_comb, 1)
                wait(dve, s_full[0], ct.next(0))
                if not (isinstance(n, int) and n == 0):
                    wait(dve, s_mr_prev[0], s_mr_prev[1])
                nc.vector.tensor_copy(nmr[:, 0, :], ring[0:2 * KT, 0, 0:P]).then_inc(s_nmr1, 1)
                wait(dve, s_nmr1, n + 1)
                nc.vector.tensor_tensor(nmr[:, 1, :], ring[0:2 * KT, 0, 0:P], nmr[:, 0, :], ALU.subtract
                                        ).then_inc(s_free[0], 1)

            s_mr_prev = [None, None]

            def outputs(ct, n, hh):
                s = 1 - hh
                wait(dve, s_full[s], ct.next(s))
                wait(dve, s_free[s], ct.n[s] - 1)
                got = ring[:, s, 0:CH].rearrange("p (c j w) -> p c j w", c=TT, j=QC)
                r = rec[:, hh, :].rearrange("p (c j) -> p c j", j=QC)
                nc.vector.reciprocal(r, got[:, :, :, HD]).then_inc(s_rec, 1)
                wait(dve, s_rec, 2 * n + hh + 1)
                dst = att[:, bass.ds(n, 1), :, hh * HD:(hh + 1) * HD].rearrange(
                    "p a (j c) w -> p c (a j) w", c=TT)
                nc.vector.tensor_tensor(dst, got[:, :, :, 0:HD], r[:, :, :, None].to_broadcast([P, TT, QC, HD]),
                                        ALU.mult).then_inc(s_free[s], 1)

            def read_acc(n, hh):
                wait(dve, s_pv, KK * n + KT * (hh + 1))
                nc.vector.tensor_copy(osb[:, hh, :], acc[:, :]).then_inc(s_o, 1)

            def prologue():
                ct = Count(0, start=True)
                for j in range(NMAX):
                    for s in range(2):
                        maxima(ct, j, s)
                rows_of_max(ct, 0)
                for j in range(LEAD):
                    for s in range(2):
                        maxima(ct, j, s)

            def pair(n, it, par, has_prev, has_next, has_then):
                ct = Count(n, last=not has_next)
                steps = plan(has_prev, has_next, has_then)
                for k in range(KK):
                    if k == 1 and has_prev:
                        read_acc(n - 1, 1)
                    if k == KT + 1:
                        read_acc(n, 0)
                    for s in range(2):
                        for op, j in steps[k]:
                            if op == MAXNEXT or op == MAXTHEN:
                                maxima(ct, j, s)
                            elif op == ROWMAX and s == 0:
                                s_mr_prev[0], s_mr_prev[1] = s_mr[par], 64 * (it + 1)
                                rows_of_max(ct, n + 1)
                            elif op == OUT and s == 1 - j:
                                outputs(ct, n - j, j)

            def epilogue():
                read_acc(NP - 1, 1)
                ct = Count(NP - 1, last=True)
                ct.next(0)
                ct.next(1)
                outputs(ct, NP - 1, 1)

            every_pair(dve, prologue, pair, epilogue)


def moe_stage(nc, x1_dram, f_dram, att, woT, ln2_w, gateT, w1T, w2T, w3T, xg_dram, y_dram, out):
    B, L, _ = x1_dram.shape
    NI = L // CH
    NE, _, FI = w1T.shape
    KF = FI // P
    BT = L // P
    NT = B * BT
    SLOT_TILES = y_dram.shape[0] // P
    assert B == 2 and NE == 8 and SLOT_TILES == slot_tiles(B * L, NE) and SLOT_TILES % 4 == 0
    REG = B * L + P
    assert xg_dram.shape[0] == NE * REG + P

    with ExitStack() as ctx:
        def sb(name, shape, dt=F32):
            return ctx.enter_context(nc.sbuf_tensor(name, shape, dt))

        def ps(name, shape, dt=F32):
            return ctx.enter_context(nc.psum_tensor(name, shape, dt))

        def sem(name):
            return ctx.enter_context(nc.semaphore(name))

        w1 = sb("w1", [P, NE, KM, FI])
        w3 = sb("w3", [P, NE, KM, FI])
        w2 = sb("w2", [P, NE, KF, DM])
        ln2 = sb("ln2", [P, KM])
        ident = sb("m_ident", [P, P])
        g = sb("g", [P, NT, DM])
        sh = sb("sh", [P, 2, NT])
        row_in = sb("row_in", [P, 2, NT], U32)
        row_out = sb("row_out", [P, 2, NT], U32)
        expert = sb("expert", [1, SLOT_TILES], U32)
        first_row = sb("first_row", [1, SLOT_TILES], U32)

        s_w = sem("m_w")
        s_we = sem("m_we")
        s_id = sem("m_id")
        s_set = sem("m_set")
        s_clear = sem("m_clear")
        s_sc = sem("m_sc")

        with ExitStack() as ctx2:
            def sb2(name, shape, dt=F32):
                return ctx2.enter_context(nc.sbuf_tensor(name, shape, dt))

            def ps2(name, shape, dt=F32):
                return ctx2.enter_context(nc.psum_tensor(name, shape, dt))

            wo = sb2("wo", [P, KM, DM])
            gate = sb2("gate", [P, KM, NE])
            epsc = sb2("m_epsc", [P, 1])
            iota = sb2("iota", [P, NE])
            starts = sb2("starts", [P, NT])
            tiles = sb2("tiles", [1, SLOT_TILES])
            before = sb2("before", [P, P], BF16)
            ones = sb2("ones", [P, P], BF16)
            zero = sb2("zero", [P, DM])
            behind = sb2("behind", [P, NE], U32)
            behind_f = sb2("behind_f", [P, NE])
            part_no = sb2("part_no", [P, 1])
            region = sb2("region", [P, NE])
            count = sb2("count", [P, NE])
            row_f = sb2("row_f", [P, 2, NT])
            one = sb2("one", [P, NT])
            idf = sb2("idf", [P, NT, 2])
            dif = sb2("dif", [P, NT])

            s_f = [sem("m_f0"), sem("m_f1")]
            s_at = sem("m_at")
            s_t1 = sem("m_t1")
            s_aT = sem("m_aT")
            s_wo = sem("m_wo")
            s_h = sem("m_h")
            s_st = sem("m_st")
            s_sd = sem("m_sd_s")
            s_rs = sem("m_rs_s")
            s_g = sem("m_g")
            s_base = sem("m_base")
            s_t2 = sem("m_t2")
            s_gT = sem("m_gT")
            s_lg = sem("m_lg")
            s_lc = sem("m_lc")
            s_top = sem("m_top")
            s_ix = sem("m_ix")
            s_dif = sem("m_dif")
            s_r = sem("m_r")
            s_ex = sem("m_ex")
            NRT = 7
            s_both1 = sem("m_both1")
            s_both = sem("m_both")
            s_rank = sem("m_rank")
            s_rt = sem("m_rt")
            s_row = sem("m_row")
            s_behind = sem("m_behind")

            def scatter(pool, c):
                pool.wait_ge(s_row, c + 1)
                tile0 = (c % 2) * BT + (c // 2) * TT
                for t in range(tile0, tile0 + TT):
                    for k in range(2):
                        nc.gpsimd.indirect_dma_start(
                            out=xg_dram[:, :],
                            out_offset=bass.IndirectOffsetOnAxis(ap=row_in[:, k, t:t + 1], axis=0),
                            in_=g[:, t, :], in_offset=None).then_inc(s_sc, 16)

            with ExitStack() as ctx3:
                def sb3(name, shape, dt=F32):
                    return ctx3.enter_context(nc.sbuf_tensor(name, shape, dt))

                def ps3(name, shape, dt=F32):
                    return ctx3.enter_context(nc.psum_tensor(name, shape, dt))

                attc = sb3("attc", [P, TT, DM])
                attT = sb3("attT", [P, KM, CH])
                gT = sb3("gT", [P, KM, CH])
                hc = sb3("hc", [P, 2, TT, DM])
                xr = sb3("xr", [P, 2, TT, DM])
                stats = sb3("m_stats", [P, TT, 6])
                mv = sb3("m_mv", [P, TT, 2])
                sd = sb3("m_sd", [P, TT])
                rs = sb3("m_rs", [P, TT])
                gs = sb3("gs", [P, 2, TT, DM])
                lgc = sb3("lgc", [P, 2, TT, NE])
                topc = sb3("topc", [P, 2, TT, 8])
                idxc = sb3("idxc", [P, 2, TT, 8], U32)
                t1_ps = ps3("t1_ps", [P, KM, CH])
                h_ps = ps3("h_ps", [P, TT, DM])
                t2_ps = ps3("t2_ps", [P, KM, CH])
                g_ps = ps3("g_ps", [P, CH])
                rank_ps = ps3("rank_ps", [P, CH])
                idc = sb3("idc", [P, TT, 2])
                hotc = sb3("hotc", [P, 2, 2, TT, NE])
                bothc = sb3("bothc", [P, 2, TT, NE], BF16)
                placec = sb3("placec", [P, TT, NE])
                pickc = sb3("pickc", [P, 2, TT, NE])
                rowc = sb3("rowc", [P, 2, TT])
                block = ctx3.enter_context(nc.Block())

                def every_chunk(eng, front, back):
                    front(0, 0)
                    front(0, 1)
                    back(0, 0)
                    with eng.Fori(1, NI) as i:
                        front(i, 0)
                        back(i - 1, 1)
                        front(i, 1)
                        back(i, 0)
                    back(NI - 1, 1)

                def every_step(eng, front, step):
                    front(0, 0)
                    step(0, 0, 0, 1)
                    with eng.Fori(1, NI) as i:
                        step(i - 1, 1, i, 0)
                        step(i, 0, i, 1)
                    step(NI - 1, 1, None, None)

                def before_it(i, b):
                    return (i, 0) if b else (i - 1, 1)

                @block.sync
                def _(sp):
                    sp.dma_start(wo[:, :, :], woT.rearrange("(k p) e -> p k e", p=P)).then_inc(s_w, 16)
                    sp.dma_start(gate[:, :, :], gateT.rearrange("(k p) e -> p k e", p=P)).then_inc(s_w, 16)
                    with nc.allow_non_contiguous_dma(reason="one small vector, once"):
                        sp.dma_start(ln2[:, :], ln2_w.rearrange("(k p) -> p k", p=P)).then_inc(s_w, 16)

                    def front(i, b):
                        c = 2 * i + b
                        wait_apart(sp, s_base, c - 1, s_w)
                        wait_apart(sp, s_g, c - 1, s_w)
                        for dst, src in ((hc, f_dram), (xr, x1_dram)):
                            sp.dma_start(dst[:, b], src[b, bass.ds(i * CH, CH), :].rearrange(
                                "(t p) e -> p t e", p=P)).then_inc(s_f[b], 16)

                    front(0, 0)
                    front(0, 1)
                    sp.wait_ge(s_set, 6)
                    sp.dma_start(xg_dram[NE * REG:NE * REG + P, :], zero[:, :]).then_inc(s_clear, 16)
                    sp.wait_ge(s_w, 48)
                    with sp.Fori(1, NI) as i:
                        front(i, 0)
                        front(i, 1)
                    for e in range(NE):
                        for dst, src in ((w1, w1T), (w3, w3T), (w2, w2T)):
                            sp.dma_start(dst[:, e], src[e].rearrange("(k p) e -> p k e", p=P)
                                         ).then_inc(s_we, 16)

                @block.gpsimd
                def _(pool):
                    nc.gpsimd.memset(epsc[:, :], EPS).then_inc(s_set, 1)
                    nc.gpsimd.memset(ones[:, :], 1.0).then_inc(s_set, 1)
                    nc.gpsimd.memset(before[:, :], 1.0).then_inc(s_set, 1)
                    nc.gpsimd.memset(zero[:, :], 0.0).then_inc(s_set, 1)
                    nc.gpsimd.iota(iota[:, :], pattern=[[1, NE]], base=0, channel_multiplier=0,
                                   allow_small_or_imprecise_dtypes=True).then_inc(s_set, 1)
                    nc.gpsimd.iota(starts[:, :], pattern=[[P, NT]], base=0, channel_multiplier=0,
                                   allow_small_or_imprecise_dtypes=True).then_inc(s_set, 1)
                    nc.gpsimd.memset(ident[:, :], 0.0).then_inc(s_id, 1)
                    pool.wait_ge(s_set, 6)
                    pool.wait_ge(s_id, 1)
                    nc.gpsimd.affine_select(out=ident[:, :], in_=ident[:, :], compare_op=ALU.not_equal, fill=1.0,
                                            base=0, pattern=[[-1, P]], channel_multiplier=1).then_inc(s_id, 1)
                    nc.gpsimd.affine_select(out=before[:, :], in_=before[:, :], compare_op=ALU.is_gt, fill=0.0,
                                            base=0, pattern=[[1, P]], channel_multiplier=-1).then_inc(s_set, 1)
                    pool.wait_ge(s_set, 7)
                    nc.gpsimd.iota(tiles[:, :], pattern=[[1, SLOT_TILES]], base=0, channel_multiplier=0,
                                   allow_small_or_imprecise_dtypes=True).then_inc(s_set, 1)
                    pool.wait_ge(s_set, 8)

                    nc.gpsimd.iota(part_no[:, :], pattern=[[0, 1]], base=0, channel_multiplier=1,
                                   allow_small_or_imprecise_dtypes=True).then_inc(s_set, 1)
                    nc.gpsimd.iota(region[:, :], pattern=[[REG, NE]], base=0, channel_multiplier=0,
                                   allow_small_or_imprecise_dtypes=True).then_inc(s_set, 1)
                    nc.gpsimd.iota(count[:, :], pattern=[[REG, NE]], base=0, channel_multiplier=0,
                                   allow_small_or_imprecise_dtypes=True).then_inc(s_set, 1)

                    def front(i, b):
                        c = 2 * i + b
                        wait_apart(pool, s_t1, c, s_id)
                        for t in range(TT):
                            src = att[:, b * HP:(b + 1) * HP, bass.ds(i * TT + t, 1), :]
                            last = nc.gpsimd.tensor_copy(attc[:, t, :].rearrange("p (n w) -> p n w", n=HP),
                                                         src.rearrange("p n o w -> p (n o) w"))
                        last.then_inc(s_at, 1)

                    front(0, 0)
                    for c in range(2 * NI):
                        if c + 1 < 2 * NI:
                            front((c + 1) // 2, (c + 1) % 2)
                        if c >= 2:
                            scatter(pool, c - 2)

                @block.scalar
                def _(act):
                    act.wait_ge(s_w, 48)
                    act.wait_ge(s_set, 6)

                    def take_attention(i, b):
                        c = 2 * i + b
                        wait(act, s_t1, c + 1)
                        wait(act, s_wo, c)
                        nc.scalar.copy(attT[:, :, :], t1_ps[:, :, :]).then_inc(s_aT, 1)

                    def root(i, b):
                        c = 2 * i + b
                        wait(act, s_st, 4 * c + 4)
                        nc.scalar.activation(sd[:, :], mv[:, :, 1], ACT.Sqrt, bias=epsc[:, 0:1]).then_inc(s_sd, 1)

                    def back(i, b):
                        c = 2 * i + b
                        wait(act, s_t2, c + 1)
                        wait(act, s_lg, c)
                        for k in range(KM):
                            nc.scalar.activation(gT[:, k, :], t2_ps[:, k, :], ACT.Identity,
                                                 scale=ln2[:, k:k + 1]).then_inc(s_gT, 1)

                    def front(i, b):
                        take_attention(i, b)
                        root(i, b)

                    def step(i, b, i2, b2):
                        if b2 is not None:
                            take_attention(i2, b2)
                        back(i, b)
                        if b2 is not None:
                            root(i2, b2)

                    every_step(act, front, step)

                @block.tensor
                def _(pe):
                    pe.wait_ge(s_w, 48)
                    pe.wait_ge(s_id, 2)

                    def turn(dst, tile):
                        for k in range(KM):
                            for t in range(TT):
                                last = nc.tensor.transpose(dst[:, k, t * P:(t + 1) * P], tile(t, k), ident[:, :])
                        return last

                    def front(i, b):
                        c = 2 * i + b
                        wait(pe, s_at, c + 1)
                        wait(pe, s_aT, c)
                        turn(t1_ps, lambda t, k: attc[:, t, k * P:(k + 1) * P]).then_inc(s_t1, 1)
                        wait(pe, s_aT, c + 1)
                        wait(pe, s_h, 2 * c)
                        for t in range(TT):
                            for k in range(KM):
                                last = nc.tensor.matmul(h_ps[:, t, :], attT[:, k, t * P:(t + 1) * P], wo[:, k, :],
                                                        start=(k == 0), stop=(k == KM - 1))
                        last.then_inc(s_wo, 1)

                    def ranks(i, b):
                        c = 2 * i + b
                        wait(pe, s_both, c + 1)
                        wait(pe, s_rt, NRT * c)
                        for t in range(TT + 1):
                            for t2 in range(min(t + 1, TT)):
                                last = nc.tensor.matmul(
                                    rank_ps[:, t * NE:(t + 1) * NE], (before if t2 == t else ones)[:, :],
                                    bothc[:, b, t2, :], start=(t2 == 0), stop=(t2 == min(t, TT - 1)))
                        last.then_inc(s_rank, 1)

                    def back(i, b):
                        c = 2 * i + b
                        wait(pe, s_g, c + 1)
                        wait(pe, s_gT, KM * c)
                        turn(t2_ps, lambda t, k: gs[:, b, t, k * P:(k + 1) * P]).then_inc(s_t2, 1)
                        if not (isinstance(c, int) and c == 0):
                            ranks(*before_it(i, b))
                        wait(pe, s_gT, KM * (c + 1))
                        wait(pe, s_lc, c)
                        for t in range(TT):
                            for k in range(KM):
                                last = nc.tensor.matmul(g_ps[:, t * NE:(t + 1) * NE], gT[:, k, t * P:(t + 1) * P],
                                                        gate[:, k, :], start=(k == 0), stop=(k == KM - 1))
                        last.then_inc(s_lg, 1)

                    pe.wait_ge(s_set, 7)
                    every_chunk(pe, front, back)
                    ranks(NI - 1, 1)

                @block.vector
                def _(dve):
                    dve.wait_ge(s_w, 48)
                    dve.wait_ge(s_set, 11)

                    def add(i, b):
                        c = 2 * i + b
                        wait(dve, s_f[b], 32 * (i + 1))
                        wait(dve, s_wo, c + 1)
                        for half in range(2):
                            part = flat(hc[:, b, 2 * half:2 * half + 2, :])
                            nc.vector.tensor_tensor(part, flat(h_ps[:, 2 * half:2 * half + 2, :]), part, ALU.add
                                                    ).then_inc(s_h, 1)
                        wait(dve, s_h, 2 * (c + 1))
                        for t in range(TT):
                            last = nc.vector.bn_stats(stats[:, t, :], hc[:, b, t, :])
                        last.then_inc(s_st, 1)
                        wait_apart(dve, s_st, 4 * c + 1, s_w)
                        for t in range(TT):
                            last = nc.vector.bn_aggr(mv[:, t, :], stats[:, t, :])
                        last.then_inc(s_st, 1)
                        wait(dve, s_st, 4 * c + 2)
                        nc.vector.tensor_tensor(mv[:, :, 0], mv[:, :, 0], mv[:, :, 0], ALU.mult).then_inc(s_st, 1)
                        wait(dve, s_st, 4 * c + 3)
                        nc.vector.tensor_tensor(mv[:, :, 1], mv[:, :, 1], mv[:, :, 0], ALU.add).then_inc(s_st, 1)

                    def normalize(i, b):
                        c = 2 * i + b
                        wait(dve, s_sd, c + 1)
                        nc.vector.reciprocal(rs[:, :], sd[:, :]).then_inc(s_rs, 1)
                        wait(dve, s_rs, c + 1)
                        wait(dve, s_t2, c - 1)
                        for t in range(TT):
                            nc.vector.tensor_scalar(gs[:, b, t, :], hc[:, b, t, :], rs[:, t:t + 1], None, ALU.mult)
                            last = nc.vector.tensor_scalar(
                                g[:, bass.ds(i * TT + (b * BT + t), 1), :].rearrange("p o e -> p (o e)"),
                                hc[:, b, t, :], rs[:, t:t + 1], None, ALU.mult)
                        last.then_inc(s_g, 1)

                    def back(i, b):
                        c = 2 * i + b
                        wait_apart(dve, s_lg, c + 1, s_w)
                        nc.vector.tensor_copy(lgc[:, b].rearrange("p t e -> p (t e)"), g_ps[:, 0:TT * NE]
                                              ).then_inc(s_lc, 1)
                        wait_apart(dve, s_lc, c + 1, s_w)
                        for t in range(TT):
                            last = nc.vector.max(topc[:, b, t, :], lgc[:, b, t, :])
                        last.then_inc(s_top, 1)
                        wait_apart(dve, s_top, c + 1, s_w)
                        for t in range(TT):
                            last = nc.vector.max_index(idxc[:, b, t, :], topc[:, b, t, :], lgc[:, b, t, :])
                        last.then_inc(s_ix, 1)
                        wait_apart(dve, s_ix, c + 1, s_w)
                        at = bass.ds(i * TT + b * BT, TT)
                        nc.vector.tensor_copy(idc[:, :, :], idxc[:, b, :, 0:2]).then_inc(s_both1, 1)
                        nc.vector.tensor_tensor(dif[:, at], topc[:, b, :, 1], topc[:, b, :, 0], ALU.subtract
                                                ).then_inc(s_dif, 1)
                        wait_apart(dve, s_both1, 4 * c + 1, s_w)
                        nc.vector.tensor_copy(idf[:, at, :], idc[:, :, :]).then_inc(s_both1, 1)
                        for k in range(2):
                            nc.vector.tensor_tensor(hotc[:, b, k], iota[:, None, :].to_broadcast([P, TT, NE]),
                                                    idc[:, :, k, None].to_broadcast([P, TT, NE]), ALU.is_equal
                                                    ).then_inc(s_both1, 1)
                        wait(dve, s_both1, 4 * c + 4)
                        nc.vector.tensor_tensor(bothc[:, b], hotc[:, b, 0], hotc[:, b, 1], ALU.add
                                                ).then_inc(s_both, 1)

                    def keep_base(i, b):
                        c = 2 * i + b
                        wait(dve, s_at, c + 1)
                        for t in range(TT):
                            dst = att[:, b * HP:(b + 1) * HP, bass.ds(i * TT + t, 1), :]
                            last = nc.vector.tensor_tensor(
                                dst.rearrange("p n o w -> p (n o) w"),
                                hc[:, b, t, :].rearrange("p (n w) -> p n w", n=HP),
                                xr[:, b, t, :].rearrange("p (n w) -> p n w", n=HP), ALU.add)
                        last.then_inc(s_base, 1)

                    def places(i, b):
                        c = 2 * i + b
                        wait_apart(dve, s_rank, c + 1, s_w)
                        nc.vector.tensor_tensor(
                            placec[:, :, :], rank_ps[:, 0:TT * NE].rearrange("p (t e) -> p t e", e=NE),
                            count[:, None, :].to_broadcast([P, TT, NE]), ALU.add).then_inc(s_rt, 1)
                        wait_apart(dve, s_rt, NRT * c + 1, s_w)
                        nc.vector.tensor_tensor(count[:, :], rank_ps[:, TT * NE:(TT + 1) * NE], count[:, :], ALU.add
                                                ).then_inc(s_rt, 1)
                        for k in range(2):
                            nc.vector.tensor_tensor(pickc[:, k], hotc[:, b, k], placec[:, :, :], ALU.mult
                                                    ).then_inc(s_rt, 1)
                        wait_apart(dve, s_rt, NRT * c + 4, s_w)
                        for k in range(2):
                            nc.vector.tensor_reduce(rowc[:, k, :], pickc[:, k], AX.X, ALU.add).then_inc(s_rt, 1)
                        wait_apart(dve, s_rt, NRT * c + 6, s_w)
                        at = bass.ds(i * TT + b * BT, TT)
                        nc.vector.tensor_copy(row_f[:, :, at], rowc[:, :, :]).then_inc(s_rt, 1)
                        nc.vector.tensor_copy(row_in[:, :, at], rowc[:, :, :]).then_inc(s_row, 1)
                        wait_apart(dve, s_row, c + 1, s_w)

                    def front(i, b):
                        add(i, b)
                        keep_base(i, b)
                        normalize(i, b)

                    def step(i, b, i2, b2):
                        if b2 is not None:
                            add(i2, b2)
                            keep_base(i2, b2)
                        back(i, b)
                        if not (isinstance(i, int) and i == 0 and b == 0):
                            places(*before_it(i, b))
                        if b2 is not None:
                            normalize(i2, b2)

                    every_step(dve, front, step)
                    places(NI - 1, 1)
                    dve.wait_ge(s_rt, NRT * 2 * NI)
                    nc.vector.tensor_tensor(behind_f[:, :], count[:, :], part_no[:, :].to_broadcast([P, NE]),
                                            ALU.add).then_inc(s_rt, 1)
                    dve.wait_ge(s_rt, NRT * 2 * NI + 1)
                    nc.vector.tensor_copy(behind[:, :], behind_f[:, :]).then_inc(s_behind, 1)

            ex = sb2("ex", [P, NT])
            den = sb2("den", [P, NT])
            hot = sb2("hot", [P, 2, NT, NE])
            cmp_ = sb2("cmp", [P, NE, NT])
            nt = sb2("nt", [P, NE])
            upto = sb2("upto", [P, NE])
            base = sb2("base", [P, NE])
            pick = sb2("pick", [P, 2, NT, NE])
            le = sb2("le", [1, SLOT_TILES, NE])
            exf = sb2("exf", [1, SLOT_TILES])
            outf = sb2("outf", [P, 2, NT])
            cnt = sb2("cnt", [P, NE])
            les = sb2("les", [1, SLOT_TILES, NE])
            tb = sb2("tb", [1, SLOT_TILES])
            rowf = sb2("rowf", [1, SLOT_TILES])
            block = ctx2.enter_context(nc.Block())

            @block.gpsimd
            def _(pool):
                for c in (2 * NI - 2, 2 * NI - 1):
                    scatter(pool, c)
                pool.wait_ge(s_behind, 1)
                for e in range(NE):
                    nc.gpsimd.indirect_dma_start(
                        out=xg_dram[:, :],
                        out_offset=bass.IndirectOffsetOnAxis(ap=behind[:, e:e + 1], axis=0),
                        in_=zero[:, :], in_offset=None).then_inc(s_sc, 16)

            @block.scalar
            def _(act):
                nc.scalar.activation(ex[:, :], dif[:, :], ACT.Exp).then_inc(s_ex, 1)

            @block.vector
            def _(dve):
                step = [0]

                def then(ins):
                    step[0] += 1
                    ins.then_inc(s_r, 1)
                    dve.wait_ge(s_r, step[0])

                def te(ap):
                    return ap.rearrange("p t e -> p (t e)")

                then(nc.vector.memset(one[:, :], 1.0))
                for k in range(2):
                    then(nc.vector.tensor_tensor(hot[:, k], iota[:, None, :].to_broadcast([P, NT, NE]),
                                                 idf[:, :, k, None].to_broadcast([P, NT, NE]), ALU.is_equal))
                dve.wait_ge(s_ex, 1)
                then(nc.vector.tensor_scalar(den[:, :], ex[:, :], 1.0, None, ALU.add))
                then(nc.vector.reciprocal(sh[:, 0, :], den[:, :]))
                then(nc.vector.tensor_tensor(sh[:, 1, :], sh[:, 0, :], ex[:, :], ALU.mult))
                then(nc.vector.tensor_tensor(cnt[:, :], count[:, :], region[:, :], ALU.subtract))
                then(nc.vector.tensor_tensor(cmp_[:, :, :], cnt[:, :, None].to_broadcast([P, NE, NT]),
                                             starts[:, None, :].to_broadcast([P, NE, NT]), ALU.is_gt))
                then(nc.vector.tensor_reduce(nt[:, :], cmp_[:, :, :], AX.X, ALU.add))
                then(nc.vector.tensor_tensor_scan(upto[:, :], one[:, 0:NE], nt[:, :], 0.0, ALU.mult, ALU.add))
                then(nc.vector.tensor_tensor(base[:, :], upto[:, :], nt[:, :], ALU.subtract))
                then(nc.vector.tensor_scalar(base[:, :], base[:, :], float(P), None, ALU.mult))
                then(nc.vector.tensor_tensor(base[:, :], base[:, :], region[:, :], ALU.subtract))
                for k in range(2):
                    then(nc.vector.tensor_tensor(pick[:, k], hot[:, k],
                                                 base[:, None, :].to_broadcast([P, NT, NE]), ALU.mult))
                    then(nc.vector.tensor_reduce(outf[:, k, :], pick[:, k], AX.X, ALU.add))
                    then(nc.vector.tensor_tensor(outf[:, k, :], outf[:, k, :], row_f[:, k, :], ALU.add))
                    then(nc.vector.tensor_copy(row_out[:, k, :], outf[:, k, :]))
                then(nc.vector.tensor_tensor(le[:, :, :], upto[0:1, None, :].to_broadcast([1, SLOT_TILES, NE]),
                                             tiles[:, :, None].to_broadcast([1, SLOT_TILES, NE]), ALU.is_le))
                then(nc.vector.tensor_reduce(exf[:, :], le[:, :, :], AX.X, ALU.add))
                then(nc.vector.tensor_tensor(les[:, :, :], le[:, :, :],
                                             nt[0:1, None, :].to_broadcast([1, SLOT_TILES, NE]), ALU.mult))
                then(nc.vector.tensor_reduce(tb[:, :], les[:, :, :], AX.X, ALU.add))
                then(nc.vector.tensor_tensor(tb[:, :], tiles[:, :], tb[:, :], ALU.subtract))
                then(nc.vector.tensor_scalar(tb[:, :], tb[:, :], float(P), None, ALU.mult))
                then(nc.vector.tensor_scalar(rowf[:, :], exf[:, :], float(REG), None, ALU.mult))
                then(nc.vector.tensor_tensor(rowf[:, :], rowf[:, :], tb[:, :], ALU.add))
                then(nc.vector.tensor_scalar(rowf[:, :], rowf[:, :], float(NE * REG), None, ALU.min))
                then(nc.vector.tensor_copy(first_row[:, :], rowf[:, :]))
                then(nc.vector.tensor_scalar(exf[:, :], exf[:, :], float(NE - 1), None, ALU.min))
                then(nc.vector.tensor_copy(expert[:, :], exf[:, :]))

        with ExitStack() as ctx2:
            def sb3(name, shape, dt=F32):
                return ctx2.enter_context(nc.sbuf_tensor(name, shape, dt))

            def ps3(name, shape, dt=F32):
                return ctx2.enter_context(nc.psum_tensor(name, shape, dt))

            xt = sb3("xt", [P, 4, DM])
            xT = sb3("m_xT", [P, 2, KM, P])
            sl = sb3("sl", [P, 2, FI])
            mid = sb3("mid", [P, 2, FI])
            midT = sb3("midT", [P, 2, KF, P])
            yt = sb3("yt", [P, 4, DM])
            a_ps = ps3("a_ps", [P, 2, FI])
            c_ps = ps3("c3_ps", [P, 2, FI])
            x_ps = ps3("x_ps", [P, FI])
            m_ps = ps3("m_ps", [P, KF, P])
            o_ps = ps3("o_ps", [P, 2, FI])

            s_xt = [sem(f"m_xt{r}") for r in range(4)]
            s_xp = sem("m_xp")
            s_xT = sem("m_xTs")
            s_up = sem("m_up")
            s_sl = sem("m_sl")
            s_mid = sem("m_mid")
            s_mp = sem("m_mp")
            s_mT = sem("m_mT")
            s_dn = sem("m_dn")
            s_yt = sem("m_yt")
            s_y = [sem(f"m_y{r}") for r in range(4)]

            NJ = SLOT_TILES
            block = ctx2.enter_context(nc.Block())

            def every_tile(eng, step):
                for j in range(8):
                    step(j, j % 4, j // 4)
                with eng.Fori(2, NJ // 4 - 1) as n:
                    for q in range(4):
                        step(4 * n + q, q, n)
                for j in range(NJ - 4, NJ + 2):
                    step(j, j % 4, j // 4)

            def there(j, back):
                return not isinstance(j, int) or 0 <= j - back < NJ

            def at(q, n, back):
                return (q - back) % 4, n + (q - back) // 4

            @block.gpsimd
            def _(pool):
                pool.wait_ge(s_clear, 16)
                pool.wait_ge(s_sc, 16 * (2 * NT + NE))

                def load(j, slot, n):
                    row = pool.value_load(first_row[0:1, bass.ds(j, 1)], min_val=0, max_val=NE * REG)
                    wait_apart(pool, s_xp, j - 3, s_sc)
                    nc.gpsimd.dma_start(xt[:, slot, :], xg_dram[bass.ds(row, P), :]).then_inc(s_xt[slot], 16)

                for j in range(4):
                    load(j, j, 0)
                with pool.Fori(1, NJ // 4) as n:
                    for q in range(4):
                        load(4 * n + q, q, n)

            @block.sync
            def _(sp):
                def store(j, slot):
                    wait_apart(sp, s_yt, j + 1, s_we)
                    sp.dma_start(y_dram[bass.ds(j * P, P), :], yt[:, slot, :]).then_inc(s_y[slot], 16)

                sp.wait_ge(s_we, 16 * 3 * NE)
                for j in range(4):
                    store(j, j)
                with sp.Fori(1, NJ // 4) as n:
                    for q in range(4):
                        store(4 * n + q, q)
                for slot in range(4):
                    sp.wait_ge(s_y[slot], 16 * (NJ // 4))

            @block.scalar
            def _(act):
                def rows(j, q, n):
                    wait(act, s_xp, j + 1)
                    wait(act, s_up, j - 1)
                    for k in range(KM):
                        nc.scalar.activation(xT[:, q % 2, k, :], x_ps[:, k * P:(k + 1) * P], ACT.Identity,
                                             scale=ln2[:, k:k + 1]).then_inc(s_xT, 1)

                def step(j, q, n):
                    if isinstance(j, int) and j == 0:
                        rows(0, 0, 0)
                    if there(j, -1):
                        rows(j + 1, (q + 1) % 4, 0)
                    if there(j, 1):
                        wait(act, s_mp, j)
                        wait(act, s_dn, j - 2)
                        nc.scalar.copy(midT[:, (q - 1) % 2], m_ps[:, :, :]).then_inc(s_mT, 1)
                    if there(j, 0):
                        wait(act, s_up, j + 1)
                        wait(act, s_mid, j - 1)
                        nc.scalar.activation(sl[:, q % 2, :], a_ps[:, q % 2, :], ACT.Silu).then_inc(s_sl, 1)

                every_tile(act, step)

            @block.vector
            def _(dve):
                def step(j, q, n):
                    if there(j, 2):
                        slot, taken = at(q, n, 2)
                        wait(dve, s_dn, j - 1)
                        wait(dve, s_y[slot], 16 * taken)
                        nc.vector.tensor_copy(yt[:, slot, :], o_ps[:, q % 2, 0:DM]).then_inc(s_yt, 1)
                    if there(j, 0):
                        wait(dve, s_sl, j + 1)
                        wait(dve, s_mp, j - 1)
                        nc.vector.tensor_tensor(mid[:, q % 2, :], sl[:, q % 2, :], c_ps[:, q % 2, :], ALU.mult
                                                ).then_inc(s_mid, 1)

                every_tile(dve, step)

            @block.tensor
            def _(pe):
                pe.wait_ge(s_we, 16 * 3 * NE)

                def turn_rows(j, slot, taken):
                    wait(pe, s_xt[slot], 16 * (taken + 1))
                    wait(pe, s_xT, KM * j)
                    for k in range(KM):
                        last = nc.tensor.transpose(x_ps[:, k * P:(k + 1) * P], xt[:, slot, k * P:(k + 1) * P],
                                                   ident[:, :])
                    last.then_inc(s_xp, 1)

                def of_expert(w, e, k):
                    return w[:, bass.ds(e, 1), k, :].rearrange("p o n -> p (o n)")

                def load_expert(j):
                    return pe.value_load(expert[0:1, bass.ds(j, 1)], min_val=0, max_val=NE - 1)

                def step(j, q, n):
                    if isinstance(j, int) and j == 0:
                        turn_rows(0, 0, 0)
                    if there(j, -1):
                        turn_rows(j + 1, *at(q, n, -1))
                    if there(j, 2):
                        e = load_expert(j - 2)
                        wait(pe, s_mT, j - 1)
                        wait(pe, s_yt, j - 3)
                        for m in range(KF):
                            last = nc.tensor.matmul(o_ps[:, q % 2, 0:DM], midT[:, q % 2, m, :],
                                                    of_expert(w2, e, m), start=(m == 0), stop=(m == KF - 1))
                        last.then_inc(s_dn, 1)
                    if there(j, 1):
                        wait(pe, s_mid, j)
                        wait(pe, s_mT, j - 1)
                        for m in range(KF):
                            last = nc.tensor.transpose(m_ps[:, m, :], mid[:, (q - 1) % 2, m * P:(m + 1) * P],
                                                       ident[:, :])
                        last.then_inc(s_mp, 1)
                    if there(j, 0):
                        e = load_expert(j)
                        wait(pe, s_xT, KM * (j + 1))
                        wait(pe, s_mid, j - 1)
                        for w, dst in ((w1, a_ps), (w3, c_ps)):
                            for k in range(KM):
                                last = nc.tensor.matmul(dst[:, q % 2, :], xT[:, q % 2, k, :],
                                                        of_expert(w, e, k), start=(k == 0), stop=(k == KM - 1))
                        last.then_inc(s_up, 1)

                every_tile(pe, step)

        with ExitStack() as ctx2:
            RG = 4
            ya = ctx2.enter_context(nc.sbuf_tensor("ya", [P, RG, 2, DM], F32))
            res = ctx2.enter_context(nc.sbuf_tensor("res", [P, RG, DM], F32))
            s_ya = [sem(f"m_ya{r}") for r in range(RG)]
            s_res = [sem("m_res0"), sem("m_res1")]
            s_out = [sem(f"m_out{r}") for r in range(RG)]
            block = ctx2.enter_context(nc.Block())

            @block.gpsimd
            def _(pool):
                for t in range(NT):
                    wait(pool, s_res[1], t - RG + 1)
                    for k in range(2):
                        nc.gpsimd.indirect_dma_start(
                            out=ya[:, t % RG, k, :], out_offset=None, in_=y_dram[:, :],
                            in_offset=bass.IndirectOffsetOnAxis(ap=row_out[:, k, t:t + 1], axis=0)
                        ).then_inc(s_ya[t % RG], 16)

            @block.vector
            def _(dve):
                def rows(ap):
                    return ap.rearrange("p (n w) -> p n w", n=HP)

                def add(t, k):
                    b, tb = t // BT, t % BT
                    r = t % RG
                    if k == 0:
                        dve.wait_ge(s_ya[r], 32 * (t // RG + 1))
                        wait(dve, s_out[r], 16 * (t // RG))
                        src = att[:, b * HP:(b + 1) * HP, tb, :]
                    else:
                        dve.wait_ge(s_res[0], t + 1)
                        src = rows(res[:, r, :])
                    nc.vector.scalar_tensor_tensor(
                        out=rows(res[:, r, :]), in0=rows(ya[:, r, k, :]), scalar=sh[:, k, t:t + 1],
                        in1=src, op0=ALU.mult, op1=ALU.add).then_inc(s_res[k], 1)

                for t in range(NT):
                    add(t, 0)
                    add(t, 1)

            @block.sync
            def _(sp):
                for t in range(NT):
                    b, tb = t // BT, t % BT
                    sp.wait_ge(s_res[1], t + 1)
                    sp.dma_start(out[b, tb * P:(tb + 1) * P, :], res[:, t % RG, :]).then_inc(s_out[t % RG], 16)
                for r in range(RG):
                    sp.wait_ge(s_out[r], 16 * (NT // RG))


def slot_tiles(tokens, experts):
    most = (2 * tokens + experts * (P - 1)) // P
    return -(-most // 4) * 4


def build(nc, a, out):
    B, L, _ = a["x"].shape
    x1 = nc.dram_tensor("x1_scratch", [B, L, DM], F32, kind="Internal").ap()
    f = nc.dram_tensor("f_scratch", [B, L, DM], F32, kind="Internal").ap()
    b_rows = nc.dram_tensor("b_rows", [2, NS, CH], F32, kind="Internal").ap()
    slots = P * slot_tiles(B * L, a["gateT"].shape[1])
    xg = nc.dram_tensor("slots_in", [a["gateT"].shape[1] * (B * L + P) + P, DM], F32, kind="Internal").ap()
    y = nc.dram_tensor("slots_out", [slots, DM], F32, kind="Internal").ap()
    parts = nc.dram_tensor("parts", [2, 3, B * DM, L], BF16, kind="Internal").ap()

    ssm_stage(nc, a["x"], a["W_inT"], a["conv_w"], a["conv_b"], a["W_xT"], a["dt_w"], a["dt_b"],
              a["A_log"], a["D_param"], a["W_outT"], x1, b_rows)
    with nc.sbuf_tensor("att", [P, B * HP, L // P, 2 * HD], F32) as att:
        with nc.sbuf_tensor("v_all", [P, B * HP, L // P, VW], F32) as v_all:
            qkv_stage(nc, x1, a["ln1_w"], a["wqT"], a["wkT"], a["wvT"], f, parts, v_all)
            attention_stage(nc, parts, v_all, att, B, L)
        moe_stage(nc, x1, f, att, a["woT"], a["ln2_w"], a["gateT"], a["w1T"], a["w2T"], a["w3T"], xg, y, out)


def kernel(**inputs):
    import numpy as np
    import concourse.bacc as bacc
    from concourse.bass_utils import run_bass_kernel_spmd

    a = {k.replace("L0_attn_", "").replace("L0_ffn_", ""): np.asarray(v) for k, v in inputs.items()}
    W_x = a["W_x"]
    laid = dict(
        x=a["x"], W_inT=a["W_in"].T, conv_w=a["conv_w"], conv_b=a["conv_b"],
        W_xT=np.concatenate([W_x[NS + 1:], W_x[:1], W_x[1:NS + 1]], axis=0).T, dt_w=a["dt_w"][:, 0], dt_b=a["dt_b"],
        A_log=a["A_log"], D_param=a["D_param"], W_outT=a["W_out"].T,
        ln1_w=a["ln1_w"], ln2_w=a["ln2_w"], wqT=a["wq"].T, wkT=a["wk"].T, wvT=a["wv"].T, woT=a["wo"].T,
        gateT=a["gate_w"].T, w1T=a["w1"].transpose(0, 2, 1), w2T=a["w2"].transpose(0, 2, 1),
        w3T=a["w3"].transpose(0, 2, 1))
    nc = bacc.Bacc("TRN2", target_bir_lowering=False, num_devices=1)
    arrays, aps = {}, {}
    for name, v in laid.items():
        v = np.ascontiguousarray(v)
        arrays[f"in_{name}"] = v
        aps[name] = nc.dram_tensor(f"in_{name}", v.shape, mybir.dt.from_np(v.dtype), kind="ExternalInput").ap()
    out = nc.dram_tensor("out_x", a["x"].shape, F32, kind="ExternalOutput").ap()
    build(nc, aps, out)
    r = run_bass_kernel_spmd(nc, [arrays], core_ids=[0])
    return r.results[0]["out_x"]
```
